# Optimizing a Trainium2 kernel written in Bass

```python
import numpy as np
import jax
import jax.numpy as jnp

def _softmax(x, axis=-1):
    return jax.nn.softmax(x, axis=axis)

def _gelu(x):
    return jax.nn.gelu(x, approximate=True)

def _silu(x):
    return jax.nn.silu(x)

def _sigmoid(x):
    return jax.nn.sigmoid(x)

def _layernorm(x, axis=-1, eps=1e-05):
    m = jnp.mean(x, axis=axis, keepdims=True)
    v = jnp.var(x, axis=axis, keepdims=True)
    return (x - m) / jnp.sqrt(v + eps)

def _scatter_add(tgt, idx, src, axis=0):
    return tgt.at[idx].add(src)

def _segment_sum(src, seg, n):
    return jax.ops.segment_sum(src, seg, n)
kernel_name = 'mk_early_fusion_d1_tok_img256_r4_0ba3ca'

def setup_inputs(seed: int=0):
    np.random.seed(seed)
    _w = jnp.asarray

    def _rec_inputs():
        import jax
        import jax.numpy as jnp
        _rk = jax.random.key(seed)
        x = -0.000596345 + 1.00056 * jax.random.normal(jax.random.fold_in(_rk, 1), (64, 64, 64, 3), jnp.float32)
        txt = -1.92552e-05 + 0.02 * jax.random.normal(jax.random.fold_in(_rk, 2), (64, 77, 64), jnp.float32)
        return (x, txt)
    x, txt = _rec_inputs()

    def _L0_tok_setup():
        import jax, jax.numpy as jnp
        import numpy as np
        M1 = 20
        M2 = 20

        def _spectral_conv(x, w):
            B, Cin, H, W = x.shape
            x_ft = jnp.fft.rfft2(x, norm='ortho')
            out = jnp.einsum('bixy,ioxy->boxy', x_ft[:, :, :M1, :M2], w.astype(x_ft.dtype))
            out_ft = jnp.zeros((B, w.shape[1], H, W // 2 + 1), dtype=x_ft.dtype)
            out_ft = out_ft.at[:, :, :M1, :M2].set(out)
            return jnp.fft.irfft2(out_ft, s=(H, W), norm='ortho')

        def _gelu(x):
            return jax.nn.gelu(x, approximate=False)
        key = jax.random.key(seed)
        ks = jax.random.split(key, 16)
        B, H, W, width = (16, 64, 64, 32)
        scale = 1.0 / (width * width)
        d = {}
        d['coords'] = jax.random.normal(ks[0], (B, H, W, 3), dtype=jnp.float32)
        d['fc0_w'] = jax.random.normal(ks[1], (3, width), dtype=jnp.float32) * 0.1
        d['fc0_b'] = jnp.zeros((width,), dtype=jnp.float32)
        for i in range(4):
            d[f'sw{i}'] = scale * jax.random.normal(ks[2 + i], (width, width, M1, M2), dtype=jnp.float32)
            d[f'cw{i}'] = jax.random.normal(ks[6 + i], (width, width), dtype=jnp.float32) * 0.1
            d[f'cb{i}'] = jnp.zeros((width,), dtype=jnp.float32)
        d['fc1_w'] = jax.random.normal(ks[10], (width, 64), dtype=jnp.float32) * 0.1
        d['fc1_b'] = jnp.zeros((64,), dtype=jnp.float32)
        d['fc2_w'] = jax.random.normal(ks[11], (64, 1), dtype=jnp.float32) * 0.1
        d['fc2_b'] = jnp.zeros((1,), dtype=jnp.float32)
        return d
    _L0_tok_all = _L0_tok_setup()
    _L0_tok_in = {k: v for k, v in _L0_tok_all.items() if k in ('fc0_w', 'fc0_b', 'sw0', 'cw0', 'cb0', 'sw1', 'cw1', 'cb1', 'sw2', 'cw2', 'cb2', 'sw3', 'cw3', 'cb3', 'fc1_w', 'fc1_b', 'fc2_w', 'fc2_b')}
    del _L0_tok_all

    def _L0_attn_setup():
        import jax, jax.numpy as jnp
        import numpy as np
        NHEAD = 8
        ATT_EPS = 1e-06
        LN_EPS = 1e-05

        def _layernorm(x, g, b):
            mu = jnp.mean(x, axis=-1, keepdims=True)
            var = jnp.mean(jnp.square(x - mu), axis=-1, keepdims=True)
            return (x - mu) * jax.lax.rsqrt(var + LN_EPS) * g + b
        key = jax.random.key(seed)
        ks = jax.random.split(key, 7)
        N, L, C = (4, 4096, 64)
        s = 1.0 / np.sqrt(C)
        return {'x': jax.random.normal(ks[0], (N, L, C), jnp.float32), 'Wq': jax.random.normal(ks[1], (C, C), jnp.float32) * s, 'Wk': jax.random.normal(ks[2], (C, C), jnp.float32) * s, 'Wv': jax.random.normal(ks[3], (C, C), jnp.float32) * s, 'Wm': jax.random.normal(ks[4], (C, C), jnp.float32) * s, 'W1': jax.random.normal(ks[5], (2 * C, 2 * C), jnp.float32) * (1.0 / np.sqrt(2 * C)), 'W2': jax.random.normal(ks[6], (2 * C, C), jnp.float32) * (1.0 / np.sqrt(2 * C)), 'g1': jnp.ones((C,), jnp.float32), 'b1': jnp.zeros((C,), jnp.float32), 'g2': jnp.ones((C,), jnp.float32), 'b2': jnp.zeros((C,), jnp.float32)}
    _L0_attn_all = _L0_attn_setup()
    _L0_attn_in = {k: v for k, v in _L0_attn_all.items() if k in ('Wq', 'Wk', 'Wv', 'Wm', 'W1', 'W2', 'g1', 'b1', 'g2', 'b2')}
    del _L0_attn_all

    def _L0_ffn_setup():
        import jax, jax.numpy as jnp
        import numpy as np
        E = 8
        K = 2
        D = 64
        H = 128
        DOUT = 64
        EPS = 1e-05
        key = jax.random.key(seed)
        ks = jax.random.split(key, 9)
        s = 0.02
        return {'x': jax.random.normal(ks[0], (4, 2048, D), jnp.float32), 'gamma': 1.0 + 0.05 * jax.random.normal(ks[1], (D,), jnp.float32), 'beta': 0.05 * jax.random.normal(ks[2], (D,), jnp.float32), 'Wr': 0.01 * jax.random.normal(ks[3], (D, E), jnp.float32), 'br': jnp.zeros((E,), jnp.float32), 'W1': s * jax.random.normal(ks[4], (E, D, H), jnp.float32), 'b1': s * jax.random.normal(ks[5], (E, H), jnp.float32), 'W2': s * jax.random.normal(ks[6], (E, H, DOUT), jnp.float32), 'b2': s * jax.random.normal(ks[7], (E, DOUT), jnp.float32)}
    _L0_ffn_all = _L0_ffn_setup()
    _L0_ffn_in = {k: v for k, v in _L0_ffn_all.items() if k in ('gamma', 'beta', 'Wr', 'br', 'W1', 'b1', 'W2', 'b2')}
    del _L0_ffn_all
    return {'x': x, 'txt': txt, 'L0_tok_fc0_w': _L0_tok_in['fc0_w'], 'L0_tok_fc0_b': _L0_tok_in['fc0_b'], 'L0_tok_sw0': _L0_tok_in['sw0'], 'L0_tok_cw0': _L0_tok_in['cw0'], 'L0_tok_cb0': _L0_tok_in['cb0'], 'L0_tok_sw1': _L0_tok_in['sw1'], 'L0_tok_cw1': _L0_tok_in['cw1'], 'L0_tok_cb1': _L0_tok_in['cb1'], 'L0_tok_sw2': _L0_tok_in['sw2'], 'L0_tok_cw2': _L0_tok_in['cw2'], 'L0_tok_cb2': _L0_tok_in['cb2'], 'L0_tok_sw3': _L0_tok_in['sw3'], 'L0_tok_cw3': _L0_tok_in['cw3'], 'L0_tok_cb3': _L0_tok_in['cb3'], 'L0_tok_fc1_w': _L0_tok_in['fc1_w'], 'L0_tok_fc1_b': _L0_tok_in['fc1_b'], 'L0_tok_fc2_w': _L0_tok_in['fc2_w'], 'L0_tok_fc2_b': _L0_tok_in['fc2_b'], 'L0_attn_Wq': _L0_attn_in['Wq'], 'L0_attn_Wk': _L0_attn_in['Wk'], 'L0_attn_Wv': _L0_attn_in['Wv'], 'L0_attn_Wm': _L0_attn_in['Wm'], 'L0_attn_W1': _L0_attn_in['W1'], 'L0_attn_W2': _L0_attn_in['W2'], 'L0_attn_g1': _L0_attn_in['g1'], 'L0_attn_b1': _L0_attn_in['b1'], 'L0_attn_g2': _L0_attn_in['g2'], 'L0_attn_b2': _L0_attn_in['b2'], 'L0_ffn_gamma': _L0_ffn_in['gamma'], 'L0_ffn_beta': _L0_ffn_in['beta'], 'L0_ffn_Wr': _L0_ffn_in['Wr'], 'L0_ffn_br': _L0_ffn_in['br'], 'L0_ffn_W1': _L0_ffn_in['W1'], 'L0_ffn_b1': _L0_ffn_in['b1'], 'L0_ffn_W2': _L0_ffn_in['W2'], 'L0_ffn_b2': _L0_ffn_in['b2']}

def reference(x, txt, L0_tok_fc0_w, L0_tok_fc0_b, L0_tok_sw0, L0_tok_cw0, L0_tok_cb0, L0_tok_sw1, L0_tok_cw1, L0_tok_cb1, L0_tok_sw2, L0_tok_cw2, L0_tok_cb2, L0_tok_sw3, L0_tok_cw3, L0_tok_cb3, L0_tok_fc1_w, L0_tok_fc1_b, L0_tok_fc2_w, L0_tok_fc2_b, L0_attn_Wq, L0_attn_Wk, L0_attn_Wv, L0_attn_Wm, L0_attn_W1, L0_attn_W2, L0_attn_g1, L0_attn_b1, L0_attn_g2, L0_attn_b2, L0_ffn_gamma, L0_ffn_beta, L0_ffn_Wr, L0_ffn_br, L0_ffn_W1, L0_ffn_b1, L0_ffn_W2, L0_ffn_b2):
    import jax
    import jax.numpy as jnp

    def _L0_tok_ref(coords, fc0_w, fc0_b, sw0, cw0, cb0, sw1, cw1, cb1, sw2, cw2, cb2, sw3, cw3, cb3, fc1_w, fc1_b, fc2_w, fc2_b):
        import jax, jax.numpy as jnp
        import numpy as np
        M1 = 20
        M2 = 20

        def _spectral_conv(x, w):
            B, Cin, H, W = x.shape
            x_ft = jnp.fft.rfft2(x, norm='ortho')
            out = jnp.einsum('bixy,ioxy->boxy', x_ft[:, :, :M1, :M2], w.astype(x_ft.dtype))
            out_ft = jnp.zeros((B, w.shape[1], H, W // 2 + 1), dtype=x_ft.dtype)
            out_ft = out_ft.at[:, :, :M1, :M2].set(out)
            return jnp.fft.irfft2(out_ft, s=(H, W), norm='ortho')

        def _gelu(x):
            return jax.nn.gelu(x, approximate=False)
        x = coords @ fc0_w + fc0_b
        x = jnp.transpose(x, (0, 3, 1, 2))
        for sw, cw, cb in ((sw0, cw0, cb0), (sw1, cw1, cb1), (sw2, cw2, cb2), (sw3, cw3, cb3)):
            x1 = _spectral_conv(x, sw)
            x2 = jnp.einsum('bchw,oc->bohw', x, cw) + cb[None, :, None, None]
            x = _gelu(x1 + x2)
        x = jnp.transpose(x, (0, 2, 3, 1))
        x = _gelu(x @ fc1_w + fc1_b)
        return (x @ fc2_w + fc2_b)[..., 0]

    def _L0_attn_ref(x, Wq, Wk, Wv, Wm, W1, W2, g1, b1, g2, b2):
        import jax, jax.numpy as jnp
        import numpy as np
        NHEAD = 8
        ATT_EPS = 1e-06
        LN_EPS = 1e-05

        def _layernorm(x, g, b):
            mu = jnp.mean(x, axis=-1, keepdims=True)
            var = jnp.mean(jnp.square(x - mu), axis=-1, keepdims=True)
            return (x - mu) * jax.lax.rsqrt(var + LN_EPS) * g + b
        N, L, C = x.shape
        H = NHEAD
        D = C // H
        q = (x @ Wq).reshape(N, L, H, D)
        k = (x @ Wk).reshape(N, L, H, D)
        v = (x @ Wv).reshape(N, L, H, D)
        Q = jax.nn.elu(q) + 1.0
        K = jax.nn.elu(k) + 1.0
        v = v / L
        KV = jnp.einsum('nshd,nshv->nhdv', K, v)
        Z = 1.0 / (jnp.einsum('nlhd,nhd->nlh', Q, K.sum(axis=1)) + ATT_EPS)
        msg = jnp.einsum('nlhd,nhdv,nlh->nlhv', Q, KV, Z) * L
        msg = msg.reshape(N, L, C) @ Wm
        msg = _layernorm(msg, g1, b1)
        h = jnp.concatenate([x, msg], axis=-1) @ W1
        h = jax.nn.relu(h) @ W2
        msg = _layernorm(h, g2, b2)
        return x + msg

    def _L0_ffn_ref(x, gamma, beta, Wr, br, W1, b1, W2, b2):
        import jax, jax.numpy as jnp
        import numpy as np
        E = 8
        K = 2
        D = 64
        H = 128
        DOUT = 64
        EPS = 1e-05
        mu = jnp.mean(x, axis=-1, keepdims=True)
        var = jnp.mean(jnp.square(x - mu), axis=-1, keepdims=True)
        xn = (x - mu) * jax.lax.rsqrt(var + EPS) * gamma + beta
        logits = jnp.einsum('bsd,de->bse', xn, Wr) + br
        top_vals, top_idx = jax.lax.top_k(logits, K)
        w = jax.nn.softmax(top_vals, axis=-1)
        w_full = jnp.einsum('bsk,bske->bse', w, jax.nn.one_hot(top_idx, E, dtype=w.dtype))
        y = jnp.zeros(x.shape[:-1] + (DOUT,), x.dtype)
        for e in range(E):
            h = jax.nn.gelu(jnp.einsum('bsd,dh->bsh', xn, W1[e]) + b1[e], approximate=False)
            y_e = jnp.einsum('bsh,hd->bsd', h, W2[e]) + b2[e]
            y = y + y_e * w_full[..., e, None]
        return y
    h = _L0_tok_ref(x, L0_tok_fc0_w, L0_tok_fc0_b, L0_tok_sw0, L0_tok_cw0, L0_tok_cb0, L0_tok_sw1, L0_tok_cw1, L0_tok_cb1, L0_tok_sw2, L0_tok_cw2, L0_tok_cb2, L0_tok_sw3, L0_tok_cw3, L0_tok_cb3, L0_tok_fc1_w, L0_tok_fc1_b, L0_tok_fc2_w, L0_tok_fc2_b)
    h = jnp.concatenate([h, txt], axis=1)
    h = h + _L0_attn_ref(_layernorm(h, axis=-1), L0_attn_Wq, L0_attn_Wk, L0_attn_Wv, L0_attn_Wm, L0_attn_W1, L0_attn_W2, L0_attn_g1, L0_attn_b1, L0_attn_g2, L0_attn_b2)
    h = h + _L0_ffn_ref(_layernorm(h, axis=-1), L0_ffn_gamma, L0_ffn_beta, L0_ffn_Wr, L0_ffn_br, L0_ffn_W1, L0_ffn_b1, L0_ffn_W2, L0_ffn_b2)
    return h

_drawn_inputs = setup_inputs


def setup_inputs(seed=0):
    import zlib

    import numpy as np

    out = dict(_drawn_inputs(seed))
    spreads = {'L0_tok_fc0_b': (0.0, 0.8),
     'L0_tok_cb0': (0.0, 0.8),
     'L0_tok_cb1': (0.0, 0.773),
     'L0_tok_cb2': (0.0, 0.8),
     'L0_tok_cb3': (0.0, 0.722),
     'L0_tok_fc1_b': (0.0, 0.601),
     'L0_attn_g1': (1.0, 0.2),
     'L0_attn_b1': (0.0, 0.1),
     'L0_attn_g2': (1.0, 0.2),
     'L0_attn_b2': (0.0, 0.1),
     'L0_ffn_br': (0.0, 0.443)}
    factors = {'L0_tok_sw0': 8.0,
     'L0_tok_sw1': 8.0,
     'L0_tok_sw2': 8.0,
     'L0_tok_sw3': 8.0,
     'L0_tok_fc2_w': 3.057,
     'L0_ffn_gamma': 8.0,
     'L0_ffn_beta': 8.0,
     'L0_ffn_Wr': 8.0,
     'L0_ffn_W1': 5.391,
     'L0_ffn_b1': 8.0,
     'L0_ffn_W2': 5.32,
     'L0_ffn_b2': 16.011}
    for name, (base, spread) in spreads.items():
        noise = np.random.default_rng([zlib.crc32(name.encode()), seed]).standard_normal(out[name].shape)
        drawn = base * np.exp(spread * noise) if base else spread * noise
        out[name] = jnp.asarray(drawn.astype(out[name].dtype))
    for name, factor in factors.items():
        out[name] = (out[name] * factor).astype(out[name].dtype)
    return out
```

```python
from contextlib import ExitStack

import numpy as np

import concourse.bass as bass
from concourse import mybir

F32 = mybir.dt.float32
F16 = mybir.dt.float16
I32 = mybir.dt.int32
ALU = mybir.AluOpType
ACT = mybir.ActivationFunctionType
AX = mybir.AxisListType

B, S, C = 64, 64, 32
CIN = 3
LAYERS = 4
M1 = M2 = 20
PIX = S * S
QB = 4
GQ = 4
GB = QB * GQ
GROUPS = B // GB
KYB = 4
KYS = M2 // KYB
BLKS = PIX // 128
MK = KYS * M1
TJ = 2 * 2 * M2
W_SCALE = 64.0
FC1 = 64
L_TXT, D = 77, 64


def wait_apart(eng, semaphore, value, passed):
    eng.wait_ge(semaphore, value)
    eng.sem_inc(passed, 1)


def split16(a):
    hi = a.astype(np.float16)
    return hi.astype(np.float32), (a - hi.astype(np.float64)).astype(np.float16).astype(np.float32)


def transforms():
    root = np.sqrt(float(S))
    ky = np.arange(M2)
    kx = np.arange(M1)
    pos = np.arange(S)
    ang = 2 * np.pi * np.outer(pos, ky) / S
    cos, sin = np.cos(ang) / root, np.sin(ang) / root
    by_step = lambda m: m.reshape(-1, KYB, KYS).transpose(0, 2, 1).reshape(-1, M2)
    f1 = np.zeros((2, S, 2, 2, M2))
    for hp in range(2):
        f1[hp, :, hp, 0] = by_step(cos)
        f1[hp, :, hp, 1] = by_step(-sin)
    f2 = np.zeros((S // 2, QB, 2, 2, M1, 2, QB))
    for hp in range(2):
        for b in range(QB):
            f2[:, b, hp, 0, :, 0, b] = cos[hp::2]
            f2[:, b, hp, 0, :, 1, b] = -sin[hp::2]
            f2[:, b, hp, 1, :, 0, b] = sin[hp::2]
            f2[:, b, hp, 1, :, 1, b] = cos[hp::2]
    i1 = np.zeros((M1, 2, 2, S))
    i1[:, 0, 0], i1[:, 1, 0] = cos.T, -sin.T
    i1[:, 0, 1], i1[:, 1, 1] = sin.T, cos.T
    twice = np.where(ky == 0, 1.0, 2.0)[None]
    i2 = np.stack([by_step(cos * twice).T, by_step(-sin * twice).T])
    f1 = f1.reshape(128, TJ)
    f2 = f2.reshape(128, 4 * M1 * QB * 2)
    i1 = i1.reshape(2 * M1, 128)
    i2 = i2.reshape(2 * M2, S)
    stack = lambda m: np.concatenate([split16(m)[0], split16(m)[0], split16(m)[1]])
    both = lambda m: np.concatenate(split16(m), axis=1)
    return {
        "f1_mat": both(f1).astype(np.float32), "f2_mat": both(f2).astype(np.float32),
        "i1_mat": stack(i1).astype(np.float32), "i2_mat": stack(i2).astype(np.float32),
        "identity": np.eye(128, dtype=np.float32),
    }


def build_operator(nc, ins, tokens):
    with ExitStack() as ctx:
        def sb(name, shape, dt):
            return ctx.enter_context(nc.sbuf_tensor(name, shape, dt))

        def sem(name):
            return ctx.enter_context(nc.semaphore(name))

        act_hl = sb("act_hl", [128, GQ, 2, PIX], F16)
        big = sb("big", [128, 32768], F16)
        v_rows = big[0:120, :].rearrange("p (h n) -> p h n", h=S)
        pixT = [big[:, n * 8192:(n + 1) * 8192].rearrange("p (s m) -> p s m", s=2)
                for n in range(2)]
        rows_flat = [big[:, 16384 + n * 5120:16384 + (n + 1) * 5120].rearrange("p (s m) -> p s m", s=2) for n in range(2)]
        rows = [big[:, 16384 + n * 5120:16384 + (n + 1) * 5120].rearrange("p (s j c) -> p s j c", s=2, j=TJ)
                for n in range(2)]
        x_in = big[0:QB * CIN, :].bitcast(F32).rearrange("p (q n) -> p q n", q=GQ)
        spec = sb("spec", [128, 2, 2 * MK, GB], F16)
        mixw = sb("mixw", [128, 2, M1, 2, 128], F16)
        w_raw = sb("w_raw", [128, 2, M1 * C], F32)
        w_hl = sb("w_hl", [128, 2, M1, 2, C], F16)
        mixed = sb("mixed", [128, 2, GB, 128], F16)
        mixedT = sb("mixedT", [128, GB, 128], F16)
        shared = sb("shared", [128, 8192], F16)
        v_out = shared[:, :].rearrange("p (u s k n) -> p u s k n", u=2, s=2, k=KYB)
        act32 = shared[:, 0:6144].bitcast(F32).rearrange("p (u n) -> p u n", u=3)
        f1_hl = sb("f1_hl", [128, 2, TJ], F16)
        f2_hl = sb("f2_hl", [128, 2, 4, 160], F16)
        i1_hl = sb("i1_hl", [120, 128], F16)
        i2_hl = sb("i2_hl", [120, S], F16)
        ident = sb("ident", [128, 128], F16)
        conv_all = sb("conv_all", [128, LAYERS, 2, 128], F16)
        conv_hl = sb("conv_hl", [128, 2, 128], F16)
        bias_all = sb("bias_all", [128, LAYERS], F32)
        bias = sb("bias", [128, 1], F32)
        lift_w = sb("lift_w", [QB * CIN, 128], F32)
        lift_b = sb("lift_b", [128, 1], F32)
        fc1_hl = sb("fc1_hl", [128, 2, 2, 128], F16)
        fc1_b = sb("fc1_b", [128, 1], F32)
        fc2_w = sb("fc2_w", [128, 2, 32], F32)
        fc2_b = sb("fc2_b", [128, 1], F32)
        hidden = shared[:, 0:4096].bitcast(F32).rearrange("p (u s n) -> p u s n", u=2, s=2)
        head_out = shared[:, 4096:6144].bitcast(F32)
        start32 = act_hl[:, 0, :, :].rearrange("p s n -> p (s n)").bitcast(F32)
        conv32 = act_hl[:, 1, :, :].rearrange("p s n -> p (s n)").bitcast(F32)

        psum = ctx.enter_context(nc.psum_tensor("psum", [128, 4096], F32))

        def bank(n, k=1):
            return psum[:, 512 * n:512 * (n + k)]

        consts_in = sem("consts_in")
        fill = sem("fill")
        zeroed = sem("zeroed")
        placed = sem("placed")
        consts_ready = sem("consts_ready")
        x_loaded = sem("x_loaded")
        layer_consts = sem("layer_consts")
        pixels_turned = sem("pixels_turned")
        turned_high = sem("turned_high")
        turned_low = sem("turned_low")
        rows_made = sem("rows_made")
        rows_high = sem("rows_high")
        rows_low = sem("rows_low")
        spec_made = sem("spec_made")
        spec_high = sem("spec_high")
        spec_low = sem("spec_low")
        w_loaded = [sem("w_loaded0"), sem("w_loaded1")]
        w_scaled = sem("w_scaled")
        w_high = sem("w_high")
        w_passed = sem("w_passed")
        w_low = sem("w_low")
        w_block = sem("w_block")
        w_spread = sem("w_spread")
        mix_made = sem("mix_made")
        mix_high = sem("mix_high")
        mix_low = sem("mix_low")
        mix_turned = sem("mix_turned")
        mixT_copied = sem("mixT_copied")
        v_made = sem("v_made")
        v_high = sem("v_high")
        v_low = sem("v_low")
        v_moved = [sem("v_moved0"), sem("v_moved1")]
        sum_made = sem("sum_made")
        gelu_made = sem("gelu_made")
        act_high = sem("act_high")
        act_low = sem("act_low")
        fc1_made = sem("fc1_made")
        hidden_made = sem("hidden_made")
        hidden_read = sem("hidden_read")
        head_copied = sem("head_copied")
        head_stored = sem("head_stored")

        CHUNKS = 4 * GQ
        MOVES = 16 * 3 * 2 * KYB
        FRONT = 8 * GQ

        def spec_sum(bank5):
            return bank5[:, 0:256 * KYS].rearrange("p (k n) -> p k n", k=KYS)[:, :, 0:8 * M1].rearrange("p k (y b) -> p k y b", b=QB)

        def spec_part(hl, q):
            return spec[:, hl, :, QB * q:QB * (q + 1)].rearrange("p (k y) b -> p k y b", k=KYS)

        def rows_sum(q, m):
            return bank(2 + (8 * q + m) % 3)[:, 0:4 * TJ].rearrange("p (c j) -> p j c", c=4)

        def mix_sum(k, half):
            return bank(2 * (k % 2) + half)[:, 0:320].rearrange("p (y b) -> p y b", b=GB)

        def mix_part(k, half, part):
            at = 40 * part + 20 * half
            return mixed[:, k % 2, :, at:at + 20].rearrange("p b y -> p y b")

        def v_sum(n):
            return bank(6 + n % 2)[:, :].rearrange("p (b k o) -> p b k o", b=4, k=KYB)

        def v_part(k, hl, n):
            return v_out[:, k % 2, hl, :, 128 * n:128 * (n + 1)].rearrange("p k (b o) -> p b k o", b=4)

        def act_chunk(hl, n):
            return act_hl[:, n // 4, hl, 1024 * (n % 4):1024 * (n % 4 + 1)]

        block = ctx.enter_context(nc.Block())

        def wait_moved(eng, it, k):
            eng.wait_ge(v_moved[k % 2], it * ((3, 2)[k % 2] * MOVES) + (k // 2 + 1) * MOVES)

        @block.sync
        def _(sp):
            sp.dma_start(start32[:, 0:160], ins["f1_mat"]).then_inc(consts_in, 16)
            sp.dma_start(start32[:, 160:1440], ins["f2_mat"]).then_inc(consts_in, 16)
            sp.dma_start(start32[0:120, 1440:1568], ins["i1_mat"]).then_inc(consts_in, 16)
            sp.dma_start(start32[0:120, 1568:1632], ins["i2_mat"]).then_inc(consts_in, 16)
            sp.dma_start(start32[:, 1632:1760], ins["identity"]).then_inc(consts_in, 16)
            sp.wait_ge(zeroed, 1)
            for b in range(QB):
                p = slice(b * C, (b + 1) * C)
                for l in range(LAYERS):
                    sp.dma_start(conv32[p, l * 128 + b * C:l * 128 + (b + 1) * C], ins["cw"][l, :, :]).then_inc(placed, 16)
                sp.dma_start(bias_all[p, :], ins["cb"]).then_inc(placed, 16)
                sp.dma_start(conv32[p, 512 + b * FC1:512 + (b + 1) * FC1], ins["fc1_w"]).then_inc(placed, 16)
                sp.dma_start(lift_w[b * CIN:(b + 1) * CIN, p], ins["fc0_w"]).then_inc(placed, 16)
                sp.dma_start(lift_b[p, :], ins["fc0_b"]).then_inc(placed, 16)
            for b2 in range(2):
                p = slice(b2 * FC1, (b2 + 1) * FC1)
                sp.dma_start(fc1_b[p, :], ins["fc1_b"]).then_inc(placed, 16)
                for pair in range(2):
                    n = 2 * pair + b2
                    sp.dma_start(fc2_w[p, pair, n:n + 1], ins["fc2_w"]).then_inc(placed, 16)
            sp.dma_start(fc2_b[:, :], ins["fc2_b"].to_broadcast([128, 1])).then_inc(placed, 16)

            with sp.Fori(0, GROUPS) as g:
                sp.wait_ge(sum_made, g * (5 * CHUNKS))
                for q in range(GQ):
                    src = ins["x"][bass.ds(g * GQ + q, 1), :, :].rearrange("a p n -> (a p) n")
                    sp.dma_start(x_in[:, q, :], src).then_inc(x_loaded, 16)
                with sp.Fori(0, LAYERS) as l:
                    it = g * LAYERS + l

                    def load_w(k):
                        sp.wait_ge(w_low, it * KYS + max(k - 1, 0))
                        src = ins["sw"][bass.ds(l * KYS + k, 1), :, :].rearrange("a p n -> (a p) n")
                        sp.dma_start(w_raw[:, k % 2, :], src).then_inc(w_loaded[k % 2], 16)

                    for k in range(KYS):
                        load_w(k)
                    for k in range(KYS):
                        sp.wait_ge(v_high, it * (4 * KYS) + 4 * k + 4)
                        sp.wait_ge(v_low, it * (4 * KYS) + 4 * k + 4)
                        for part in range(3):
                            for ri in range(2):
                                for kb in range(KYB):
                                    r = 40 * part + 20 * ri + k * KYB + kb
                                    sp.dma_start(v_rows[r:r + 1, :, :], v_out[ri * S:(ri + 1) * S, k % 2, part % 2, kb, :])\
                                        .then_inc(v_moved[k % 2], 16)
                for q in range(GQ):
                    sp.wait_ge(head_copied, g * GQ + q + 1)
                    for j in range(4):
                        dst = tokens[bass.ds(g * GB + q * QB, QB), :].rearrange("b (u j n) -> b u j n", u=2, j=4)[:, :, j, :]
                        src = head_out[32 * j:32 * j + QB, :].rearrange("p (u n) -> p u n", u=2)
                        sp.dma_start(dst, src).then_inc(head_stored, 16)
            sp.wait_ge(head_stored, GROUPS * GQ * 4 * 16)

        @block.gpsimd
        def _(pool):
            with pool.Fori(0, GROUPS * LAYERS) as it:
                for k in range(KYS):
                    pool.wait_ge(w_loaded[k % 2], it * (16 * (3, 2)[k % 2]) + 16 * (k // 2 + 1))
                    wait_apart(pool, w_spread, it * KYS + max(k - 1, 0), w_passed)
                    raw = w_raw[:, k % 2, :].rearrange("p (x o) -> p x o", x=M1)
                    nc.gpsimd.tensor_scalar(raw, raw, W_SCALE, None, ALU.mult).then_inc(w_scaled, 1)
                    wait_apart(pool, w_scaled, it * KYS + k + 1, w_passed)
                    nc.gpsimd.tensor_copy(w_hl[:, k % 2, :, 0, :], raw).then_inc(w_high, 1)
                    pool.wait_ge(w_high, it * KYS + k + 1)
                    nc.gpsimd.tensor_tensor(w_hl[:, k % 2, :, 1, :], raw, w_hl[:, k % 2, :, 0, :], ALU.subtract).then_inc(w_low, 1)

        @block.scalar
        def _(act):
            act.wait_ge(consts_ready, 1)

            def activate(n5, n, func, add):
                act.wait_ge(sum_made, n5 * CHUNKS + n + 1)
                act.wait_ge(act_low, n5 * CHUNKS + max(n - 2, 0))
                nc.scalar.activation(act32[:, n % 3, :], bank(2 * (n % 4), 2), func, bias=add).then_inc(gelu_made, 1)

            with act.Fori(0, GROUPS) as g:
                act.wait_ge(head_stored, g * (GQ * 4 * 16))
                for n in range(CHUNKS):
                    activate(g * 5, n, ACT.Identity, lift_b[:, :])
                with act.Fori(0, LAYERS) as l:
                    it = g * LAYERS + l

                    def copy_turned(q):
                        for n in range(0, 8, 2):
                            act.wait_ge(pixels_turned, it * FRONT + 8 * q + n + 1)
                            if q >= 2:
                                act.wait_ge(rows_made, it * FRONT + 8 * (q - 1))
                            nc.scalar.activation(pixT[q % 2][:, 0, 1024 * (n // 2):1024 * (n // 2 + 1)], bank(0).bitcast(F16), ACT.Copy)\
                                .then_inc(turned_high, 1)

                    copy_turned(0)
                    for q in range(GQ):
                        for m in range(8):
                            act.wait_ge(rows_made, it * FRONT + 8 * q + m + 1)
                            if q >= 2:
                                act.wait_ge(spec_made, it * GQ + q - 1)
                            nc.scalar.activation(rows[q % 2][:, 0, :, 4 * m:4 * m + 4], rows_sum(q, m), ACT.Copy).then_inc(rows_high, 1)
                        if q + 1 < GQ:
                            copy_turned(q + 1)
                        act.wait_ge(spec_made, it * GQ + q + 1)
                        nc.scalar.activation(spec_part(0, q), spec_sum(bank(5, 3)), ACT.Copy).then_inc(spec_high, 1)
                    for step in range(KYS + 2):
                        k = step
                        if k < KYS:
                            for half in range(2):
                                act.wait_ge(mix_made, it * (2 * KYS) + 2 * k + half + 1)
                                if k >= 2:
                                    act.wait_ge(mix_turned, it * (2 * KYS) + 2 * (k - 1))
                                for part in (0, 2):
                                    nc.scalar.activation(mix_part(k, half, part), mix_sum(k, half), ACT.Copy, scale=1.0 / W_SCALE)\
                                        .then_inc(mix_high, 1)
                        k = step - 2
                        if k >= 0:
                            for n in range(4):
                                act.wait_ge(v_made, it * (4 * KYS) + 4 * k + n + 1)
                                if n == 0 and k >= 2:
                                    wait_moved(act, it, k - 2)
                                nc.scalar.activation(v_part(k, 0, n), v_sum(n), ACT.Copy).then_inc(v_high, 1)
                    act.wait_ge(layer_consts, it * 2 + 2)
                    for n in range(CHUNKS):
                        activate(g * 5 + (l + 1), n, ACT.Gelu, bias[:, :])
                for n in range(8 * GQ):
                    act.wait_ge(fc1_made, g * (8 * GQ) + n + 1)
                    if n < 2:
                        act.wait_ge(act_low, (g * 5 + 5) * CHUNKS)
                    else:
                        act.wait_ge(hidden_read, g * (8 * GQ) + n - 1)
                    nc.scalar.activation(hidden[:, n % 2, :, :], bank(2 * (n % 3), 2).rearrange("p (s n) -> p s n", s=2), ACT.Gelu, bias=fc1_b[:, :])\
                        .then_inc(hidden_made, 1)

        @block.vector
        def _(dve):
            for t in (conv32[:, 0:768], lift_w[:, :], fc2_w[:, :, :], mixw[:, :, :, :, :], mixed[:, :, :, :]):
                nc.vector.memset(t, 0.0).then_inc(fill, 1)
            dve.wait_ge(fill, 5)
            dve.sem_inc(zeroed, 1)
            dve.wait_ge(consts_in, 5 * 16)
            nc.vector.tensor_copy(f1_hl[:, :, :], start32[:, 0:160].rearrange("p (s n) -> p s n", s=2)).then_inc(fill, 1)
            nc.vector.tensor_copy(f2_hl[:, :, :, :], start32[:, 160:1440].rearrange("p (s m n) -> p s m n", s=2, m=4)).then_inc(fill, 1)
            nc.vector.tensor_copy(i1_hl[:, :], start32[0:120, 1440:1568]).then_inc(fill, 1)
            nc.vector.tensor_copy(i2_hl[:, :], start32[0:120, 1568:1632]).then_inc(fill, 1)
            nc.vector.tensor_copy(ident[:, :], start32[:, 1632:1760]).then_inc(fill, 1)
            dve.wait_ge(placed, 16 * (8 * QB + 7))
            conv_raw = conv32[:, 0:512].rearrange("p (l n) -> p l n", l=LAYERS)
            fc1_raw = conv32[:, 512:768].rearrange("p (l n) -> p l n", l=2)
            nc.vector.tensor_copy(conv_all[:, :, 0, :], conv_raw).then_inc(fill, 1)
            nc.vector.tensor_copy(fc1_hl[:, :, 0, :], fc1_raw).then_inc(fill, 1)
            dve.wait_ge(fill, 12)
            nc.vector.tensor_tensor(conv_all[:, :, 1, :], conv_raw, conv_all[:, :, 0, :], ALU.subtract).then_inc(fill, 1)
            nc.vector.tensor_tensor(fc1_hl[:, :, 1, :], fc1_raw, fc1_hl[:, :, 0, :], ALU.subtract).then_inc(fill, 1)
            dve.wait_ge(fill, 14)
            dve.sem_inc(consts_ready, 1)

            def split_chunk(n5, n):
                dve.wait_ge(gelu_made, n5 * CHUNKS + n + 1)
                nc.vector.tensor_copy(act_chunk(0, n), act32[:, n % 3, :]).then_inc(act_high, 1)
                dve.wait_ge(act_high, n5 * CHUNKS + n + 1)
                nc.vector.tensor_tensor(act_chunk(1, n), act32[:, n % 3, :], act_chunk(0, n), ALU.subtract).then_inc(act_low, 1)

            with dve.Fori(0, GROUPS) as g:
                for n in range(CHUNKS):
                    split_chunk(g * 5, n)
                with dve.Fori(0, LAYERS) as l:
                    it = g * LAYERS + l
                    nc.vector.tensor_copy(conv_hl[:, :, :], conv_all[:, bass.ds(l, 1), :, :].rearrange("p a s n -> p (a s) n")).then_inc(layer_consts, 1)
                    nc.vector.tensor_copy(bias[:, :], bias_all[:, bass.ds(l, 1)]).then_inc(layer_consts, 1)

                    def spread(k):
                        dve.wait_ge(w_low, it * KYS + k + 1)
                        if k >= 2:
                            dve.wait_ge(mix_made, it * (2 * KYS) + 2 * (k - 1))
                        for b in range(KYB):
                            p = slice(b * C, (b + 1) * C)
                            last = nc.vector.tensor_copy(mixw[p, k % 2, :, :, b * C:(b + 1) * C], w_hl[p, k % 2, :, :, :])
                            last.then_inc(w_block, 1)
                        dve.wait_ge(w_block, it * (KYS * KYB) + (k + 1) * KYB)
                        dve.sem_inc(w_spread, 1)

                    def copy_turned(q):
                        for n in range(1, 8, 2):
                            dve.wait_ge(pixels_turned, it * FRONT + 8 * q + n + 1)
                            if q >= 2:
                                dve.wait_ge(rows_made, it * FRONT + 8 * (q - 1))
                            nc.vector.tensor_copy(pixT[q % 2][:, 1, 1024 * (n // 2):1024 * (n // 2 + 1)], bank(1).bitcast(F16)).then_inc(turned_low, 1)

                    spread(0)
                    spread(1)
                    copy_turned(0)
                    for q in range(GQ):
                        for m in range(8):
                            dve.wait_ge(rows_high, it * FRONT + 8 * q + m + 1)
                            nc.vector.tensor_tensor(rows[q % 2][:, 1, :, 4 * m:4 * m + 4], rows_sum(q, m), rows[q % 2][:, 0, :, 4 * m:4 * m + 4],
                                                    ALU.subtract).then_inc(rows_low, 1)
                        if q + 1 < GQ:
                            copy_turned(q + 1)
                        dve.wait_ge(spec_high, it * GQ + q + 1)
                        nc.vector.tensor_tensor(spec_part(1, q), spec_sum(bank(5, 3)), spec_part(0, q), ALU.subtract).then_inc(spec_low, 1)
                    for step in range(KYS + 2):
                        k = step
                        if k < KYS:
                            for half in range(2):
                                dve.wait_ge(mix_high, it * (4 * KYS) + 4 * k + 2 * half + 2)
                                nc.vector.scalar_tensor_tensor(out=mix_part(k, half, 1), in0=mix_sum(k, half), scalar=1.0 / W_SCALE,
                                                               in1=mix_part(k, half, 0), op0=ALU.mult, op1=ALU.subtract).then_inc(mix_low, 1)
                            if k + 2 < KYS:
                                spread(k + 2)
                        k = step - 2
                        if k >= 0:
                            for n in range(4):
                                dve.wait_ge(v_high, it * (4 * KYS) + 4 * k + n + 1)
                                nc.vector.tensor_tensor(v_part(k, 1, n), v_sum(n), v_part(k, 0, n), ALU.subtract).then_inc(v_low, 1)
                        k = step - 1
                        if 0 <= k < KYS:
                            for half in range(2):
                                dve.wait_ge(mix_turned, it * (2 * KYS) + 2 * k + half + 1)
                                if k >= 1:
                                    dve.wait_ge(v_made, it * (4 * KYS) + 4 * (k - 1) + 2 * half + 2)
                                nc.vector.tensor_copy(mixedT[:, 8 * half:8 * half + 8, :].rearrange("p b n -> p (b n)"), bank(4 + half).bitcast(F16))\
                                    .then_inc(mixT_copied, 1)
                    for n in range(CHUNKS):
                        split_chunk(g * 5 + (l + 1), n)
                for q in range(GQ):
                    dve.wait_ge(hidden_read, g * (8 * GQ) + 8 * q + 8)
                    dve.wait_ge(head_stored, (g * GQ + q) * (4 * 16))
                    nc.vector.tensor_scalar(head_out, bank(6, 2), fc2_b[:, :], None, ALU.add).then_inc(head_copied, 1)

        @block.tensor
        def _(pe):
            pe.wait_ge(consts_ready, 1)

            def three(out, weights, data, start, stop):
                for n, (a, b) in enumerate(((0, 0), (0, 1), (1, 0))):
                    last = nc.tensor.matmul(out, weights[a], data[b], start=start and n == 0, stop=stop and n == 2)
                return last

            with pe.Fori(0, GROUPS) as g:
                for n in range(CHUNKS):
                    if n == 0:
                        pe.wait_ge(x_loaded, (g + 1) * (GQ * 16))
                        pe.wait_ge(head_copied, g * GQ)
                    if n >= 4:
                        pe.wait_ge(gelu_made, (g * 5) * CHUNKS + n - 3)
                    for half in range(2):
                        at = 1024 * (n % 4) + 512 * half
                        last = nc.tensor.matmul(bank(2 * (n % 4) + half), lift_w[:, :], x_in[:, n // 4, at:at + 512], start=True, stop=True)
                    last.then_inc(sum_made, 1)
                with pe.Fori(0, LAYERS) as l:
                    it = g * LAYERS + l

                    def turn_pixels(q):
                        pe.wait_ge(act_low, (g * 5 + l) * CHUNKS + 4 * (q + 1))
                        for n in range(8):
                            t = 8 * q + n
                            if t == 0:
                                pe.wait_ge(gelu_made, (g * 5 + (l + 1)) * CHUNKS)
                            if t >= 2:
                                done = (turned_high, turned_low)[n % 2]
                                pe.wait_ge(done, it * (FRONT // 2) + t // 2)
                            for j in range(8):
                                at = 128 * (8 * (n // 2) + j)
                                last = nc.tensor.transpose(bank(n % 2).bitcast(F16)[:, 128 * j:128 * (j + 1)],
                                                           act_hl[:, q, n % 2, at:at + 128], ident[:, :])
                            last.then_inc(pixels_turned, 1)

                    def to_rows(q):
                        pe.wait_ge(turned_high, it * (FRONT // 2) + 4 * (q + 1))
                        pe.wait_ge(turned_low, it * (FRONT // 2) + 4 * (q + 1))
                        for m in range(8):
                            t = 8 * q + m
                            if t >= 3:
                                pe.wait_ge(rows_low, it * FRONT + t - 2)
                            for j in range(4):
                                c = 4 * m + j
                                pix = [pixT[q % 2][:, s, c::C] for s in range(2)]
                                last = three(bank(2 + t % 3)[:, TJ * j:TJ * (j + 1)], pix, [f1_hl[:, 0, :], f1_hl[:, 1, :]], True, True)
                            last.then_inc(rows_made, 1)

                    def to_spectrum(q):
                        pe.wait_ge(rows_low, it * FRONT + 8 * (q + 1))
                        if q >= 1:
                            pe.wait_ge(spec_low, it * GQ + q)
                        for k in range(KYS):
                            out = bank(5, 3)[:, 256 * k:256 * k + 160]
                            for r in range(4):
                                at = (r * KYS + k) * KYB
                                lhs = [rows_flat[q % 2][:, s, C * at:C * (at + KYB)] for s in range(2)]
                                last = three(out, lhs, [f2_hl[:, 0, r, :], f2_hl[:, 1, r, :]], r == 0, r == 3)
                        last.then_inc(spec_made, 1)

                    turn_pixels(0)
                    for q in range(GQ):
                        to_rows(q)
                        if q + 1 < GQ:
                            turn_pixels(q + 1)
                        to_spectrum(q)

                    pe.wait_ge(spec_low, it * GQ + GQ)
                    for step in range(KYS + 2):
                        k = step
                        if k < KYS:
                            pe.wait_ge(w_spread, it * KYS + k + 1)
                            if k >= 2:
                                pe.wait_ge(mix_high, it * (4 * KYS) + 4 * (k - 1))
                                pe.wait_ge(mix_low, it * (2 * KYS) + 2 * (k - 1))
                            for x in range(M1):
                                out = bank(2 * (k % 2) + x // 10)[:, 32 * (x % 10):32 * (x % 10 + 1)]
                                w = [mixw[:, k % 2, x, s, :] for s in range(2)]
                                last = three(out, w, [spec[:, s, 2 * (k * M1 + x):2 * (k * M1 + x) + 2, :] for s in range(2)], True, True)
                                if x % 10 == 9:
                                    last.then_inc(mix_made, 1)
                        k = step - 1
                        if 0 <= k < KYS:
                            pe.wait_ge(mix_high, it * (4 * KYS) + 4 * (k + 1))
                            pe.wait_ge(mix_low, it * (2 * KYS) + 2 * (k + 1))
                            for half in range(2):
                                if k >= 1:
                                    pe.wait_ge(mixT_copied, it * (2 * KYS) + 2 * (k - 1) + half + 1)
                                for j in range(8):
                                    last = nc.tensor.transpose(bank(4 + half).bitcast(F16)[:, 128 * j:128 * (j + 1)],
                                                               mixed[:, k % 2, 8 * half + j, :], ident[:, :])
                                last.then_inc(mix_turned, 1)
                        k = step - 2
                        if k >= 0:
                            for n in range(4):
                                t = 4 * k + n
                                pe.wait_ge(mixT_copied, it * (2 * KYS) + 2 * k + n // 2 + 1)
                                if t >= 2:
                                    pe.wait_ge(v_low, it * (4 * KYS) + t - 1)
                                nc.tensor.matmul(bank(6 + n % 2), i1_hl[:, :], mixedT[0:120, 4 * n:4 * n + 4, :], start=True, stop=True)\
                                    .then_inc(v_made, 1)

                    pe.wait_ge(layer_consts, it * 2 + 2)
                    wait_moved(pe, it, KYS - 1)
                    wait_moved(pe, it, KYS - 2)
                    for n in range(CHUNKS):
                        if n >= 4:
                            pe.wait_ge(gelu_made, (g * 5 + (l + 1)) * CHUNKS + n - 3)
                        for half in range(2):
                            out = bank(2 * (n % 4) + half)
                            at = 1024 * (n % 4) + 512 * half
                            three(out, [conv_hl[:, s, :] for s in range(2)], [act_hl[:, n // 4, s, at:at + 512] for s in range(2)], True, False)
                            for r in range(8):
                                last = nc.tensor.matmul(out[:, S * r:S * (r + 1)], v_rows[:, at // S + r, 128 * (n // 4):128 * (n // 4 + 1)],
                                                        i2_hl[:, :], start=False, stop=r == 7)
                        last.then_inc(sum_made, 1)

                pe.wait_ge(act_low, (g * 5 + 5) * CHUNKS)
                for n in range(8 * GQ + 1):
                    if n < 8 * GQ:
                        if n >= 3:
                            pe.wait_ge(hidden_made, g * (8 * GQ) + n - 2)
                        at = 512 * (n % 8)
                        for pair in range(2):
                            last = three(bank(2 * (n % 3) + pair), [fc1_hl[:, pair, s, :] for s in range(2)],
                                         [act_hl[:, n // 8, s, at:at + 512] for s in range(2)], True, True)
                        last.then_inc(fc1_made, 1)
                    if n >= 1:
                        m = n - 1
                        pe.wait_ge(hidden_made, g * (8 * GQ) + m + 1)
                        if m % 8 == 0:
                            pe.wait_ge(head_copied, g * GQ + m // 8)
                        row = 32 * (m % 4)
                        for pair in range(2):
                            last = nc.tensor.matmul(bank(6 + (m % 8) // 4)[row:row + 32, :], fc2_w[:, pair, :], hidden[:, m % 2, pair, :],
                                                    start=pair == 0, stop=pair == 1)
                        last.then_inc(hidden_read, 1)


PAIRS = 4
BATCHES = B // (2 * PAIRS)
CH = 3 * PAIRS
PW = 3 * 128
HEADS = 8
HD = D // HEADS
FF = 2 * D
EXPERTS, TOP = 8, 2
LN_EPS, ATT_EPS = 1e-5, 1e-6


def token_tables():
    head = np.arange(D) // HD
    one_head = (head[:, None] == head[None, :]).astype(np.float32)
    pick = np.repeat(np.eye(EXPERTS, dtype=np.float32)[:, :, None], 128, axis=2).reshape(EXPERTS, EXPERTS * 128)
    before = (np.arange(EXPERTS)[None, :] < np.arange(EXPERTS)[:, None]).astype(np.float32).reshape(1, -1)
    return {"one_head": one_head, "pick": pick, "before": np.ascontiguousarray(np.broadcast_to(before, (128, 64))),
            "identity": np.eye(128, dtype=np.float32)}


def build_tokens(nc, ins, tokens, out):
    with ExitStack() as ctx:
        def sb(name, shape, dt=F32):
            return ctx.enter_context(nc.sbuf_tensor(name, shape, dt))

        def sem(name):
            return ctx.enter_context(nc.semaphore(name))

        h_in = sb("h_in", [128, CH, D])
        h_mid = sb("h_mid", [128, CH, D])
        h_out = sb("h_out", [128, CH, D])
        xm = sb("xm", [128, CH, 2 * D])
        centred = sb("centred", [128, CH, D])
        squares = sb("squares", [128, CH, D])
        stat = sb("stat", [128, 4, CH])
        xT = sb("xT", [D, PAIRS, PW])
        q_neg = sb("q_neg", [D, PAIRS, PW])
        q_exp = sb("q_exp", [D, PAIRS, PW])
        q_pos = sb("q_pos", [D, PAIRS, PW])
        k_neg = sb("k_neg", [128, CH, D])
        k_exp = sb("k_exp", [128, CH, D])
        k_pos = sb("k_pos", [128, CH, D])
        v_one = sb("v_one", [128, CH, D + 1])
        kv_head = sb("kv_head", [D, 2 * PAIRS, 2, D])
        z_inv = sb("z_inv", [D, PAIRS, PW])
        msgT = sb("msgT", [D, PAIRS, PW])
        xmT = sb("xmT", [128, PAIRS, PW])
        hid = sb("hid", [128, PAIRS, PW])
        xn = sb("xn", [128, CH, D])
        xnT = sb("xnT", [D, PAIRS, PW])
        logit = sb("logit", [128, CH, EXPERTS])
        cmp_gt = sb("cmp_gt", [128, CH, EXPERTS, EXPERTS])
        cmp_eq = sb("cmp_eq", [128, CH, EXPERTS, EXPERTS])
        rank = sb("rank", [128, CH, EXPERTS])
        rexp = sb("rexp", [128, CH, EXPERTS])
        gate = sb("gate", [128, CH, EXPERTS])
        gateT = sb("gateT", [EXPERTS, PAIRS, PW])
        eh = sb("eh", [128, 2, PW])
        eg = sb("eg", [128, 2, PW])
        yT = sb("yT", [D, PAIRS, PW])
        ident = sb("t_ident", [128, 128])
        one_head = sb("one_head", [D, D])
        pick = sb("pick", [EXPERTS, EXPERTS, 128])
        before = sb("before", [128, EXPERTS, EXPERTS])
        wq = sb("wq", [D, D])
        wkv = sb("wkv", [D, 2 * D])
        wm = sb("wm", [D, D])
        w1 = sb("w1", [FF, FF])
        w2 = sb("w2", [FF, D])
        vecs = sb("vecs", [128, 6, D])
        wr = sb("wr", [D, EXPERTS])
        br = sb("br", [128, EXPERTS])
        ew1 = sb("ew1", [D, EXPERTS, FF])
        eb1 = sb("eb1", [FF, EXPERTS])
        ew2 = sb("ew2", [FF, EXPERTS, D])
        eb2 = sb("eb2", [EXPERTS, D])
        psum = ctx.enter_context(nc.psum_tensor("t_psum", [128, 4096], F32))

        def pairs_at(first, rows=128):
            return psum[0:rows, 512 * first:512 * (first + PAIRS)].rearrange("p (n w) -> p n w", n=PAIRS)[:, :, 0:PW]

        def chunk_at(first, ch, width):
            per = 512 // width
            at = 512 * (first + ch // per) + width * (ch % per)
            return psum[:, at:at + width]

        def chunks_at(first, width):
            return psum[:, 512 * first:512 * first + width * CH].rearrange("p (n w) -> p n w", n=CH)

        def col(t, ch):
            return t[:, ch // 3, 128 * (ch % 3):128 * (ch % 3 + 1)]

        w_in = sem("w_in")
        ones_set = sem("ones_set")
        pe_passed = sem("pe_passed")
        loaded = sem("loaded")
        dve_step = sem("dve_step")
        x_made = sem("x_made")
        x_turned = sem("x_turned")
        xT_copied = sem("xT_copied")
        qkv_made = sem("qkv_made")
        neg_made = sem("neg_made")
        exp_made = sem("exp_made")
        v_copied = sem("v_copied")
        qk_made = sem("qk_made")
        kv_made = sem("kv_made")
        kv_masked = sem("kv_masked")
        msg_summed = sem("msg_summed")
        msg_made = sem("msg_made")
        msg_mixed = sem("msg_mixed")
        message_normed = sem("message_normed")
        xm_turned = sem("xm_turned")
        xmT_copied = sem("xmT_copied")
        hid_summed = sem("hid_summed")
        hid_made = sem("hid_made")
        msg2_made = sem("msg2_made")
        h_mid_made = sem("h_mid_made")
        xn_made = sem("xn_made")
        xn_turned = sem("xn_turned")
        xnT_copied = sem("xnT_copied")
        logits_made = sem("logits_made")
        rexp_in = sem("rexp_in")
        rexp_made = sem("rexp_made")
        gate_made = sem("gate_made")
        gate_turned = sem("gate_turned")
        gateT_copied = sem("gateT_copied")
        e_summed = sem("e_summed")
        e_gelu = sem("e_gelu")
        e_gated = sem("e_gated")
        e_added = sem("e_added")
        y_copied = sem("y_copied")
        y_turned = sem("y_turned")
        out_made = sem("out_made")
        stored = sem("stored")

        block = ctx.enter_context(nc.Block())
        weights = [(ident[:, :], "identity"), (one_head[:, :], "one_head"), (pick[:, :, :].rearrange("p e n -> p (e n)"), "pick"),
                   (before[:, :, :].rearrange("p a b -> p (a b)"), "before"), (wq[:, :], "Wq"), (wkv[:, 0:D], "Wk"), (wkv[:, D:2 * D], "Wv"),
                   (wm[:, :], "Wm"), (w1[:, :], "W1"), (w2[:, :], "W2"), (wr[:, :], "Wr"), (eb1[:, :], "eb1"), (eb2[:, :], "eb2"),
                   (ew1[:, :, :], "ew1"), (ew2[:, :, :], "ew2")]
        vectors = ["g1", "b1", "g2", "b2", "gamma", "beta"]
        N_W = len(weights) + len(vectors) + 1
        tok_rows = tokens.rearrange("b (h w) -> (b h) w", h=S)
        rows_view = lambda t: t[:, :, :].rearrange("p (n t) w -> p n t w", t=3)

        @block.sync
        def _(sp):
            for dst, name in weights:
                sp.dma_start(dst, ins[name]).then_inc(w_in, 16)
            for n, name in enumerate(vectors):
                sp.dma_start(vecs[:, n, :], ins[name].to_broadcast([128, D])).then_inc(w_in, 16)
            sp.dma_start(br[:, :], ins["br"].to_broadcast([128, EXPERTS])).then_inc(w_in, 16)
            sp.wait_ge(ones_set, 1)
            with sp.Fori(0, BATCHES) as it:
                sp.wait_ge(h_mid_made, it)
                src = tok_rows[bass.ds(it * (PAIRS * 128), PAIRS * 128), :].rearrange("(n p) w -> p n w", p=128)
                sp.dma_start(rows_view(h_in)[:, :, 1, :], src).then_inc(loaded, 16)
                src = ins["txt"][bass.ds(it * PAIRS, PAIRS), :, :, :].rearrange("n t p w -> p n t w")
                for t in range(2):
                    sp.dma_start(rows_view(h_in)[0:L_TXT, :, 2 * t, :], src[:, :, t, :]).then_inc(loaded, 16)
                sp.wait_ge(out_made, it + 1)
                dst = out[bass.ds(it * PAIRS, PAIRS), :, :, :].rearrange("n t p w -> p n t w")
                for t in range(2):
                    sp.dma_start(dst[0:S, :, t, :], rows_view(h_out)[S * t:S * (t + 1), :, 1, :]).then_inc(stored, 16)
                    sp.dma_start(dst[S:S + L_TXT, :, t, :], rows_view(h_out)[0:L_TXT, :, 2 * t, :]).then_inc(stored, 16)
            sp.wait_ge(stored, BATCHES * 4 * 16)

        @block.tensor
        def _(pe):
            mm = nc.tensor.matmul
            pe.wait_ge(w_in, 16 * N_W)
            with pe.Fori(0, BATCHES) as it:
                wait_apart(pe, x_made, it + 1, pe_passed)
                for ch in range(CH):
                    last = nc.tensor.transpose(col(pairs_at(0, D), ch), xm[:, ch, 0:D], ident[:, :])
                last.then_inc(x_turned, 1)
                wait_apart(pe, xT_copied, it + 1, pe_passed)
                for n in range(PAIRS):
                    mm(pairs_at(0, D)[:, n, :], wq[:, :], xT[:, n, :], start=True, stop=True)
                for ch in range(CH):
                    last = mm(chunk_at(4, ch, 128), col(xT, ch), wkv[:, :], start=True, stop=True)
                last.then_inc(qkv_made, 1)
                wait_apart(pe, qk_made, it + 1, pe_passed)
                wait_apart(pe, v_copied, it + 1, pe_passed)
                for i in range(2 * PAIRS):
                    n, t = i // 2, i % 2
                    dst = psum[0:D, 512 * (4 + t) + 65 * n:512 * (4 + t) + 65 * (n + 1)]
                    r = slice(S * t, S * (t + 1))
                    mm(dst, k_pos[r, 3 * n + 1, :], v_one[r, 3 * n + 1, :], start=True, stop=False)
                    last = mm(dst, k_pos[0:L_TXT, 3 * n + 2 * t, :], v_one[0:L_TXT, 3 * n + 2 * t, :], start=False, stop=True)
                last.then_inc(kv_made, 1)
                wait_apart(pe, kv_masked, it + 1, pe_passed)
                for i in range(2 * PAIRS):
                    n, t = i // 2, i % 2
                    c = slice(192 * t, 192 * (t + 1))
                    for part in range(2):
                        last = mm(pairs_at(4 * part, D)[:, n, c], kv_head[:, i, part, :], q_pos[:, n, c], start=True, stop=True)
                last.then_inc(msg_summed, 1)
                wait_apart(pe, msg_made, it + 1, pe_passed)
                for ch in range(CH):
                    last = mm(chunk_at(0, ch, D), col(msgT, ch), wm[:, :], start=True, stop=True)
                last.then_inc(msg_mixed, 1)
                wait_apart(pe, message_normed, it + 1, pe_passed)
                for ch in range(CH):
                    last = nc.tensor.transpose(col(pairs_at(4), ch), xm[:, ch, :], ident[:, :])
                last.then_inc(xm_turned, 1)
                pe.wait_ge(xmT_copied, it + 1)
                for n in range(PAIRS):
                    last = mm(pairs_at(0)[:, n, :], w1[:, :], xmT[:, n, :], start=True, stop=True)
                last.then_inc(hid_summed, 1)
                pe.wait_ge(hid_made, it + 1)
                for ch in range(CH):
                    last = mm(chunk_at(4, ch, D), col(hid, ch), w2[:, :], start=True, stop=True)
                last.then_inc(msg2_made, 1)
                wait_apart(pe, xn_made, it + 1, pe_passed)
                for ch in range(CH):
                    last = nc.tensor.transpose(col(pairs_at(0, D), ch), xn[:, ch, :], ident[:, :])
                last.then_inc(xn_turned, 1)
                wait_apart(pe, xnT_copied, it + 1, pe_passed)
                for ch in range(CH):
                    last = mm(chunk_at(4, ch, EXPERTS), col(xnT, ch), wr[:, :], start=True, stop=True)
                last.then_inc(logits_made, 1)
                wait_apart(pe, gate_made, it + 1, pe_passed)
                for ch in range(CH):
                    last = nc.tensor.transpose(col(pairs_at(0, EXPERTS), ch), gate[:, ch, :], ident[:, :])
                last.then_inc(gate_turned, 1)
                wait_apart(pe, gateT_copied, it + 1, pe_passed)
                STEPS = PAIRS * EXPERTS
                for s in range(STEPS + 1):
                    if s < STEPS:
                        if s >= 2:
                            pe.wait_ge(e_gated, it * STEPS + s - 1)
                        n, e = s // EXPERTS, s % EXPERTS
                        mm(psum[:, 512 * (s % 2):512 * (s % 2) + PW], ew1[:, e, :], xnT[:, n, :], start=True, stop=True)
                        mm(psum[:, 512 * (2 + s % 2):512 * (2 + s % 2) + PW], pick[:, e, :], gateT[:, n, :], start=True, stop=True)\
                            .then_inc(e_summed, 1)
                    if s >= 1:
                        m = s - 1
                        n, e = m // EXPERTS, m % EXPERTS
                        wait_apart(pe, e_gated, it * STEPS + m + 1, pe_passed)
                        if e == 0:
                            mm(pairs_at(4, D)[:, n, :], eb2[:, :], gateT[:, n, :], start=True, stop=False)
                        mm(pairs_at(4, D)[:, n, :], ew2[:, e, :], eg[:, m % 2, :], start=False, stop=e == EXPERTS - 1).then_inc(e_added, 1)
                wait_apart(pe, y_copied, it + 1, pe_passed)
                for ch in range(CH):
                    last = nc.tensor.transpose(chunk_at(0, ch, D), col(yT, ch), ident[0:D, 0:D])
                last.then_inc(y_turned, 1)

        @block.scalar
        def _(act):
            A = nc.scalar.activation
            act.wait_ge(w_in, 16 * N_W)
            with act.Fori(0, BATCHES) as it:
                act.wait_ge(x_turned, it + 1)
                A(xT[:, :, :], pairs_at(0, D), ACT.Copy).then_inc(xT_copied, 1)
                act.wait_ge(neg_made, it + 1)
                A(q_exp[:, :, :], q_neg[:, :, :], ACT.Exp)
                A(k_exp[:, :, :], k_neg[:, :, :], ACT.Exp).then_inc(exp_made, 1)
                act.wait_ge(qk_made, it + 1)
                A(v_one[:, :, 0:D], chunks_at(4, 128)[:, :, D:2 * D], ACT.Copy).then_inc(v_copied, 1)
                act.wait_ge(xm_turned, it + 1)
                A(xmT[:, :, :], pairs_at(4), ACT.Copy).then_inc(xmT_copied, 1)
                act.wait_ge(hid_summed, it + 1)
                A(hid[:, :, :], pairs_at(0), ACT.Relu).then_inc(hid_made, 1)
                act.wait_ge(xn_turned, it + 1)
                A(xnT[:, :, :], pairs_at(0, D), ACT.Copy).then_inc(xnT_copied, 1)
                act.wait_ge(rexp_in, it + 1)
                A(rexp[:, :, :], logit[:, :, :], ACT.Exp).then_inc(rexp_made, 1)
                act.wait_ge(gate_turned, it + 1)
                A(gateT[:, :, :], pairs_at(0, EXPERTS), ACT.Copy).then_inc(gateT_copied, 1)
                STEPS = PAIRS * EXPERTS
                for s in range(STEPS):
                    act.wait_ge(e_summed, it * STEPS + s + 1)
                    if s >= 2:
                        act.wait_ge(e_gated, it * STEPS + s - 1)
                    A(eh[:, s % 2, :], psum[:, 512 * (s % 2):512 * (s % 2) + PW], ACT.Gelu, bias=eb1[:, s % EXPERTS:s % EXPERTS + 1]).then_inc(e_gelu, 1)
                act.wait_ge(e_added, (it + 1) * STEPS)
                A(yT[:, :, :], pairs_at(4, D), ACT.Copy).then_inc(y_copied, 1)

        @block.vector
        def _(dve):
            V = nc.vector
            V.memset(h_in[:, :, :], 0.0).then_inc(dve_step, 1)
            V.memset(v_one[:, :, :], 1.0).then_inc(dve_step, 1)
            dve.wait_ge(dve_step, 2)
            dve.sem_inc(ones_set, 1)
            dve.wait_ge(w_in, 16 * N_W)
            LINKS = 122
            with dve.Fori(0, BATCHES) as it:
                n = [2]

                def link(instruction):
                    n[0] += 1
                    instruction.then_inc(dve_step, 1)
                    dve.wait_ge(dve_step, it * LINKS + n[0])

                def wide(t):
                    return t.unsqueeze(2).to_broadcast([128, CH, D])

                def rsqrt(y, v, t, u):
                    link(V.tensor_scalar(t.bitcast(I32), v.bitcast(I32), 1, None, ALU.logical_shift_right))
                    link(V.tensor_scalar(y.bitcast(I32), t.bitcast(I32), -1.0, float(0x5F3759DF), ALU.mult, ALU.add))
                    for _ in range(3):
                        link(V.tensor_tensor(t, v, y, ALU.mult))
                        link(V.tensor_tensor(u, t, y, ALU.mult))
                        link(V.tensor_scalar(t, u, -0.5, 1.5, ALU.mult, ALU.add))
                        link(V.tensor_tensor(y, y, t, ALU.mult))

                def norm(dst, src):
                    link(V.tensor_reduce(stat[:, 0, :], src, AX.X, ALU.add))
                    link(V.tensor_scalar(stat[:, 1, :], stat[:, 0, :], 1.0 / D, None, ALU.mult))
                    link(V.tensor_tensor(centred[:, :, :], src, wide(stat[:, 1, :]), ALU.subtract))
                    link(V.tensor_tensor(squares[:, :, :], centred[:, :, :], centred[:, :, :], ALU.mult))
                    link(V.tensor_reduce(stat[:, 2, :], squares[:, :, :], AX.X, ALU.add))
                    link(V.tensor_scalar(stat[:, 3, :], stat[:, 2, :], 1.0 / D, LN_EPS, ALU.mult, ALU.add))
                    rsqrt(stat[:, 0, :], stat[:, 3, :], stat[:, 1, :], stat[:, 2, :])
                    return V.tensor_tensor(dst, centred[:, :, :], wide(stat[:, 0, :]), ALU.mult)

                def row(v):
                    return vecs[:, v:v + 1, :].to_broadcast([128, CH, D])

                dve.wait_ge(loaded, (it + 1) * 48)
                norm(xm[:, :, 0:D], h_in[:, :, :]).then_inc(x_made, 1)
                dve.wait_ge(qkv_made, it + 1)
                q_sum, k_sum = pairs_at(0, D), chunks_at(4, 128)[:, :, 0:D]
                V.tensor_scalar(q_neg[:, :, :], q_sum, 0.0, None, ALU.min)
                V.tensor_scalar(k_neg[:, :, :], k_sum, 0.0, None, ALU.min).then_inc(neg_made, 1)
                dve.wait_ge(exp_made, it + 1)
                V.scalar_tensor_tensor(out=q_pos[:, :, :], in0=q_sum, scalar=0.0, in1=q_exp[:, :, :], op0=ALU.max, op1=ALU.add)
                V.scalar_tensor_tensor(out=k_pos[:, :, :], in0=k_sum, scalar=0.0, in1=k_exp[:, :, :], op0=ALU.max, op1=ALU.add).then_inc(qk_made, 1)
                dve.wait_ge(kv_made, it + 1)
                for half in range(2):
                    kv = psum[0:D, 512 * (4 + half):512 * (4 + half) + 65 * PAIRS].rearrange("p (i c) -> p i c", i=PAIRS)
                    masked = kv_head[:, :, :, :].rearrange("p (n t) a w -> p n t a w", t=2)[:, :, half, :, :]
                    mask = one_head[:, :].unsqueeze(1).to_broadcast([D, PAIRS, D])
                    V.tensor_tensor(masked[:, :, 0, :], kv[:, :, 0:D], mask, ALU.mult)
                    last = V.tensor_tensor(masked[:, :, 1, :], kv[:, :, D:D + 1].to_broadcast([D, PAIRS, D]), mask, ALU.mult)
                last.then_inc(kv_masked, 1)
                dve.wait_ge(msg_summed, it + 1)
                link(V.tensor_scalar(q_neg[:, :, :], pairs_at(4, D), ATT_EPS, None, ALU.add))
                link(V.reciprocal(z_inv[:, :, :], q_neg[:, :, :]))
                V.tensor_tensor(msgT[:, :, :], pairs_at(0, D), z_inv[:, :, :], ALU.mult).then_inc(msg_made, 1)
                dve.wait_ge(msg_mixed, it + 1)
                link(norm(squares[:, :, :], chunks_at(0, D)))
                link(V.tensor_tensor(centred[:, :, :], squares[:, :, :], row(0), ALU.mult))
                V.tensor_tensor(xm[:, :, D:2 * D], centred[:, :, :], row(1), ALU.add).then_inc(message_normed, 1)
                dve.wait_ge(msg2_made, it + 1)
                link(norm(squares[:, :, :], chunks_at(4, D)))
                link(V.tensor_tensor(centred[:, :, :], squares[:, :, :], row(2), ALU.mult))
                link(V.tensor_tensor(squares[:, :, :], centred[:, :, :], row(3), ALU.add))
                link(V.tensor_tensor(centred[:, :, :], squares[:, :, :], xm[:, :, 0:D], ALU.add))
                ins_ = V.tensor_tensor(h_mid[:, :, :], centred[:, :, :], h_in[:, :, :], ALU.add)
                link(ins_)
                dve.sem_inc(h_mid_made, 1)
                link(norm(squares[:, :, :], h_mid[:, :, :]))
                link(norm(xn[:, :, :], squares[:, :, :]))
                link(V.tensor_tensor(centred[:, :, :], xn[:, :, :], row(4), ALU.mult))
                V.tensor_tensor(xn[:, :, :], centred[:, :, :], row(5), ALU.add).then_inc(xn_made, 1)
                dve.wait_ge(logits_made, it + 1)
                link(V.tensor_tensor(gate[:, :, :], chunks_at(4, EXPERTS), br[:, :].unsqueeze(1).to_broadcast([128, CH, EXPERTS]), ALU.add))
                link(V.tensor_reduce(stat[:, 0, :], gate[:, :, :], AX.X, ALU.max))
                V.tensor_tensor(logit[:, :, :], gate[:, :, :], stat[:, 0, :].unsqueeze(2).to_broadcast([128, CH, EXPERTS]), ALU.subtract).then_inc(rexp_in, 1)
                for e in range(EXPERTS):
                    mine = gate[:, :, e:e + 1].to_broadcast([128, CH, EXPERTS])
                    V.tensor_tensor(cmp_gt[:, :, e, :], gate[:, :, :], mine, ALU.is_gt)
                    last = V.tensor_tensor(cmp_eq[:, :, e, :], gate[:, :, :], mine, ALU.is_equal)
                earlier = before[:, :, :].rearrange("p a b -> p (a b)").unsqueeze(1).to_broadcast([128, CH, 64])
                flat = lambda t: t[:, :, :, :].rearrange("p n a b -> p n (a b)")
                link(last)
                link(V.tensor_tensor(flat(cmp_eq), flat(cmp_eq), earlier, ALU.mult))
                link(V.tensor_tensor(flat(cmp_gt), flat(cmp_gt), flat(cmp_eq), ALU.add))
                link(V.tensor_reduce(rank[:, :, :].rearrange("p n e -> p (n e)"), cmp_gt[:, :, :, :].rearrange("p n a b -> p (n a) b"), AX.X, ALU.add))
                dve.wait_ge(rexp_made, it + 1)
                link(V.scalar_tensor_tensor(out=gate[:, :, :], in0=rank[:, :, :], scalar=TOP - 0.5, in1=rexp[:, :, :], op0=ALU.is_lt, op1=ALU.mult))
                link(V.tensor_reduce(stat[:, 1, :], gate[:, :, :], AX.X, ALU.add))
                link(V.reciprocal(stat[:, 2, :], stat[:, 1, :]))
                link(V.tensor_tensor(gate[:, :, :], gate[:, :, :], stat[:, 2, :].unsqueeze(2).to_broadcast([128, CH, EXPERTS]), ALU.mult))
                dve.sem_inc(gate_made, 1)
                STEPS = PAIRS * EXPERTS
                for s in range(STEPS):
                    dve.wait_ge(e_gelu, it * STEPS + s + 1)
                    if s >= 2:
                        dve.wait_ge(e_added, it * STEPS + s - 1)
                    V.tensor_tensor(eg[:, s % 2, :], eh[:, s % 2, :], psum[:, 512 * (2 + s % 2):512 * (2 + s % 2) + PW], ALU.mult).then_inc(e_gated, 1)
                dve.wait_ge(y_turned, it + 1)
                dve.wait_ge(stored, it * 64)
                V.tensor_tensor(h_out[:, :, :], h_mid[:, :, :], chunks_at(0, D), ALU.add).then_inc(out_made, 1)
                assert n[0] - 2 == LINKS, n[0] - 2


def kernel(**inputs):
    import concourse.bacc as _bacc
    from concourse.bass_utils import run_bass_kernel_spmd as _run

    tok = lambda name: np.asarray(inputs["L0_tok_" + name])
    attn = lambda name: np.asarray(inputs["L0_attn_" + name])
    ffn = lambda name: np.asarray(inputs["L0_ffn_" + name])
    sw = np.stack([tok(f"sw{l}") for l in range(LAYERS)]).reshape(LAYERS, C, C, M1, KYB, KYS)
    arrays = {
        **transforms(), **token_tables(),
        "x": np.asarray(inputs["x"]).transpose(0, 3, 1, 2).reshape(B // QB, QB * CIN, PIX),
        "sw": sw.transpose(0, 5, 4, 1, 3, 2).reshape(LAYERS * KYS, KYB * C, M1 * C),
        "cw": np.stack([tok(f"cw{l}").T for l in range(LAYERS)]),
        "cb": np.stack([tok(f"cb{l}") for l in range(LAYERS)], axis=1),
        "fc0_w": tok("fc0_w"), "fc0_b": tok("fc0_b").reshape(C, 1),
        "fc1_w": tok("fc1_w"), "fc1_b": tok("fc1_b").reshape(FC1, 1),
        "fc2_w": tok("fc2_w"), "fc2_b": tok("fc2_b").reshape(1, 1),
        "txt": np.asarray(inputs["txt"]).reshape(B // 2, 2, L_TXT, D),
        **{n: attn(n) for n in ("Wq", "Wk", "Wv", "Wm", "W1", "W2")},
        **{n: attn(n).reshape(1, D) for n in ("g1", "b1", "g2", "b2")},
        "gamma": ffn("gamma").reshape(1, D), "beta": ffn("beta").reshape(1, D),
        "Wr": ffn("Wr"), "br": ffn("br").reshape(1, EXPERTS),
        "ew1": ffn("W1").transpose(1, 0, 2), "eb1": ffn("b1").T,
        "ew2": ffn("W2").transpose(1, 0, 2), "eb2": ffn("b2"),
    }
    nc = _bacc.Bacc("TRN2", target_bir_lowering=False, num_devices=1)
    arrays = {f"in_{name}_dram": np.ascontiguousarray(a) for name, a in arrays.items()}
    ins = {name[3:-5]: nc.dram_tensor(name, a.shape, mybir.dt.from_np(a.dtype), kind="ExternalInput").ap() for name, a in arrays.items()}
    tokens = nc.dram_tensor("tokens_dram", (B, PIX), F32, kind="Internal").ap()
    out = nc.dram_tensor("out_0_dram", (B // 2, 2, S + L_TXT, D), F32, kind="ExternalOutput").ap()
    build_operator(nc, ins, tokens)
    build_tokens(nc, ins, tokens, out)
    r = _run(nc, [arrays], core_ids=[0])
    return r.results[0]["out_0_dram"].reshape(B, S + L_TXT, D)
```

```python
from contextlib import ExitStack

import numpy as np

import concourse.bass as bass
from concourse import mybir

F32 = mybir.dt.float32
F16 = mybir.dt.float16
I32 = mybir.dt.int32
ALU = mybir.AluOpType
ACT = mybir.ActivationFunctionType
AX = mybir.AxisListType

B, S, C = 64, 64, 32
CIN = 3
LAYERS = 4
M1 = M2 = 20
PIX = S * S
QB = 4
GQ = 4
GB = QB * GQ
GROUPS = B // GB
HB = GB // 2
KYB = 4
KYS = M2 // KYB
BLKS = PIX // 128
MK = KYS * M1
TJ = 2 * 2 * M2
W_SCALE = 64.0
FC1 = 64
L_TXT, D = 77, 64


def wait_apart(eng, semaphore, value, passed):
    eng.wait_ge(semaphore, value)
    eng.sem_inc(passed, 1)


def split16(a):
    hi = a.astype(np.float16)
    return hi.astype(np.float32), (a - hi.astype(np.float64)).astype(np.float16).astype(np.float32)


def transforms():
    root = np.sqrt(float(S))
    ky = np.arange(M2)
    kx = np.arange(M1)
    pos = np.arange(S)
    ang = 2 * np.pi * np.outer(pos, ky) / S
    cos, sin = np.cos(ang) / root, np.sin(ang) / root
    by_step = lambda m: m.reshape(-1, KYB, KYS).transpose(0, 2, 1).reshape(-1, M2)
    f1 = np.zeros((2, S, 2, 2, M2))
    for hp in range(2):
        f1[hp, :, hp, 0] = by_step(cos)
        f1[hp, :, hp, 1] = by_step(-sin)
    f2 = np.zeros((S // 2, QB, 2, 2, M1, 2, QB))
    for hp in range(2):
        for b in range(QB):
            f2[:, b, hp, 0, :, 0, b] = cos[hp::2]
            f2[:, b, hp, 0, :, 1, b] = -sin[hp::2]
            f2[:, b, hp, 1, :, 0, b] = sin[hp::2]
            f2[:, b, hp, 1, :, 1, b] = cos[hp::2]
    i1 = np.zeros((M1, 2, 2, S))
    i1[:, 0, 0], i1[:, 1, 0] = cos.T, -sin.T
    i1[:, 0, 1], i1[:, 1, 1] = sin.T, cos.T
    twice = np.where(ky == 0, 1.0, 2.0)[None]
    i2 = np.stack([(cos * twice).T, (-sin * twice).T])
    f1 = f1.reshape(128, TJ)
    f2 = f2.reshape(128, 4 * M1 * QB * 2)
    i1 = i1.reshape(2 * M1, 128)
    i2 = i2.reshape(2 * M2, S)
    stack = lambda m: np.concatenate([split16(m)[0], split16(m)[0], split16(m)[1]])
    both = lambda m: np.concatenate(split16(m), axis=1)
    return {
        "f1_mat": both(f1).astype(np.float32), "f2_mat": both(f2).astype(np.float32),
        "i1_mat": stack(i1).astype(np.float32), "i2_mat": stack(i2).astype(np.float32),
        "identity": np.eye(128, dtype=np.float32),
    }


def build_operator(nc, ins, split_weights, scratch, tokens):
    with ExitStack() as ctx:
        def sb(name, shape, dt):
            return ctx.enter_context(nc.sbuf_tensor(name, shape, dt))

        def sem(name):
            return ctx.enter_context(nc.semaphore(name))

        act_hl = sb("act_hl", [128, GQ, 2, PIX], F16)
        v_rows = sb("v_rows", [120, S, HB * C], F16)
        x_in = v_rows[0:QB * CIN, :, :].rearrange("p h n -> p (h n)").bitcast(F32).rearrange("p (u n) -> p u n", u=2)
        pixT = sb("pixT", [128, 2, PIX], F16)
        rows = sb("rows", [128, 2, 2, TJ * C], F16)
        spec = sb("spec", [128, 2, 2 * MK, HB], F16)
        mixw = sb("mixw", [128, 2, 2, M1, 128], F16)
        w_hl = sb("w_hl", [128, KYS, 2, M1, C], F16)
        mixed = sb("mixed", [128, 2, HB, 128], F16)
        mixedT = sb("mixedT", [128, HB, 128], F16)
        v_out = sb("v_out", [128, 2, 2, KYB, HB * C], F16)
        act32 = sb("act32", [128, 3, 1024], F32)
        f1_hl = sb("f1_hl", [128, 2, TJ], F16)
        f2_hl = sb("f2_hl", [128, 2, 4, 160], F16)
        i1_hl = sb("i1_hl", [120, 128], F16)
        i2_hl = sb("i2_hl", [120, S], F16)
        ident = sb("ident", [128, 128], F16)
        conv_all = sb("conv_all", [128, LAYERS, 2, 128], F16)
        conv_hl = sb("conv_hl", [128, 2, 2, 128], F16)
        bias_all = sb("bias_all", [128, LAYERS], F32)
        bias = sb("bias", [128, 2], F32)
        lift_w = sb("lift_w", [QB * CIN, 128], F32)
        lift_b = sb("lift_b", [128, 1], F32)
        fc1_hl = sb("fc1_hl", [128, 2, 2, 128], F16)
        fc1_b = sb("fc1_b", [128, 1], F32)
        fc2_w = sb("fc2_w", [128, 2, 32], F32)
        fc2_b = sb("fc2_b", [128, 1], F32)
        flat32 = act32[:, :, :].rearrange("p u n -> p (u n)")
        hidden = flat32[:, 0:2048].rearrange("p (u s n) -> p u s n", u=2, s=2)
        head_out = flat32[:, 2048:3072]
        start32 = act_hl[:, 0, :, :].rearrange("p s n -> p (s n)").bitcast(F32)
        conv32 = act_hl[:, 1, :, :].rearrange("p s n -> p (s n)").bitcast(F32)
        WL = KYS * M1 * C
        w_raw = [act_hl[:, 2 + n, :, :].rearrange("p s n -> p (s n)").bitcast(F32)[:, 0:WL].rearrange("p (k n) -> p k n", k=KYS) for n in range(2)]
        w_halves = [t.rearrange("p (k s n) -> p k s n", k=KYS, s=2) for t in
                    (pixT[:, :, :].rearrange("p s n -> p (s n)")[:, 0:2 * WL], rows[:, :, :, :].rearrange("p q s n -> p (q s n)")[:, 0:2 * WL])]

        psum = ctx.enter_context(nc.psum_tensor("psum", [128, 4096], F32))

        def bank(n, k=1):
            return psum[:, 512 * n:512 * (n + k)]

        consts_in = sem("consts_in")
        fill = sem("fill")
        zeroed = sem("zeroed")
        placed = sem("placed")
        consts_ready = sem("consts_ready")
        x_loaded = [sem("x_loaded0"), sem("x_loaded1")]
        layer_consts = sem("layer_consts")
        pixels_turned = sem("pixels_turned")
        turned_high = sem("turned_high")
        turned_low = sem("turned_low")
        rows_made = sem("rows_made")
        rows_high = sem("rows_high")
        rows_low = sem("rows_low")
        spec_made = sem("spec_made")
        spec_high = sem("spec_high")
        spec_low = sem("spec_low")
        w_raw_in = [sem("w_raw_in0"), sem("w_raw_in1")]
        w_high = sem("w_high")
        w_low = sem("w_low")
        w_stored = [sem("w_stored0"), sem("w_stored1")]
        w_loaded = sem("w_loaded")
        w_spread = sem("w_spread")
        w_spread_pool = sem("w_spread_pool")
        pool_passed = sem("pool_passed")
        sp_passed = sem("sp_passed")
        mix_made = sem("mix_made")
        mix_high = sem("mix_high")
        mix_low = sem("mix_low")
        mix_turned = sem("mix_turned")
        mixT_copied = sem("mixT_copied")
        v_made = sem("v_made")
        v_high = sem("v_high")
        v_low = sem("v_low")
        v_out_written = [sem("v_out_written0"), sem("v_out_written1")]
        v_moved = [sem("v_moved0"), sem("v_moved1")]
        sum_made = sem("sum_made")
        gelu_made = sem("gelu_made")
        act_high = sem("act_high")
        act_low = sem("act_low")
        fc1_made = sem("fc1_made")
        hidden_made = sem("hidden_made")
        hidden_read = sem("hidden_read")
        head_copied = sem("head_copied")
        head_stored = sem("head_stored")

        EARLY = 4
        CHUNKS = 4 * GQ
        PASSES = 2 * LAYERS
        HCH = CHUNKS // 2
        ALL_CH = CHUNKS + PASSES * HCH
        TURNS = 8 * 2 * PASSES
        MOVES = 16 * 3


        def spec_sum():
            return bank(5, 3)[:, 0:256 * KYS].rearrange("p (k n) -> p k n", k=KYS)[:, :, 0:8 * M1].rearrange("p k (y b) -> p k y b", b=QB)

        def spec_part(hl, q):
            return spec[:, hl, :, QB * q:QB * (q + 1)].rearrange("p (k y) b -> p k y b", k=KYS)

        def rows_bank(t):
            return bank((3, 2, 4)[t % 3])[:, 0:4 * TJ]

        def rows_sum(t):
            return rows_bank(t).rearrange("p (c j) -> p j c", c=4)

        def rows_part(q, hl, m):
            return rows[:, q, hl, :].rearrange("p (j c) -> p j c", c=C)[:, :, 4 * m:4 * m + 4]

        def mix_sum(k):
            return bank(2 + k % 2)[:, 0:2 * M1 * HB].rearrange("p (y b) -> p y b", b=HB)

        def mix_part(k, part):
            return mixed[:, k % 2, :, 2 * M1 * part:2 * M1 * (part + 1)].rearrange("p b y -> p y b")

        def v_sum(t):
            return bank(5 + t % 3)[:, :].rearrange("p (b k o) -> p b k o", b=4, k=KYB)

        def v_part(k, hl, n):
            return v_out[:, k % 2, hl, :, 128 * n:128 * (n + 1)].rearrange("p k (b o) -> p b k o", b=4)

        def act_chunk(hl, n):
            return act_hl[:, n // 4, hl, 1024 * (n % 4):1024 * (n % 4 + 1)]

        def chunk_banks(n):
            return bank(2 + 2 * (n % 3), 2)

        def turned_part(n):
            return pixT[:, n % 2, 1024 * (n // 2):1024 * (n // 2 + 1)]

        def first_chunk(g, l, half):
            return g * ALL_CH + (l * 2 + half) * HCH + CHUNKS

        def first_turn(g, l, j):
            return g * TURNS + l * 32 + 8 * j

        block = ctx.enter_context(nc.Block())

        def wait_written(eng, p, k):
            eng.wait_ge(v_out_written[k % 2], p * ((3, 2)[k % 2] * 32) + (k // 2 + 1) * 32)

        def wait_moved(eng, p, k):
            eng.wait_ge(v_moved[k % 2], p * ((3, 2)[k % 2] * MOVES) + (k // 2 + 1) * MOVES)

        @block.sync
        def _(sp):
            raw_in = lambda l: sp.dma_start(w_raw[l % 2], ins["sw"][l].rearrange("p (k n) -> p k n", k=KYS)).then_inc(w_raw_in[l % 2], 16)
            raw_in(0)
            sp.dma_start(start32[:, 0:160], ins["f1_mat"]).then_inc(consts_in, 16)
            sp.dma_start(start32[:, 160:1440], ins["f2_mat"]).then_inc(consts_in, 16)
            sp.dma_start(start32[0:120, 1440:1568], ins["i1_mat"]).then_inc(consts_in, 16)
            sp.dma_start(start32[0:120, 1568:1632], ins["i2_mat"]).then_inc(consts_in, 16)
            sp.dma_start(start32[:, 1632:1760], ins["identity"]).then_inc(consts_in, 16)
            raw_in(1)
            sp.wait_ge(zeroed, 1)
            for b in range(QB):
                p = slice(b * C, (b + 1) * C)
                for l in range(LAYERS):
                    sp.dma_start(conv32[p, l * 128 + b * C:l * 128 + (b + 1) * C], ins["cw"][l, :, :]).then_inc(placed, 16)
                sp.dma_start(bias_all[p, :], ins["cb"]).then_inc(placed, 16)
                sp.dma_start(conv32[p, 512 + b * FC1:512 + (b + 1) * FC1], ins["fc1_w"]).then_inc(placed, 16)
                sp.dma_start(lift_w[b * CIN:(b + 1) * CIN, p], ins["fc0_w"]).then_inc(placed, 16)
                sp.dma_start(lift_b[p, :], ins["fc0_b"]).then_inc(placed, 16)
            for b2 in range(2):
                p = slice(b2 * FC1, (b2 + 1) * FC1)
                sp.dma_start(fc1_b[p, :], ins["fc1_b"]).then_inc(placed, 16)
                for pair in range(2):
                    n = 2 * pair + b2
                    sp.dma_start(fc2_w[p, pair, n:n + 1], ins["fc2_w"]).then_inc(placed, 16)
            sp.dma_start(fc2_b[:, :], ins["fc2_b"].to_broadcast([128, 1])).then_inc(placed, 16)

            for l in range(LAYERS):
                sp.wait_ge(w_low, l + 1)
                sp.dma_start(split_weights[l].rearrange("p (k s n) -> p k s n", k=KYS, s=2), w_halves[l % 2]).then_inc(w_stored[l % 2], 16)
                if l + 2 < LAYERS:
                    raw_in(l + 2)
            for n in range(2):
                sp.wait_ge(w_stored[n], 16 * (LAYERS // 2))

            def passes(g, l):
                wait_apart(sp, w_spread, (g * PASSES + l * 2) * (3 * KYS), sp_passed)
                wait_apart(sp, w_spread_pool, (g * PASSES + l * 2) * KYS, sp_passed)
                src = split_weights[bass.ds(l, 1), :, :].rearrange("a p n -> (a p) n")
                sp.dma_start(w_hl[:, :, :, :, :].rearrange("p k s x o -> p (k s x o)"), src).then_inc(w_loaded, 16)
                for half in range(2):
                    p = g * PASSES + l * 2 + half
                    for step in range(KYS + 1):
                        k = step
                        if k < KYS:
                            sp.wait_ge(v_high, p * (2 * KYS) + 2 * k + 2)
                            sp.wait_ge(v_low, p * (2 * KYS) + 2 * k + 2)
                            for ri in range(2):
                                sp.dma_start(scratch[k, ri, :, :, :, :].rearrange("s y h n -> h (s y) n"),
                                             v_out[ri * S:(ri + 1) * S, k % 2, :, :, :].rearrange("p s y n -> p (s y) n"))\
                                    .then_inc(v_out_written[k % 2], 16)
                        k = step - 1
                        if k >= 0:
                            wait_written(sp, p, k)
                            for part in range(3):
                                sp.dma_start(v_rows[40 * part + k:40 * (part + 1):KYS, :, :].rearrange("p h n -> p (h n)"),
                                             scratch[k, :, part % 2, :, :, :].rearrange("r y h n -> r y (h n)"))\
                                    .then_inc(v_moved[k % 2], 16)

            with sp.Fori(0, GROUPS) as g:
                for q in range(GQ):
                    sp.wait_ge(sum_made, g * ALL_CH + 4 * max(q - 1, 0))
                    src = ins["x"][bass.ds(g * GQ + q, 1), :, :].rearrange("a p n -> (a p) n")
                    sp.dma_start(x_in[:, q % 2, :], src).then_inc(x_loaded[q % 2], 16)
                with sp.Fori(0, LAYERS) as l:
                    passes(g, l)
                for q in range(GQ):
                    sp.wait_ge(head_copied, g * GQ + q + 1)
                    for j in range(4):
                        dst = tokens[bass.ds(g * GB + q * QB, QB), :].rearrange("b (u j n) -> b u j n", u=2, j=4)[:, :, j, :]
                        src = head_out[32 * j:32 * j + QB, :].rearrange("p (u n) -> p u n", u=2)
                        sp.dma_start(dst, src).then_inc(head_stored, 16)
            sp.wait_ge(head_stored, GROUPS * GQ * 4 * 16)

        def spread_block(engine, k, b):
            r = slice(b * C, (b + 1) * C)
            dst = mixw[r, k % 2, :, :, b * C:(b + 1) * C].bitcast(F32).rearrange("p s x o -> p (s x) o")
            return engine.tensor_copy(dst, w_hl[r, k, :, :, :].bitcast(F32).rearrange("p s x o -> p (s x) o"))

        @block.gpsimd
        def _(pool):
            with pool.Fori(0, GROUPS * LAYERS) as layer:
                for half in range(2):
                    for k in range(KYS):
                        wait_apart(pool, w_loaded, layer * 16 + 16, pool_passed)
                        wait_apart(pool, mix_made, (2 * layer + half) * KYS + max(k - 1, 0), pool_passed)
                        spread_block(nc.gpsimd, k, KYB - 1).then_inc(w_spread_pool, 1)

        @block.scalar
        def _(act):
            for l in range(LAYERS):
                act.wait_ge(w_raw_in[l % 2], 16 * (l // 2 + 1))
                if l >= 2:
                    act.wait_ge(w_stored[l % 2], 16 * (l // 2))
                nc.scalar.activation(w_halves[l % 2][:, :, 0, :], w_raw[l % 2], ACT.Copy, scale=W_SCALE).then_inc(w_high, 1)
            act.wait_ge(consts_ready, 1)

            def activate(first, n, func, add):
                act.wait_ge(sum_made, first + n + 1)
                act.wait_ge(act_low, first + n - 2 if n >= 2 else first)
                nc.scalar.activation(act32[:, n % 3, :], chunk_banks(n), func, bias=add).then_inc(gelu_made, 1)

            def copy_turned(turn, n):
                act.wait_ge(pixels_turned, turn + n + 1)
                nc.scalar.activation(turned_part(n), bank(0).bitcast(F16), ACT.Copy).then_inc(turned_high, 1)

            def rows_of(p, t):
                act.wait_ge(rows_made, p * 16 + t + 1)
                nc.scalar.activation(rows_part(t // 8, 0, t % 8), rows_sum(t), ACT.Copy).then_inc(rows_high, 1)

            def one_pass(g, l, half, inverse_of, last=False):
                p = g * PASSES + l * 2 + half
                for q in range(2):
                    for t in range(8 * q, 8 * q + 8):
                        if t >= EARLY or inverse_of is None:
                            rows_of(p, t)
                    if q == 0:
                        for n in range(0, 8, 2):
                            copy_turned(first_turn(g, l, 2 * half + 1), n)
                    act.wait_ge(spec_made, p * 2 + q + 1)
                    nc.scalar.activation(spec_part(0, q), spec_sum(), ACT.Copy).then_inc(spec_high, 1)
                if inverse_of is not None:
                    inverse(g, *inverse_of)
                for step in range(KYS + 2):
                    k = step
                    if k < KYS:
                        act.wait_ge(mix_made, p * KYS + k + 1)
                        if k >= 2:
                            act.wait_ge(mix_turned, p * KYS + k - 1)
                        for part in (0, 2):
                            nc.scalar.activation(mix_part(k, part), mix_sum(k), ACT.Copy, scale=1.0 / W_SCALE).then_inc(mix_high, 1)
                    if step < 4 and not last:
                        copy_turned(first_turn(g, l, 2 * half + 2), 2 * step)
                    if step >= KYS and not last:
                        for t in (0, 1) if step == KYS else (2, 3):
                            rows_of(p + 1, t)
                    k = step - 1
                    if 0 <= k < KYS:
                        act.wait_ge(mix_turned, p * KYS + k + 1)
                        if k >= 1:
                            act.wait_ge(v_made, p * (2 * KYS) + 2 * k)
                        nc.scalar.activation(mixedT[:, :, :].rearrange("p b n -> p (b n)"), bank(4).bitcast(F16), ACT.Copy).then_inc(mixT_copied, 1)
                    k = step - 2
                    if k >= 0:
                        for n in range(2):
                            act.wait_ge(v_made, p * (2 * KYS) + 2 * k + n + 1)
                            if n == 0 and k >= 2:
                                wait_written(act, p, k - 2)
                            nc.scalar.activation(v_part(k, 0, n), v_sum(2 * k + n), ACT.Copy).then_inc(v_high, 1)

            def inverse(g, l, half):
                act.wait_ge(layer_consts, (g * PASSES + l * 2 + half) * 2 + 2)
                for n in range(HCH):
                    activate(first_chunk(g, l, half), n, ACT.Gelu, bias[:, half:half + 1])

            with act.Fori(0, GROUPS) as g:
                act.wait_ge(head_stored, g * (GQ * 4 * 16))
                for n in range(CHUNKS):
                    activate(g * ALL_CH, n, ACT.Identity, lift_b[:, :])
                act.wait_ge(w_stored[0], 16 * (LAYERS // 2))
                act.wait_ge(w_stored[1], 16 * (LAYERS // 2))
                for n in range(0, 8, 2):
                    copy_turned(first_turn(g, 0, 0), n)
                one_pass(g, 0, 0, None)
                one_pass(g, 0, 1, (0, 0))
                with act.Fori(1, LAYERS - 1) as l:
                    one_pass(g, l, 0, (l - 1, 1))
                    one_pass(g, l, 1, (l, 0))
                one_pass(g, LAYERS - 1, 0, (LAYERS - 2, 1))
                one_pass(g, LAYERS - 1, 1, (LAYERS - 1, 0), last=True)
                inverse(g, LAYERS - 1, 1)
                for n in range(8 * GQ):
                    act.wait_ge(fc1_made, g * (8 * GQ) + n + 1)
                    if n < 2:
                        act.wait_ge(act_low, g * ALL_CH + ALL_CH)
                    else:
                        act.wait_ge(hidden_read, g * (8 * GQ) + n - 1)
                    nc.scalar.activation(hidden[:, n % 2, :, :], chunk_banks(n).rearrange("p (s n) -> p s n", s=2), ACT.Gelu, bias=fc1_b[:, :])\
                        .then_inc(hidden_made, 1)

        @block.vector
        def _(dve):
            for t in (conv32[:, 0:768], lift_w[:, :], fc2_w[:, :, :], mixw[:, :, :, :, :], mixed[:, :, :, :]):
                nc.vector.memset(t, 0.0).then_inc(fill, 1)
            dve.wait_ge(fill, 5)
            dve.sem_inc(zeroed, 1)
            dve.wait_ge(consts_in, 5 * 16)
            nc.vector.tensor_copy(f1_hl[:, :, :], start32[:, 0:160].rearrange("p (s n) -> p s n", s=2)).then_inc(fill, 1)
            nc.vector.tensor_copy(f2_hl[:, :, :, :], start32[:, 160:1440].rearrange("p (s m n) -> p s m n", s=2, m=4)).then_inc(fill, 1)
            nc.vector.tensor_copy(i1_hl[:, :], start32[0:120, 1440:1568]).then_inc(fill, 1)
            nc.vector.tensor_copy(i2_hl[:, :], start32[0:120, 1568:1632]).then_inc(fill, 1)
            nc.vector.tensor_copy(ident[:, :], start32[:, 1632:1760]).then_inc(fill, 1)
            dve.wait_ge(placed, 16 * (8 * QB + 7))
            conv_raw = conv32[:, 0:512].rearrange("p (l n) -> p l n", l=LAYERS)
            fc1_raw = conv32[:, 512:768].rearrange("p (l n) -> p l n", l=2)
            nc.vector.tensor_copy(conv_all[:, :, 0, :], conv_raw).then_inc(fill, 1)
            nc.vector.tensor_copy(fc1_hl[:, :, 0, :], fc1_raw).then_inc(fill, 1)
            dve.wait_ge(fill, 12)
            nc.vector.tensor_tensor(conv_all[:, :, 1, :], conv_raw, conv_all[:, :, 0, :], ALU.subtract).then_inc(fill, 1)
            nc.vector.tensor_tensor(fc1_hl[:, :, 1, :], fc1_raw, fc1_hl[:, :, 0, :], ALU.subtract).then_inc(fill, 1)
            dve.wait_ge(fill, 14)
            dve.sem_inc(consts_ready, 1)
            for l in range(LAYERS):
                dve.wait_ge(w_high, l + 1)
                nc.vector.scalar_tensor_tensor(out=w_halves[l % 2][:, :, 1, :], in0=w_raw[l % 2], scalar=W_SCALE, in1=w_halves[l % 2][:, :, 0, :],
                                               op0=ALU.mult, op1=ALU.subtract).then_inc(w_low, 1)

            def split_chunk(first, n, at):
                dve.wait_ge(gelu_made, first + n + 1)
                nc.vector.tensor_copy(act_chunk(0, at), act32[:, n % 3, :]).then_inc(act_high, 1)
                dve.wait_ge(act_high, first + n + 1)
                nc.vector.tensor_tensor(act_chunk(1, at), act32[:, n % 3, :], act_chunk(0, at), ALU.subtract).then_inc(act_low, 1)

            def copy_turned(turn, n):
                dve.wait_ge(pixels_turned, turn + n + 1)
                nc.vector.tensor_copy(turned_part(n), bank(1).bitcast(F16)).then_inc(turned_low, 1)

            def spread(layer, p, k):
                dve.wait_ge(w_loaded, layer * 16 + 16)
                if k >= 2:
                    dve.wait_ge(mix_made, p * KYS + k - 1)
                for b in range(KYB - 1):
                    spread_block(nc.vector, k, b).then_inc(w_spread, 1)

            def layer_consts_of(l, half):
                nc.vector.tensor_copy(conv_hl[:, half, :, :], conv_all[:, bass.ds(l, 1), :, :].rearrange("p a s n -> p (a s) n")).then_inc(layer_consts, 1)
                nc.vector.tensor_copy(bias[:, half:half + 1], bias_all[:, bass.ds(l, 1)]).then_inc(layer_consts, 1)

            def inverse(g, l, half):
                for n in range(HCH):
                    split_chunk(first_chunk(g, l, half), n, HCH * half + n)

            def rows_of(p, t):
                dve.wait_ge(rows_high, p * 16 + t + 1)
                nc.vector.tensor_tensor(rows_part(t // 8, 1, t % 8), rows_sum(t), rows_part(t // 8, 0, t % 8), ALU.subtract).then_inc(rows_low, 1)

            def one_pass(g, l, half, inverse_of, last=False):
                p = g * PASSES + l * 2 + half
                for q in range(2):
                    for t in range(8 * q, 8 * q + 8):
                        if t >= EARLY or inverse_of is None:
                            rows_of(p, t)
                    if q == 0:
                        for n in range(1, 8, 2):
                            copy_turned(first_turn(g, l, 2 * half + 1), n)
                    dve.wait_ge(spec_high, p * 2 + q + 1)
                    nc.vector.tensor_tensor(spec_part(1, q), spec_sum(), spec_part(0, q), ALU.subtract).then_inc(spec_low, 1)
                layer = g * LAYERS + l
                spread(layer, p, 0)
                spread(layer, p, 1)
                if inverse_of is not None:
                    inverse(g, *inverse_of)
                layer_consts_of(l, half)
                for step in range(KYS + 2):
                    k = step
                    if k < KYS:
                        dve.wait_ge(mix_high, p * (2 * KYS) + 2 * k + 2)
                        nc.vector.scalar_tensor_tensor(out=mix_part(k, 1), in0=mix_sum(k), scalar=1.0 / W_SCALE, in1=mix_part(k, 0),
                                                       op0=ALU.mult, op1=ALU.subtract).then_inc(mix_low, 1)
                    if step < 4 and not last:
                        copy_turned(first_turn(g, l, 2 * half + 2), 2 * step + 1)
                    if step >= KYS and not last:
                        for t in (0, 1) if step == KYS else (2, 3):
                            rows_of(p + 1, t)
                    if k + 2 < KYS:
                        spread(layer, p, k + 2)
                    k = step - 2
                    if k >= 0:
                        for n in range(2):
                            dve.wait_ge(v_high, p * (2 * KYS) + 2 * k + n + 1)
                            nc.vector.tensor_tensor(v_part(k, 1, n), v_sum(2 * k + n), v_part(k, 0, n), ALU.subtract).then_inc(v_low, 1)

            with dve.Fori(0, GROUPS) as g:
                for n in range(CHUNKS):
                    split_chunk(g * ALL_CH, n, n)
                dve.wait_ge(w_stored[0], 16 * (LAYERS // 2))
                dve.wait_ge(w_stored[1], 16 * (LAYERS // 2))
                for n in range(1, 8, 2):
                    copy_turned(first_turn(g, 0, 0), n)
                one_pass(g, 0, 0, None)
                one_pass(g, 0, 1, (0, 0))
                with dve.Fori(1, LAYERS - 1) as l:
                    one_pass(g, l, 0, (l - 1, 1))
                    one_pass(g, l, 1, (l, 0))
                one_pass(g, LAYERS - 1, 0, (LAYERS - 2, 1))
                one_pass(g, LAYERS - 1, 1, (LAYERS - 1, 0), last=True)
                inverse(g, LAYERS - 1, 1)
                for q in range(GQ):
                    dve.wait_ge(hidden_read, g * (8 * GQ) + 8 * q + 8)
                    dve.wait_ge(head_stored, (g * GQ + q) * (4 * 16))
                    nc.vector.tensor_scalar(head_out, bank(0, 2), fc2_b[:, :], None, ALU.add).then_inc(head_copied, 1)

        @block.tensor
        def _(pe):
            pe.wait_ge(consts_ready, 1)

            def three(out, weights, data, start, stop):
                for n, (a, b) in enumerate(((0, 0), (0, 1), (1, 0))):
                    last = nc.tensor.matmul(out, weights[a], data[b], start=start and n == 0, stop=stop and n == 2)
                return last

            def turn(first, act_done, q, n):
                if n == 0:
                    pe.wait_ge(act_low, act_done)
                pe.wait_ge((turned_high, turned_low)[n % 2], first + n // 2)
                for j in range(8):
                    at = 128 * (8 * (n // 2) + j)
                    last = nc.tensor.transpose(bank(n % 2).bitcast(F16)[:, 128 * j:128 * (j + 1)], act_hl[:, q, n % 2, at:at + 128], ident[:, :])
                last.then_inc(pixels_turned, 1)

            def quad_ready(g, l, half, q):
                return first_chunk(g, l - 1, half) + 4 * (q + 1)

            def to_rows(g, l, quad, p, t):
                if t % 8 == 0:
                    done = g * (TURNS // 2) + l * 16 + 4 * quad + 4
                    pe.wait_ge(turned_high, done)
                    pe.wait_ge(turned_low, done)
                if t >= 3:
                    pe.wait_ge(rows_low, p * 16 + t - 2)
                for j in range(4):
                    c = 4 * (t % 8) + j
                    last = three(rows_bank(t)[:, TJ * j:TJ * (j + 1)], [pixT[:, s, c::C] for s in range(2)],
                                 [f1_hl[:, s, :] for s in range(2)], True, True)
                last.then_inc(rows_made, 1)

            def to_spectrum(p, q, k):
                if k == 0:
                    pe.wait_ge(rows_low, p * 16 + 8 * (q + 1))
                    if q == 0:
                        pe.wait_ge(v_low, p * (2 * KYS))
                    else:
                        pe.wait_ge(spec_low, p * 2 + q)
                for r in range(4):
                    at = C * (r * KYS + k) * KYB
                    last = three(bank(5, 3)[:, 256 * k:256 * k + 8 * M1], [rows[:, q, s, at:at + 128] for s in range(2)],
                                 [f2_hl[:, s, r, :] for s in range(2)], r == 0, r == 3)
                if k == KYS - 1:
                    last.then_inc(spec_made, 1)

            def inverse(g, l, half, after):
                p = g * PASSES + l * 2 + half
                first = first_chunk(g, l, half)
                pe.wait_ge(layer_consts, p * 2 + 2)
                for n in range(HCH):
                    if n == 1:
                        after()
                    if n >= 3:
                        pe.wait_ge(gelu_made, first + n - 2)
                    q = 2 * half + n // 4
                    banks = 2 + 2 * (n % 3)
                    for u in range(2):
                        at = 1024 * (n % 4) + 512 * u
                        three(bank(banks + u), [conv_hl[:, half, s, :] for s in range(2)], [act_hl[:, q, s, at:at + 512] for s in range(2)], True, False)
                    if n == 0:
                        wait_moved(pe, p, KYS - 1)
                        wait_moved(pe, p, KYS - 2)
                    for r in range(16):
                        last = nc.tensor.matmul(bank(banks + r // 8)[:, S * (r % 8):S * (r % 8 + 1)],
                                                v_rows[:, 16 * (n % 4) + r, 128 * (n // 4):128 * (n // 4 + 1)], i2_hl[:, :],
                                                start=False, stop=r % 8 == 7)
                    last.then_inc(sum_made, 1)

            def one_pass(g, l, half, inverse_of, last=False):
                p = g * PASSES + l * 2 + half
                for q in range(2):
                    for t in range(8 * q, 8 * q + 8):
                        if t >= EARLY or inverse_of is None:
                            to_rows(g, l, 2 * half + q, p, t)
                    for n in range(8):
                        if q == 0:
                            turn_at(g, l, 2 * half + 1, n)
                        if n >= 1 and n <= KYS:
                            to_spectrum(p, q, n - 1)
                spec_split = lambda: pe.wait_ge(spec_low, p * 2 + 2)
                if inverse_of is not None:
                    inverse(g, *inverse_of, spec_split)
                    pe.wait_ge(gelu_made, first_chunk(g, *inverse_of) + HCH - 1)
                else:
                    spec_split()
                for step in range(KYS + 2):
                    k = step
                    if k < KYS:
                        pe.wait_ge(w_spread, p * (3 * KYS) + 3 * k + 3)
                        pe.wait_ge(w_spread_pool, p * KYS + k + 1)
                        if k >= 2:
                            pe.wait_ge(mix_low, p * KYS + k - 1)
                        for x in range(M1):
                            y = 2 * (k * M1 + x)
                            mixing = three(bank(2 + k % 2)[:, 2 * HB * x:2 * HB * (x + 1)], [mixw[:, k % 2, s, x, :] for s in range(2)],
                                         [spec[:, s, y:y + 2, :] for s in range(2)], True, True)
                        mixing.then_inc(mix_made, 1)
                    if step < 4 and not last:
                        for n in (2 * step, 2 * step + 1):
                            turn_at(g, l, 2 * half + 2, n)
                    if step == KYS and not last:
                        to_rows(g, l, 2 * half + 2, p + 1, 0)
                    k = step - 1
                    if 0 <= k < KYS:
                        pe.wait_ge(mix_low, p * KYS + k + 1)
                        if k == 0 and inverse_of is not None:
                            pe.wait_ge(gelu_made, first_chunk(g, *inverse_of) + HCH)
                        if k >= 1:
                            pe.wait_ge(mixT_copied, p * KYS + k)
                        for j in range(HB):
                            turned = nc.tensor.transpose(bank(4).bitcast(F16)[:, 128 * j:128 * (j + 1)], mixed[:, k % 2, j, :], ident[:, :])
                        turned.then_inc(mix_turned, 1)
                    if step == KYS and not last:
                        to_rows(g, l, 2 * half + 2, p + 1, 1)
                    k = step - 2
                    if k >= 0:
                        pe.wait_ge(mixT_copied, p * KYS + k + 1)
                        for n in range(2):
                            t = 2 * k + n
                            if t >= 3:
                                pe.wait_ge(v_low, p * (2 * KYS) + t - 2)
                            nc.tensor.matmul(bank(5 + t % 3), i1_hl[:, :], mixedT[0:120, 4 * n:4 * n + 4, :], start=True, stop=True)\
                                .then_inc(v_made, 1)
                    if step == KYS + 1 and not last:
                        for t in (2, 3):
                            to_rows(g, l, 2 * half + 2, p + 1, t)

            def turn_at(g, l, j, n):
                ready = quad_ready(g, l, j // 2, j % 2) if j < 4 else quad_ready(g, l + 1, 0, 0)
                if j < 4 and isinstance(l, int) and l == 0:
                    ready = g * ALL_CH + 4 * (j + 1)
                turn(g * (TURNS // 2) + l * 16 + 4 * j, ready, j % 4, n)

            with pe.Fori(0, GROUPS) as g:
                for n in range(CHUNKS):
                    if n % 4 == 0:
                        pe.wait_ge(x_loaded[(n // 4) % 2], g * 32 + 16 * (n // 8 + 1))
                    if n == 0:
                        pe.wait_ge(hidden_made, g * (8 * GQ))
                    if n >= 3:
                        pe.wait_ge(gelu_made, g * ALL_CH + n - 2)
                    for u in range(2):
                        at = 1024 * (n % 4) + 512 * u
                        last = nc.tensor.matmul(bank(2 + 2 * (n % 3) + u), lift_w[:, :], x_in[:, (n // 4) % 2, at:at + 512], start=True, stop=True)
                    last.then_inc(sum_made, 1)
                pe.wait_ge(head_copied, g * GQ)
                for n in range(8):
                    turn_at(g, 0, 0, n)
                pe.wait_ge(gelu_made, g * ALL_CH + CHUNKS)
                one_pass(g, 0, 0, None)
                one_pass(g, 0, 1, (0, 0))
                with pe.Fori(1, LAYERS - 1) as l:
                    one_pass(g, l, 0, (l - 1, 1))
                    one_pass(g, l, 1, (l, 0))
                one_pass(g, LAYERS - 1, 0, (LAYERS - 2, 1))
                one_pass(g, LAYERS - 1, 1, (LAYERS - 1, 0), last=True)
                inverse(g, LAYERS - 1, 1, lambda: pe.wait_ge(v_low, (g + 1) * (PASSES * 2 * KYS)))

                pe.wait_ge(turned_high, (g + 1) * (TURNS // 2))
                pe.wait_ge(turned_low, (g + 1) * (TURNS // 2))
                pe.wait_ge(act_low, g * ALL_CH + ALL_CH)
                for n in range(8 * GQ + 1):
                    if n < 8 * GQ:
                        if n >= 3:
                            pe.wait_ge(hidden_made, g * (8 * GQ) + n - 2)
                        at = 512 * (n % 8)
                        for pair in range(2):
                            last = three(bank(2 + 2 * (n % 3) + pair), [fc1_hl[:, pair, s, :] for s in range(2)],
                                         [act_hl[:, n // 8, s, at:at + 512] for s in range(2)], True, True)
                        last.then_inc(fc1_made, 1)
                    if n >= 1:
                        m = n - 1
                        pe.wait_ge(hidden_made, g * (8 * GQ) + m + 1)
                        if m % 8 == 0:
                            pe.wait_ge(head_copied, g * GQ + m // 8)
                        row = 32 * (m % 4)
                        for pair in range(2):
                            last = nc.tensor.matmul(bank((m % 8) // 4)[row:row + 32, :], fc2_w[:, pair, :], hidden[:, m % 2, pair, :],
                                                    start=pair == 0, stop=pair == 1)
                        last.then_inc(hidden_read, 1)


SIDES = 2
PAIRS = 2 * SIDES
BATCHES = B // (2 * PAIRS)
CH = 3 * PAIRS
VJ = CH // 2
PW = 3 * 128
HEADS = 8
HD = D // HEADS
FF = 2 * D
EXPERTS, TOP = 8, 2
STEPS = PAIRS * EXPERTS
LAG = 3
LN_EPS, ATT_EPS = 1e-5, 1e-6
AT_X, AT_QK, AT_KV, AT_MSG, AT_NORM1, AT_NORM2, AT_NORM3, AT_NORM4 = 5, 7, 9, 12, 17, 25, 30, STEPS + LAG + 1


def token_tables():
    head = np.arange(2 * D) // HD
    one_head = (head[:, None] == head[None, :]).astype(np.float32)
    pick = np.zeros((128, EXPERTS, 128), np.float32)
    for e in range(EXPERTS):
        pick[[e, EXPERTS + e], e] = 1.0
    before = (np.arange(EXPERTS)[None, :] < np.arange(EXPERTS)[:, None]).astype(np.float32).reshape(1, -1)
    return {"one_head": one_head, "pick": pick.reshape(128, -1), "before": np.ascontiguousarray(np.broadcast_to(before, (128, 64)))}


def build_tokens(nc, ins, tokens, out):
    with ExitStack() as ctx:
        def sb(name, shape, dt=F32):
            return ctx.enter_context(nc.sbuf_tensor(name, shape, dt))

        def sem(name):
            return ctx.enter_context(nc.semaphore(name))

        h_in = sb("h_in", [128, CH, D])
        x = sb("x", [128, CH, D])
        msg = sb("msg", [128, CH, D])
        centred = sb("centred", [128, CH, D])
        squares = sb("squares", [128, CH, D])
        stat = sb("stat", [128, 4, CH])
        xT = sb("xT", [128, SIDES, PW])
        q_neg = sb("q_neg", [128, SIDES, PW])
        q_exp = sb("q_exp", [128, SIDES, PW])
        q_pos = sb("q_pos", [128, SIDES, PW])
        k_neg = sb("k_neg", [128, CH, D])
        k_exp = sb("k_exp", [128, CH, D])
        k_pos = sb("k_pos", [128, CH, D])
        v_one = sb("v_one", [128, CH, D + 1])
        kv_head = sb("kv_head", [128, 4, 2, 2, D])
        z_inv = sb("z_inv", [128, SIDES, PW])
        msgT = sb("msgT", [128, SIDES, PW])
        normT = sb("normT", [128, SIDES, PW])
        hid = sb("hid", [128, PAIRS, PW])
        logit = sb("logit", [128, CH, EXPERTS])
        cmp_gt = sb("cmp_gt", [128, CH, EXPERTS, EXPERTS])
        cmp_eq = sb("cmp_eq", [128, CH, EXPERTS, EXPERTS])
        rank = sb("rank", [128, CH, EXPERTS])
        rexp = sb("rexp", [128, CH, EXPERTS])
        gate = sb("gate", [128, CH, EXPERTS])
        gate_hl = sb("gate_hl", [128, CH, 128], F16)
        xn = sb("xn", [128, CH, D])
        xn_hl = sb("xn_hl", [128, CH, 2, D], F16)
        h_mid = sb("h_mid", [128, 2, CH, D])
        xnT = sb("xnT", [128, 2, PAIRS, PW], F16)
        gateT = sb("gateT", [128, 2, PAIRS, PW], F16)
        h_out = sb("h_out", [128, CH, D])
        eh = sb("eh", [128, 2, PW])
        eg = sb("eg", [128, 4, PW])
        eg_hl = sb("eg_hl", [128, 4, 2, PW], F16)
        ident = sb("t_ident", [128, 128])
        ident16 = sb("t_ident16", [128, 128], F16)
        one_head = sb("one_head", [128, 2, D])
        before = sb("before", [128, EXPERTS, EXPERTS])
        proj = sb("proj", [128, 4, 128])
        w1 = sb("w1", [128, 2, 2, FF])
        w2 = sb("w2", [FF, D])
        vecs = sb("vecs", [128, 6, D])
        br = sb("br", [128, EXPERTS])
        raw = sb("raw", [128, EXPERTS, FF])
        raw2 = sb("raw2", [FF, EXPERTS, D])
        raw_r = sb("raw_r", [128, EXPERTS])
        raw_b = sb("raw_b", [128, D])
        raw_p = sb("raw_p", [128, EXPERTS, 128])
        pick = sb("pick", [128, EXPERTS, 128], F16)
        wr = sb("wr", [128, 2, EXPERTS], F16)
        ew1 = sb("ew1", [128, 2, EXPERTS, FF], F16)
        eb1 = sb("eb1", [FF, EXPERTS])
        ew2 = sb("ew2", [FF, 2, EXPERTS, D], F16)
        eb2 = sb("eb2", [128, 2, D], F16)
        zeros = sb("zeros", [128, 3 * D], F16)
        psum = ctx.enter_context(nc.psum_tensor("t_psum", [128, 4096], F32))

        def sides_at(first):
            return psum[:, 512 * first:512 * (first + 2)].rearrange("p (v w) -> p v w", v=2)[:, :, 0:PW]

        def block_at(first, block):
            return sides_at(first)[:, block // 3, 128 * (block % 3):128 * (block % 3 + 1)]

        def blocks_at(first):
            return sides_at(first)

        def tiles(t):
            return t.rearrange("p (v c) w -> p v (c w)", v=2)

        def block_of(t, block):
            return t[:, 2 * block:2 * block + 2, :].rearrange("p c w -> p (c w)")

        def turned_block(t, block):
            return t[:, block // 3, 128 * (block % 3):128 * (block % 3 + 1)]

        HIDDEN, GATES, SUMS = 4, 6, 7
        def bank(n, cols=PW):
            return psum[:, 512 * n:512 * n + cols]

        w_in = sem("w_in")
        zeros_set = sem("zeros_set")
        weights_ready = sem("weights_ready")
        pe_passed = sem("pe_passed")
        dve_passed = sem("dve_passed")
        loaded = sem("loaded")
        dve_step = sem("dve_step")
        x_made = sem("x_made")
        x_turned = sem("x_turned")
        xT_copied = sem("xT_copied")
        qk_summed = sem("qk_summed")
        neg_made = sem("neg_made")
        exp_made = sem("exp_made")
        q_made = sem("q_made")
        k_made = sem("k_made")
        v_made_t = sem("v_made_t")
        v_copied = sem("v_copied")
        kv_made = sem("kv_made")
        kv_masked = sem("kv_masked")
        msg_summed = sem("msg_summed")
        msg_made = sem("msg_made")
        msg_mixed = sem("msg_mixed")
        message_normed = sem("message_normed")
        norm_turned = sem("norm_turned")
        normT_copied = sem("normT_copied")
        hid_summed = sem("hid_summed")
        hid_made = sem("hid_made")
        msg2_made = sem("msg2_made")
        h_mid_made = sem("h_mid_made")
        xn_made = sem("xn_made")
        xn_turned = sem("xn_turned")
        xnT_copied = sem("xnT_copied")
        logits_made = sem("logits_made")
        rexp_in = sem("rexp_in")
        rexp_made = sem("rexp_made")
        gate_made = sem("gate_made")
        gate_turned = sem("gate_turned")
        gateT_copied = sem("gateT_copied")
        e_summed = sem("e_summed")
        e_gates = sem("e_gates")
        e_gelu = sem("e_gelu")
        e_gated = sem("e_gated")
        e_high = sem("e_high")
        e_low = sem("e_low")
        e_added = sem("e_added")
        e_read = sem("e_read")
        stored = sem("stored")

        block = ctx.enter_context(nc.Block())
        weights = [(ident[:, :], "identity"), (one_head[:, :, :].rearrange("p u n -> p (u n)"), "one_head"),
                   (raw_p[:, :, :].rearrange("p e n -> p (e n)"), "pick"),
                   (before[:, :, :].rearrange("p a b -> p (a b)"), "before"), (w2[:, :], "W2"), (eb1[:, :], "eb1"), (raw2[:, :, :], "ew2")]
        for u in range(2):
            rows = slice(D * u, D * (u + 1))
            weights += [(proj[rows, n, D * u:D * (u + 1)], name) for n, name in enumerate(("Wq", "Wk", "Wv", "Wm"))]
            weights += [(raw[rows, :, :], "ew1"), (raw_r[rows, :], "Wr"), (raw_b[EXPERTS * u:EXPERTS * (u + 1), :], "eb2")]
            weights += [(w1[rows, part, u, :], "W1_" + part_name) for part, part_name in enumerate(("x", "m"))]
        vectors = ["g1", "b1", "g2", "b2", "gamma", "beta"]
        N_W = len(weights) + len(vectors) + 1
        tok_rows = tokens.rearrange("b (h w) -> (b h) w", h=S)
        chunks = lambda t: t.rearrange("p (v j u) w -> p v j u w", v=2, j=3)

        def batches(engine, run):
            run((0, 0), None)
            with engine.Fori(0, BATCHES // 2 - 1) as two:
                run((two * 2 + 1, 1), (two * 2, 0))
                run((two * 2 + 2, 0), (two * 2 + 1, 1))
            run((BATCHES - 1, 1), (BATCHES - 2, 0))
            run(None, (BATCHES - 1, 1))

        @block.sync
        def _(sp):
            sp.wait_ge(zeros_set, 1)
            for dst, name in weights:
                sp.dma_start(dst, ins[name]).then_inc(w_in, 16)
            for n, name in enumerate(vectors):
                sp.dma_start(vecs[:, n, :], ins[name].to_broadcast([128, D])).then_inc(w_in, 16)
            sp.dma_start(br[:, :], ins["br"].to_broadcast([128, EXPERTS])).then_inc(w_in, 16)

            def run(a, e):
                if a is not None:
                    it = a[0]
                    if not isinstance(it, int) or it > 0:
                        sp.wait_ge(h_mid_made, it)
                    src = tok_rows[bass.ds(it * (PAIRS * 128), PAIRS * 128), :].rearrange("(v u p) w -> p v u w", p=128, u=2)
                    txt = ins["txt"][bass.ds(it * PAIRS, PAIRS), :, :, :].rearrange("(v u) t p w -> p v u t w", u=2)
                    for u in range(2):
                        sp.dma_start(chunks(h_in[:, :, :])[:, :, 1, u, :], src[:, :, u, :]).then_inc(loaded, 16)
                        for t in range(2):
                            sp.dma_start(chunks(h_in[0:L_TXT, :, :])[:, :, 2 * t, u, :], txt[:, :, u, t, :]).then_inc(loaded, 16)
                if e is not None:
                    it = e[0]
                    sp.wait_ge(e_read, (it + 1) * PAIRS)
                    dst = out[bass.ds(it * PAIRS, PAIRS), :, :, :].rearrange("(v u) t p w -> p v u t w", u=2)
                    for u in range(2):
                        for t in range(2):
                            sp.dma_start(dst[0:S, :, u, t, :], chunks(h_out[S * t:S * (t + 1), :, :])[:, :, 1, u, :]).then_inc(stored, 16)
                            sp.dma_start(dst[S:S + L_TXT, :, u, t, :], chunks(h_out[0:L_TXT, :, :])[:, :, 2 * t, u, :]).then_inc(stored, 16)

            batches(sp, run)
            sp.wait_ge(stored, BATCHES * 8 * 16)

        @block.tensor
        def _(pe):
            mm = nc.tensor.matmul
            pe.wait_ge(weights_ready, 1)

            def run(a, e):
                done = [0]

                def experts_to(target):
                    while e is not None and done[0] < target:
                        step(e[0], e[1], done[0])
                        done[0] += 1

                def step(it, parity, s):
                    if s < STEPS:
                        n, x = s // EXPERTS, s % EXPERTS
                        if s == 0:
                            wait_apart(pe, gateT_copied, it + 1, pe_passed)
                        if s >= 2:
                            pe.wait_ge(e_gelu, it * STEPS + s - 1)
                        for part in range(2):
                            last = mm(bank(HIDDEN + s % 2), ew1[:, part, x, :], xnT[:, parity, n, :], start=part == 0, stop=part == 1)
                        last.then_inc(e_summed, 1)
                        if s >= 1:
                            pe.wait_ge(e_gated, it * STEPS + s)
                        mm(bank(GATES), pick[:, x, :], gateT[:, parity, n, :], start=True, stop=True).then_inc(e_gates, 1)
                    m = s - LAG
                    if 0 <= m < STEPS:
                        n, x = m // EXPERTS, m % EXPERTS
                        if m % EXPERTS == 0 and m > 0:
                            pe.wait_ge(e_read, it * PAIRS + n)
                        pe.wait_ge(e_low, it * STEPS + m + 1)
                        pe.wait_ge(e_high, it * STEPS + m + 1)
                        if x == 0:
                            mm(bank(SUMS, 3 * D), gateT[:, parity, n, 0:128], zeros[:, :], start=True, stop=False)
                        for j in range(3):
                            at = slice(128 * j, 128 * (j + 1))
                            dst = bank(SUMS)[:, D * j:D * (j + 1)]
                            if x == 0:
                                for part in range(2):
                                    mm(dst, gateT[:, parity, n, at], eb2[:, part, :], start=False, stop=False)
                            mm(dst, eg_hl[:, m % 4, 0, at], ew2[:, 0, x, :], start=False, stop=False)
                            mm(dst, eg_hl[:, m % 4, 0, at], ew2[:, 1, x, :], start=False, stop=False)
                            last = mm(dst, eg_hl[:, m % 4, 1, at], ew2[:, 0, x, :], start=False, stop=x == EXPERTS - 1 and j == 2)
                        last.then_inc(e_added, 1)

                if a is None:
                    experts_to(STEPS + LAG + 1)
                    return
                it, parity = a
                experts_to(AT_X)
                wait_apart(pe, x_made, it + 1, pe_passed)
                for n in range(VJ):
                    last = nc.tensor.transpose(block_at(0, n), block_of(x, n), ident[:, :])
                last.then_inc(x_turned, 1)
                wait_apart(pe, xT_copied, it + 1, pe_passed)
                for v in range(2):
                    mm(sides_at(0)[:, v, :], proj[:, 0, :], xT[:, v, :], start=True, stop=True)
                for n in range(VJ):
                    last = mm(block_at(2, n), turned_block(xT, n), proj[:, 1, :], start=True, stop=True)
                last.then_inc(qk_summed, 1)
                experts_to(AT_QK)
                wait_apart(pe, q_made, it + 1, pe_passed)
                for n in range(VJ):
                    last = mm(block_at(0, n), turned_block(xT, n), proj[:, 2, :], start=True, stop=True)
                last.then_inc(v_made_t, 1)
                wait_apart(pe, k_made, it + 1, pe_passed)
                wait_apart(pe, v_copied, it + 1, pe_passed)
                for v in range(2):
                    for t in range(2):
                        dst = bank(2 + t, 512)[:, 130 * v:130 * (v + 1)]
                        for r, j in ((slice(S * t, S * (t + 1)), 1), (slice(0, L_TXT), 2 * t)):
                            c = 2 * (3 * v + j)
                            last = mm(dst, k_pos[r, c:c + 2, :].rearrange("p u w -> p (u w)"), v_one[r, c:c + 2, :].rearrange("p u w -> p (u w)"),
                                      start=j == 1, stop=j != 1)
                last.then_inc(kv_made, 1)
                experts_to(AT_KV)
                wait_apart(pe, kv_masked, it + 1, pe_passed)
                for part in (1, 0):
                    for v in range(2):
                        for t in range(2):
                            c = slice(192 * t, 192 * (t + 1))
                            last = mm(sides_at(2 * part)[:, v, c], kv_head[:, 2 * t + v, part, :, :].rearrange("p u w -> p (u w)"), q_pos[:, v, c],
                                      start=True, stop=True)
                last.then_inc(msg_summed, 1)
                experts_to(AT_MSG)
                wait_apart(pe, msg_made, it + 1, pe_passed)
                for n in range(VJ):
                    last = mm(block_at(0, n), turned_block(msgT, n), proj[:, 3, :], start=True, stop=True)
                last.then_inc(msg_mixed, 1)
                experts_to(AT_NORM1)
                wait_apart(pe, message_normed, it + 1, pe_passed)
                for n in range(VJ):
                    last = nc.tensor.transpose(block_at(2, n), block_of(msg, n), ident[:, :])
                last.then_inc(norm_turned, 1)
                wait_apart(pe, normT_copied, it + 1, pe_passed)
                for n in range(PAIRS):
                    v, u = n // 2, n % 2
                    mm(bank(n), w1[:, 0, u, :], xT[:, v, :], start=True, stop=False)
                    last = mm(bank(n), w1[:, 1, u, :], normT[:, v, :], start=False, stop=True)
                last.then_inc(hid_summed, 1)
                wait_apart(pe, hid_made, it + 1, pe_passed)
                for v in range(2):
                    for j in range(3):
                        for u in range(2):
                            last = mm(sides_at(0)[:, v, 128 * j + D * u:128 * j + D * (u + 1)], hid[:, 2 * v + u, 128 * j:128 * (j + 1)], w2[:, :],
                                      start=True, stop=True)
                last.then_inc(msg2_made, 1)
                experts_to(AT_NORM4)
                wait_apart(pe, xn_made, it + 1, pe_passed)
                for n in range(PAIRS):
                    for j in range(3):
                        at = 128 * (3 * n + j)
                        last = nc.tensor.transpose(bank(0, 1024).bitcast(F16)[:, at:at + 128],
                                                   xn_hl[:, 2 * (3 * (n // 2) + j) + n % 2, :, :].rearrange("p s w -> p (s w)"), ident16[:, :])
                last.then_inc(xn_turned, 1)
                wait_apart(pe, xnT_copied, it + 1, pe_passed)
                for n in range(PAIRS):
                    for j in range(3):
                        c = 2 * (3 * (n // 2) + j) + n % 2
                        for part in range(2):
                            last = mm(bank(2)[:, EXPERTS * c:EXPERTS * (c + 1)], xnT[:, parity, n, 128 * j:128 * (j + 1)], wr[:, part, :],
                                      start=part == 0, stop=part == 1)
                last.then_inc(logits_made, 1)
                wait_apart(pe, gate_made, it + 1, pe_passed)
                for n in range(PAIRS):
                    for j in range(3):
                        at = 128 * (3 * n + j)
                        last = nc.tensor.transpose(bank(0, 1024).bitcast(F16)[:, at:at + 128], gate_hl[:, 2 * (3 * (n // 2) + j) + n % 2, :], ident16[:, :])
                last.then_inc(gate_turned, 1)

            batches(pe, run)

        @block.gpsimd
        def _(pool):
            with pool.Fori(0, BATCHES * STEPS // 4) as four:
                for s in range(4):
                    pool.wait_ge(e_high, four * 4 + s + 1)
                    nc.gpsimd.tensor_tensor(eg_hl[:, s, 1, :], eg[:, s, :], eg_hl[:, s, 0, :], ALU.subtract).then_inc(e_low, 1)

        @block.scalar
        def _(act):
            A = nc.scalar.activation
            act.wait_ge(weights_ready, 1)

            def run(a, e):
                done = [0]

                def experts_to(target):
                    while e is not None and done[0] < target:
                        step(e[0], e[1], done[0])
                        done[0] += 1

                def step(it, parity, s):
                    if s < STEPS:
                        act.wait_ge(e_summed, it * STEPS + s + 1)
                        if s >= 2:
                            act.wait_ge(e_gated, it * STEPS + s - 1)
                        A(eh[:, s % 2, :], bank(HIDDEN + s % 2), ACT.Gelu, bias=eb1[:, s % EXPERTS:s % EXPERTS + 1]).then_inc(e_gelu, 1)
                    m = s - 1
                    if 0 <= m < STEPS:
                        act.wait_ge(e_gated, it * STEPS + m + 1)
                        if m >= 4:
                            act.wait_ge(e_added, it * STEPS + m - 3)
                        A(eg_hl[:, m % 4, 0, :], eg[:, m % 4, :], ACT.Copy).then_inc(e_high, 1)

                if a is None:
                    experts_to(STEPS + LAG + 1)
                    return
                it, parity = a
                experts_to(AT_X)
                act.wait_ge(x_turned, it + 1)
                A(xT[:, :, :], sides_at(0), ACT.Copy).then_inc(xT_copied, 1)
                act.wait_ge(neg_made, it + 1)
                A(q_exp[:, :, :], q_neg[:, :, :], ACT.Exp)
                A(k_exp[:, :, :], k_neg[:, :, :], ACT.Exp).then_inc(exp_made, 1)
                experts_to(AT_QK)
                act.wait_ge(v_made_t, it + 1)
                A(v_one[:, :, 0:D].rearrange("p (v c) w -> p v c w", v=2), sides_at(0).rearrange("p v (c w) -> p v c w", w=D), ACT.Copy).then_inc(v_copied, 1)
                experts_to(AT_NORM1)
                act.wait_ge(norm_turned, it + 1)
                A(normT[:, :, :], sides_at(2), ACT.Copy).then_inc(normT_copied, 1)
                act.wait_ge(hid_summed, it + 1)
                A(hid[:, :, :], psum[:, 0:2048].rearrange("p (n w) -> p n w", n=PAIRS)[:, :, 0:PW], ACT.Relu).then_inc(hid_made, 1)
                experts_to(AT_NORM4)
                act.wait_ge(xn_turned, it + 1)
                A(xnT[:, parity, :, :].rearrange("p n w -> p (n w)"), bank(0, 1024).bitcast(F16)[:, 0:PAIRS * PW], ACT.Copy).then_inc(xnT_copied, 1)
                act.wait_ge(rexp_in, it + 1)
                A(rexp[:, :, :], logit[:, :, :], ACT.Exp).then_inc(rexp_made, 1)
                act.wait_ge(gate_turned, it + 1)
                A(gateT[:, parity, :, :].rearrange("p n w -> p (n w)"), bank(0, 1024).bitcast(F16)[:, 0:PAIRS * PW], ACT.Copy).then_inc(gateT_copied, 1)

            batches(act, run)

        @block.vector
        def _(dve):
            V = nc.vector
            start = (h_in[:, :, :], proj[:, :, :], w1[:, :, :, :], raw_b[:, :], gate_hl[:, :, :], ew1[D:128, 1, :, :], wr[D:128, 1, :], eb2[:, :, :], zeros[:, :])
            for t in start:
                V.memset(t, 0.0).then_inc(dve_step, 1)
            V.memset(v_one[:, :, :], 1.0).then_inc(dve_step, 1)
            dve.wait_ge(dve_step, len(start) + 1)
            dve.sem_inc(zeros_set, 1)
            dve.wait_ge(w_in, 16 * N_W)
            splits = ((ew1[:, 0, :, :], ew1[0:D, 0, :, :], ew1[0:D, 1, :, :], raw[:, :, :], raw[0:D, :, :]),
                      (wr[:, 0, :], wr[0:D, 0, :], wr[0:D, 1, :], raw_r[:, :], raw_r[0:D, :]),
                      (ew2[:, 0, :, :], ew2[:, 0, :, :], ew2[:, 1, :, :], raw2[:, :, :], raw2[:, :, :]),
                      (eb2[:, 0, :], eb2[0:EXPERTS, 0, :], eb2[0:EXPERTS, 1, :], raw_b[:, :], raw_b[0:EXPERTS, :]))
            for high, _, _, whole, _ in splits:
                V.tensor_copy(high, whole).then_inc(dve_step, 1)
            V.tensor_copy(ident16[:, :], ident[:, :]).then_inc(dve_step, 1)
            V.tensor_copy(pick[:, :, :], raw_p[:, :, :]).then_inc(dve_step, 1)
            STARTED = len(start) + 1 + len(splits) + 2
            dve.wait_ge(dve_step, STARTED)
            for _, high, low, _, whole in splits:
                V.tensor_tensor(low, whole, high, ALU.subtract).then_inc(dve_step, 1)
            STARTED += len(splits)
            dve.wait_ge(dve_step, STARTED)
            dve.sem_inc(weights_ready, 1)
            LINKS = 126

            def run(a, e):
                done = [0]

                def experts_to(target):
                    while e is not None and done[0] < target:
                        step(e[0], e[1], done[0])
                        done[0] += 1

                def step(it, parity, s):
                    if s >= LAG + EXPERTS and (s - LAG) % EXPERTS == 0:
                        n = (s - LAG) // EXPERTS - 1
                        dve.wait_ge(e_added, it * STEPS + EXPERTS * (n + 1))
                        if n == 0 and (not isinstance(it, int) or it > 0):
                            wait_apart(dve, stored, it * (8 * 16), dve_passed)
                        V.tensor_tensor(chunks(h_out[:, :, :])[:, n // 2, :, n % 2, :], chunks(h_mid[:, parity, :, :])[:, n // 2, :, n % 2, :],
                                        bank(SUMS, 3 * D).rearrange("p (j w) -> p j w", j=3), ALU.add).then_inc(e_read, 1)
                    if s < STEPS:
                        dve.wait_ge(e_gelu, it * STEPS + s + 1)
                        dve.wait_ge(e_gates, it * STEPS + s + 1)
                        if s >= 4:
                            dve.wait_ge(e_low, it * STEPS + s - 3)
                        V.tensor_tensor(eg[:, s % 4, :], eh[:, s % 2, :], bank(GATES), ALU.mult).then_inc(e_gated, 1)

                if a is None:
                    experts_to(STEPS + LAG + 1)
                    return
                it, parity = a
                n = [STARTED]

                def link(instruction):
                    n[0] += 1
                    instruction.then_inc(dve_step, 1)
                    dve.wait_ge(dve_step, it * LINKS + n[0])

                def wide(t):
                    return t.unsqueeze(2).to_broadcast([128, CH, D])

                def rsqrt(y, v, t, u):
                    link(V.tensor_scalar(t.bitcast(I32), v.bitcast(I32), 1, None, ALU.logical_shift_right))
                    link(V.tensor_scalar(y.bitcast(I32), t.bitcast(I32), -1.0, float(0x5F3759DF), ALU.mult, ALU.add))
                    for _ in range(3):
                        link(V.tensor_tensor(t, v, y, ALU.mult))
                        link(V.tensor_tensor(u, t, y, ALU.mult))
                        link(V.tensor_scalar(t, u, -0.5, 1.5, ALU.mult, ALU.add))
                        link(V.tensor_tensor(y, y, t, ALU.mult))

                def norm(dst, src, steps, by_side=False):
                    link(V.tensor_reduce(stat[:, 0, :] if not by_side else stat[:, 0, :].rearrange("p (v c) -> p v c", v=2), src, AX.X, ALU.add))
                    experts_to(steps + 1)
                    link(V.tensor_scalar(stat[:, 1, :], stat[:, 0, :], 1.0 / D, None, ALU.mult))
                    if by_side:
                        for v in range(2):
                            c = slice(VJ * v, VJ * (v + 1))
                            last = V.tensor_tensor(centred[:, c, :], src[:, v, :, :], stat[:, 1, c].unsqueeze(2).to_broadcast([128, VJ, D]), ALU.subtract)
                        link(last)
                    else:
                        link(V.tensor_tensor(centred[:, :, :], src, wide(stat[:, 1, :]), ALU.subtract))
                    experts_to(steps + 2)
                    link(V.tensor_tensor(squares[:, :, :], centred[:, :, :], centred[:, :, :], ALU.mult))
                    experts_to(steps + 3)
                    link(V.tensor_reduce(stat[:, 2, :], squares[:, :, :], AX.X, ALU.add))
                    experts_to(steps + 4)
                    link(V.tensor_scalar(stat[:, 3, :], stat[:, 2, :], 1.0 / D, LN_EPS, ALU.mult, ALU.add))
                    rsqrt(stat[:, 0, :], stat[:, 3, :], stat[:, 1, :], stat[:, 2, :])
                    experts_to(steps + 5)
                    return V.tensor_tensor(dst, centred[:, :, :], wide(stat[:, 0, :]), ALU.mult)

                def row(v):
                    return vecs[:, v:v + 1, :].to_broadcast([128, CH, D])

                by_chunk = lambda t: t.rearrange("p v (c w) -> p v c w", w=D)

                dve.wait_ge(loaded, (it + 1) * (6 * 16))
                norm(x[:, :, :], h_in[:, :, :], 0).then_inc(x_made, 1)
                assert AT_X == 5
                dve.wait_ge(qk_summed, it + 1)
                q_sum, k_sum = sides_at(0), sides_at(2)
                V.tensor_scalar(q_neg[:, :, :], q_sum, 0.0, None, ALU.min)
                V.tensor_scalar(tiles(k_neg[:, :, :]), k_sum, 0.0, None, ALU.min).then_inc(neg_made, 1)
                experts_to(AT_QK - 1)
                dve.wait_ge(exp_made, it + 1)
                V.scalar_tensor_tensor(out=q_pos[:, :, :], in0=q_sum, scalar=0.0, in1=q_exp[:, :, :], op0=ALU.max, op1=ALU.add).then_inc(q_made, 1)
                V.scalar_tensor_tensor(out=tiles(k_pos[:, :, :]), in0=k_sum, scalar=0.0, in1=tiles(k_exp[:, :, :]), op0=ALU.max, op1=ALU.add)\
                    .then_inc(k_made, 1)
                experts_to(AT_QK)
                dve.wait_ge(kv_made, it + 1)
                for t in range(2):
                    kv = bank(2 + t, 260).rearrange("p (v u c) -> p v u c", v=2, u=2)
                    for v in range(2):
                        V.tensor_tensor(kv_head[:, 2 * t + v, 0, :, :], kv[:, v, :, 0:D], one_head[:, :, :], ALU.mult)
                        last = V.tensor_tensor(kv_head[:, 2 * t + v, 1, :, :], kv[:, v, :, D:D + 1].to_broadcast([128, 2, D]), one_head[:, :, :], ALU.mult)
                    experts_to(AT_QK + t + 1)
                last.then_inc(kv_masked, 1)
                dve.wait_ge(msg_summed, it + 1)
                link(V.tensor_scalar(q_neg[:, :, :], sides_at(2), ATT_EPS, None, ALU.add))
                experts_to(AT_KV + 1)
                for v in range(2):
                    link(V.reciprocal(z_inv[:, v, :], q_neg[:, v, :]))
                    experts_to(AT_KV + 2 + v)
                V.tensor_tensor(msgT[:, :, :], sides_at(0), z_inv[:, :, :], ALU.mult).then_inc(msg_made, 1)
                dve.wait_ge(msg_mixed, it + 1)
                link(norm(squares[:, :, :], by_chunk(sides_at(0)), AT_MSG, by_side=True))
                link(V.tensor_tensor(centred[:, :, :], squares[:, :, :], row(0), ALU.mult))
                V.tensor_tensor(msg[:, :, :], centred[:, :, :], row(1), ALU.add).then_inc(message_normed, 1)
                dve.wait_ge(msg2_made, it + 1)
                link(norm(squares[:, :, :], by_chunk(sides_at(0)), AT_NORM1, by_side=True))
                experts_to(AT_NORM1 + 6)
                link(V.tensor_tensor(centred[:, :, :], squares[:, :, :], row(2), ALU.mult))
                link(V.tensor_tensor(squares[:, :, :], centred[:, :, :], row(3), ALU.add))
                experts_to(AT_NORM1 + 7)
                link(V.tensor_tensor(centred[:, :, :], squares[:, :, :], x[:, :, :], ALU.add))
                experts_to(AT_NORM2)
                link(V.tensor_tensor(h_mid[:, parity, :, :], centred[:, :, :], h_in[:, :, :], ALU.add))
                dve.sem_inc(h_mid_made, 1)
                link(norm(squares[:, :, :], h_mid[:, parity, :, :], AT_NORM2))
                link(norm(xn[:, :, :], squares[:, :, :], AT_NORM3))
                link(V.tensor_tensor(centred[:, :, :], xn[:, :, :], row(4), ALU.mult))
                link(V.tensor_tensor(xn[:, :, :], centred[:, :, :], row(5), ALU.add))
                link(V.tensor_copy(xn_hl[:, :, 0, :], xn[:, :, :]))
                V.tensor_tensor(xn_hl[:, :, 1, :], xn[:, :, :], xn_hl[:, :, 0, :], ALU.subtract).then_inc(xn_made, 1)
                experts_to(AT_NORM4)
                dve.wait_ge(logits_made, it + 1)
                link(V.tensor_tensor(gate[:, :, :], bank(2, CH * EXPERTS).rearrange("p (c e) -> p c e", e=EXPERTS),
                                     br[:, :].unsqueeze(1).to_broadcast([128, CH, EXPERTS]), ALU.add))
                link(V.tensor_reduce(stat[:, 0, :], gate[:, :, :], AX.X, ALU.max))
                V.tensor_tensor(logit[:, :, :], gate[:, :, :], stat[:, 0, :].unsqueeze(2).to_broadcast([128, CH, EXPERTS]), ALU.subtract).then_inc(rexp_in, 1)
                for x_ in range(EXPERTS):
                    mine = gate[:, :, x_:x_ + 1].to_broadcast([128, CH, EXPERTS])
                    V.tensor_tensor(cmp_gt[:, :, x_, :], gate[:, :, :], mine, ALU.is_gt)
                    last = V.tensor_tensor(cmp_eq[:, :, x_, :], gate[:, :, :], mine, ALU.is_equal)
                earlier = before[:, :, :].rearrange("p a b -> p (a b)").unsqueeze(1).to_broadcast([128, CH, 64])
                flat = lambda t: t[:, :, :, :].rearrange("p n a b -> p n (a b)")
                link(last)
                link(V.tensor_tensor(flat(cmp_eq), flat(cmp_eq), earlier, ALU.mult))
                link(V.tensor_tensor(flat(cmp_gt), flat(cmp_gt), flat(cmp_eq), ALU.add))
                link(V.tensor_reduce(rank[:, :, :].rearrange("p n e -> p (n e)"), cmp_gt[:, :, :, :].rearrange("p n a b -> p (n a) b"), AX.X, ALU.add))
                dve.wait_ge(rexp_made, it + 1)
                link(V.scalar_tensor_tensor(out=gate[:, :, :], in0=rank[:, :, :], scalar=TOP - 0.5, in1=rexp[:, :, :], op0=ALU.is_lt, op1=ALU.mult))
                link(V.tensor_reduce(stat[:, 1, :], gate[:, :, :], AX.X, ALU.add))
                link(V.reciprocal(stat[:, 2, :], stat[:, 1, :]))
                link(V.tensor_tensor(gate[:, :, :], gate[:, :, :], stat[:, 2, :].unsqueeze(2).to_broadcast([128, CH, EXPERTS]), ALU.mult))
                link(V.tensor_copy(gate_hl[:, :, 0:EXPERTS], gate[:, :, :]))
                V.tensor_tensor(gate_hl[:, :, EXPERTS:2 * EXPERTS], gate[:, :, :], gate_hl[:, :, 0:EXPERTS], ALU.subtract).then_inc(gate_made, 1)
                assert n[0] - STARTED == LINKS, n[0] - STARTED

            batches(dve, run)


def kernel(**inputs):
    import concourse.bacc as _bacc
    from concourse.bass_utils import run_bass_kernel_spmd as _run

    tok = lambda name: np.asarray(inputs["L0_tok_" + name])
    attn = lambda name: np.asarray(inputs["L0_attn_" + name])
    ffn = lambda name: np.asarray(inputs["L0_ffn_" + name])
    sw = np.stack([tok(f"sw{l}") for l in range(LAYERS)]).reshape(LAYERS, C, C, M1, KYB, KYS)
    arrays = {
        **transforms(), **token_tables(),
        "x": np.asarray(inputs["x"]).transpose(0, 3, 1, 2).reshape(B // QB, QB * CIN, PIX),
        "sw": sw.transpose(0, 4, 1, 5, 3, 2).reshape(LAYERS, KYB * C, KYS * M1 * C),
        "cw": np.stack([tok(f"cw{l}").T for l in range(LAYERS)]),
        "cb": np.stack([tok(f"cb{l}") for l in range(LAYERS)], axis=1),
        "fc0_w": tok("fc0_w"), "fc0_b": tok("fc0_b").reshape(C, 1),
        "fc1_w": tok("fc1_w"), "fc1_b": tok("fc1_b").reshape(FC1, 1),
        "fc2_w": tok("fc2_w"), "fc2_b": tok("fc2_b").reshape(1, 1),
        "txt": np.asarray(inputs["txt"]).reshape(B // 2, 2, L_TXT, D),
        **{n: attn(n) for n in ("Wq", "Wk", "Wv", "Wm", "W2")}, "W1_x": attn("W1")[:D], "W1_m": attn("W1")[D:],
        **{n: attn(n).reshape(1, D) for n in ("g1", "b1", "g2", "b2")},
        "gamma": ffn("gamma").reshape(1, D), "beta": ffn("beta").reshape(1, D),
        "Wr": ffn("Wr"), "br": ffn("br").reshape(1, EXPERTS),
        "ew1": ffn("W1").transpose(1, 0, 2), "eb1": ffn("b1").T,
        "ew2": ffn("W2").transpose(1, 0, 2), "eb2": ffn("b2"),
    }
    nc = _bacc.Bacc("TRN2", target_bir_lowering=False, num_devices=1)
    arrays = {f"in_{name}_dram": np.ascontiguousarray(a) for name, a in arrays.items()}
    ins = {name[3:-5]: nc.dram_tensor(name, a.shape, mybir.dt.from_np(a.dtype), kind="ExternalInput").ap() for name, a in arrays.items()}
    tokens = nc.dram_tensor("tokens_dram", (B, PIX), F32, kind="Internal").ap()
    scratch = nc.dram_tensor("scratch_dram", (KYS, 2, 2, KYB, S, HB * C), F16, kind="Internal").ap()
    split_weights = nc.dram_tensor("split_weights_dram", (LAYERS, KYB * C, KYS * 2 * M1 * C), F16, kind="Internal").ap()
    out = nc.dram_tensor("out_0_dram", (B // 2, 2, S + L_TXT, D), F32, kind="ExternalOutput").ap()
    build_operator(nc, ins, split_weights, scratch, tokens)
    build_tokens(nc, ins, tokens, out)
    r = _run(nc, [arrays], core_ids=[0])
    return r.results[0]["out_0_dram"].reshape(B, S + L_TXT, D)
```

```python
from contextlib import ExitStack

import numpy as np

import concourse.bass as bass
from concourse import mybir

F32 = mybir.dt.float32
F16 = mybir.dt.float16
I32 = mybir.dt.int32
ALU = mybir.AluOpType
ACT = mybir.ActivationFunctionType
AX = mybir.AxisListType

B, S, C = 64, 64, 32
CIN = 3
LAYERS = 4
M1 = M2 = 20
PIX = S * S
QB = 4
GQ = 4
GB = QB * GQ
GROUPS = B // GB
HB = GB // 2
KYB = 4
KYS = M2 // KYB
MK = KYS * M1
TJ = 2 * 2 * M2
W_SCALE = 64.0
FC1 = 64
FIRST = 1
L_TXT, D = 77, 64


def wait_apart(eng, semaphore, value, passed):
    eng.wait_ge(semaphore, value)
    eng.sem_inc(passed, 1)


def split16(a):
    hi = a.astype(np.float16)
    return hi.astype(np.float32), (a - hi.astype(np.float64)).astype(np.float16).astype(np.float32)


def transforms():
    root = np.sqrt(float(S))
    ky = np.arange(M2)
    kx = np.arange(M1)
    pos = np.arange(S)
    ang = 2 * np.pi * np.outer(pos, ky) / S
    cos, sin = np.cos(ang) / root, np.sin(ang) / root
    by_step = lambda m: m.reshape(-1, KYB, KYS).transpose(0, 2, 1).reshape(-1, M2)
    f1 = np.zeros((2, S, 2, 2, M2))
    for hp in range(2):
        f1[hp, :, hp, 0] = by_step(cos)
        f1[hp, :, hp, 1] = by_step(-sin)
    f2 = np.zeros((S // 2, QB, 2, 2, M1, 2, QB))
    for hp in range(2):
        for b in range(QB):
            f2[:, b, hp, 0, :, 0, b] = cos[hp::2]
            f2[:, b, hp, 0, :, 1, b] = -sin[hp::2]
            f2[:, b, hp, 1, :, 0, b] = sin[hp::2]
            f2[:, b, hp, 1, :, 1, b] = cos[hp::2]
    i1 = np.zeros((M1, 2, 2, S))
    i1[:, 0, 0], i1[:, 1, 0] = cos.T, -sin.T
    i1[:, 0, 1], i1[:, 1, 1] = sin.T, cos.T
    twice = np.where(ky == 0, 1.0, 2.0)[None]
    i2 = np.stack([(cos * twice).T, (-sin * twice).T])
    f1 = f1.reshape(128, TJ)
    f2 = f2.reshape(128, 4 * M1 * QB * 2)
    i1 = i1.reshape(2 * M1, 128)
    i2 = i2.reshape(2 * M2, S)
    stack = lambda m: np.concatenate([split16(m)[0], split16(m)[0], split16(m)[1]])
    both = lambda m: np.concatenate(split16(m), axis=1)
    return {
        "f1_mat": both(f1).astype(np.float32), "f2_mat": both(f2).astype(np.float32),
        "i1_mat": stack(i1).astype(np.float32), "i2_mat": stack(i2).astype(np.float32),
        "identity": np.eye(128, dtype=np.float32),
    }


def build_operator(nc, ins, split_weights, scratch, tokens):
    with ExitStack() as ctx:
        def sb(name, shape, dt):
            return ctx.enter_context(nc.sbuf_tensor(name, shape, dt))

        def sem(name):
            return ctx.enter_context(nc.semaphore(name))

        act_hl = sb("act_hl", [128, GQ, 2, PIX], F16)
        v_rows = sb("v_rows", [120, S, HB * C], F16)
        x_in = v_rows[0:QB * CIN, :, :].rearrange("p h n -> p (h n)").bitcast(F32).rearrange("p (u n) -> p u n", u=2)
        pixT = sb("pixT", [128, 2, PIX], F16)
        rows = sb("rows", [128, 2, 2, TJ * C], F16)
        spec = sb("spec", [128, 2, 2 * MK, HB], F16)
        mixw = sb("mixw", [128, 2, 2, M1, 128], F16)
        w_hl = sb("w_hl", [128, KYS, 2, M1, C], F16)
        mixed = sb("mixed", [128, 2, HB, 128], F16)
        mixedT = sb("mixedT", [128, HB, 128], F16)
        v_out = sb("v_out", [128, 2, 2, KYB, HB * C], F16)
        act32 = sb("act32", [128, 3, 1024], F32)
        f1_hl = sb("f1_hl", [128, 2, TJ], F16)
        f2_hl = sb("f2_hl", [128, 2, 4, 160], F16)
        i1_hl = sb("i1_hl", [120, 128], F16)
        i2_hl = sb("i2_hl", [120, S], F16)
        ident = sb("ident", [128, 128], F16)
        conv_all = sb("conv_all", [128, LAYERS, 2, 128], F16)
        conv_hl = sb("conv_hl", [128, 2, 2, 128], F16)
        bias_all = sb("bias_all", [128, LAYERS], F32)
        bias = sb("bias", [128, 2], F32)
        lift_w = sb("lift_w", [QB * CIN, 128], F32)
        lift_b = sb("lift_b", [128, 1], F32)
        fc1_hl = sb("fc1_hl", [128, 2, 2, 128], F16)
        fc1_b = sb("fc1_b", [128, 1], F32)
        fc2_w = sb("fc2_w", [128, 2, 32], F32)
        fc2_b = sb("fc2_b", [128, 1], F32)
        flat32 = act32[:, :, :].rearrange("p u n -> p (u n)")
        hidden = flat32[:, 0:2048].rearrange("p (u s n) -> p u s n", u=2, s=2)
        head_out = flat32[:, 2048:3072]
        start32 = act_hl[:, 0, :, :].rearrange("p s n -> p (s n)").bitcast(F32)
        conv32 = act_hl[:, 1, :, :].rearrange("p s n -> p (s n)").bitcast(F32)
        WL = KYS * M1 * C
        w_raw = [act_hl[:, 2 + n, :, :].rearrange("p s n -> p (s n)").bitcast(F32)[:, 0:WL].rearrange("p (k n) -> p k n", k=KYS) for n in range(2)]
        w_halves = [t.rearrange("p (k s n) -> p k s n", k=KYS, s=2) for t in
                    (pixT[:, :, :].rearrange("p s n -> p (s n)")[:, 0:2 * WL], rows[:, :, :, :].rearrange("p q s n -> p (q s n)")[:, 0:2 * WL])]

        psum = ctx.enter_context(nc.psum_tensor("psum", [128, 4096], F32))

        def bank(n, k=1):
            return psum[:, 512 * n:512 * (n + k)]

        consts_in = sem("consts_in")
        fill = sem("fill")
        zeroed = sem("zeroed")
        placed = sem("placed")
        consts_ready = sem("consts_ready")
        x_loaded = [sem("x_loaded0"), sem("x_loaded1")]
        layer_consts = sem("layer_consts")
        pixels_turned = sem("pixels_turned")
        turned_high = sem("turned_high")
        turned_low = sem("turned_low")
        rows_made = sem("rows_made")
        rows_high = sem("rows_high")
        rows_low = sem("rows_low")
        spec_made = sem("spec_made")
        spec_high = sem("spec_high")
        spec_low = sem("spec_low")
        w_raw_in = [sem("w_raw_in0"), sem("w_raw_in1")]
        w_high = sem("w_high")
        w_low = sem("w_low")
        w_stored = [sem("w_stored0"), sem("w_stored1")]
        w_loaded = sem("w_loaded")
        w_spread = sem("w_spread")
        w_spread_pool = sem("w_spread_pool")
        pool_passed = sem("pool_passed")
        sp_passed = sem("sp_passed")
        mix_made = sem("mix_made")
        mix_high = sem("mix_high")
        mix_low = sem("mix_low")
        mix_turned = sem("mix_turned")
        mixT_copied = sem("mixT_copied")
        v_made = sem("v_made")
        v_high = sem("v_high")
        v_low = sem("v_low")
        v_out_written = [sem("v_out_written0"), sem("v_out_written1")]
        v_moved = [sem("v_moved0"), sem("v_moved1")]
        sum_made = sem("sum_made")
        gelu_made = sem("gelu_made")
        act_high = sem("act_high")
        act_low = sem("act_low")
        fc1_made = sem("fc1_made")
        hidden_made = sem("hidden_made")
        hidden_read = sem("hidden_read")
        head_copied = sem("head_copied")
        head_stored = sem("head_stored")

        EARLY = 4
        SPLIT_AT = 8
        CHUNKS = 4 * GQ
        PASSES = 2 * LAYERS
        HCH = CHUNKS // 2
        ALL_CH = CHUNKS + PASSES * HCH
        TURNS = 8 * 2 * PASSES
        MOVES = 16 * 3


        def spec_sum():
            return bank(5, 3)[:, 0:256 * KYS].rearrange("p (k n) -> p k n", k=KYS)[:, :, 0:8 * M1].rearrange("p k (y b) -> p k y b", b=QB)

        def spec_part(hl, q):
            return spec[:, hl, :, QB * q:QB * (q + 1)].rearrange("p (k y) b -> p k y b", k=KYS)

        def rows_bank(t):
            return bank((3, 2, 4)[t % 3])[:, 0:4 * TJ]

        def rows_sum(t):
            return rows_bank(t).rearrange("p (c j) -> p j c", c=4)

        def rows_part(q, hl, m):
            return rows[:, q, hl, :].rearrange("p (j c) -> p j c", c=C)[:, :, 4 * m:4 * m + 4]

        def mix_sum(k):
            return bank(2 + k % 2)[:, 0:2 * M1 * HB].rearrange("p (y b) -> p y b", b=HB)

        def mix_part(k, part):
            return mixed[:, k % 2, :, 2 * M1 * part:2 * M1 * (part + 1)].rearrange("p b y -> p y b")

        def v_sum(t):
            return bank(5 + t % 3)[:, :].rearrange("p (b k o) -> p b k o", b=4, k=KYB)

        def v_part(k, hl, n):
            return v_out[:, k % 2, hl, :, 128 * n:128 * (n + 1)].rearrange("p k (b o) -> p b k o", b=4)

        def act_chunk(hl, n):
            return act_hl[:, n // 4, hl, 1024 * (n % 4):1024 * (n % 4 + 1)]

        def chunk_banks(n):
            return bank(2 + 2 * (n % 3), 2)

        def turned_part(n):
            return pixT[:, n % 2, 1024 * (n // 2):1024 * (n // 2 + 1)]

        def first_chunk(g, l, half):
            return g * ALL_CH + (l * 2 + half) * HCH + CHUNKS

        def first_turn(g, l, j):
            return g * TURNS + l * 32 + 8 * j

        block = ctx.enter_context(nc.Block())

        def wait_written(eng, p, k):
            eng.wait_ge(v_out_written[k % 2], p * ((3, 2)[k % 2] * 32) + (k // 2 + 1) * 32)

        def wait_moved(eng, p, k):
            eng.wait_ge(v_moved[k % 2], p * ((3, 2)[k % 2] * MOVES) + (k // 2 + 1) * MOVES)

        @block.sync
        def _(sp):
            raw_in = lambda l: sp.dma_start(w_raw[l % 2], ins["sw"][l].rearrange("p (k n) -> p k n", k=KYS)).then_inc(w_raw_in[l % 2], 16)
            raw_in(0)
            sp.dma_start(start32[:, 0:160], ins["f1_mat"]).then_inc(consts_in, 16)
            sp.dma_start(start32[:, 160:1440], ins["f2_mat"]).then_inc(consts_in, 16)
            sp.dma_start(start32[0:120, 1440:1568], ins["i1_mat"]).then_inc(consts_in, 16)
            sp.dma_start(start32[0:120, 1568:1632], ins["i2_mat"]).then_inc(consts_in, 16)
            sp.dma_start(start32[:, 1632:1760], ins["identity"]).then_inc(consts_in, 16)
            raw_in(1)

            def store_split(l):
                sp.wait_ge(w_low, l + 1)
                sp.dma_start(split_weights[l].rearrange("p (k s n) -> p k s n", k=KYS, s=2), w_halves[l % 2]).then_inc(w_stored[l % 2], 16)
                if l + 2 < LAYERS:
                    raw_in(l + 2)

            def load_x(group, q):
                src = ins["x"][bass.ds(group * GQ + q, 1), :, :].rearrange("a p n -> (a p) n")
                sp.dma_start(x_in[:, q % 2, :], src).then_inc(x_loaded[q % 2], 16)

            store_split(0)
            sp.wait_ge(zeroed, 1)
            for b in range(QB):
                p = slice(b * C, (b + 1) * C)
                sp.dma_start(conv32[p, 0:512].rearrange("p (l n) -> p l n", l=LAYERS)[:, :, b * C:(b + 1) * C], ins["cw"]).then_inc(placed, 16)
                sp.dma_start(bias_all[p, :], ins["cb"]).then_inc(placed, 16)
                sp.dma_start(conv32[p, 512 + b * FC1:512 + (b + 1) * FC1], ins["fc1_w"]).then_inc(placed, 16)
                sp.dma_start(lift_w[b * CIN:(b + 1) * CIN, p], ins["fc0_w"]).then_inc(placed, 16)
                sp.dma_start(lift_b[p, :], ins["fc0_b"]).then_inc(placed, 16)
            for b2 in range(2):
                p = slice(b2 * FC1, (b2 + 1) * FC1)
                sp.dma_start(fc1_b[p, :], ins["fc1_b"]).then_inc(placed, 16)
                for pair in range(2):
                    n = 2 * pair + b2
                    sp.dma_start(fc2_w[p, pair, n:n + 1], ins["fc2_w"]).then_inc(placed, 16)
            sp.dma_start(fc2_b[:, :], ins["fc2_b"].to_broadcast([128, 1])).then_inc(placed, 16)

            for l in range(1, LAYERS):
                store_split(l)
                if l == 1:
                    load_x(0, 0)
                    load_x(0, 1)
            for n in range(2):
                sp.wait_ge(w_stored[n], 16 * (LAYERS // 2))

            def passes(g, l):
                wait_apart(sp, w_spread, (g * PASSES + l * 2) * (3 * KYS) + FIRST, sp_passed)
                wait_apart(sp, w_spread_pool, (g * PASSES + l * 2) * KYS + FIRST, sp_passed)
                src = split_weights[bass.ds(l, 1), :, :].rearrange("a p n -> (a p) n")
                sp.dma_start(w_hl[:, :, :, :, :].rearrange("p k s x o -> p (k s x o)"), src).then_inc(w_loaded, 16)
                for half in range(2):
                    p = g * PASSES + l * 2 + half
                    for step in range(KYS + 1):
                        k = step
                        if k < KYS:
                            wait_apart(sp, v_high, p * (2 * KYS) + 2 * k + 2, sp_passed)
                            sp.wait_ge(v_low, p * (2 * KYS) + 2 * k + 2 + FIRST)
                            for ri in range(2):
                                sp.dma_start(scratch[k, ri, :, :, :, :].rearrange("s y h n -> h (s y) n"),
                                             v_out[ri * S:(ri + 1) * S, k % 2, :, :, :].rearrange("p s y n -> p (s y) n"))\
                                    .then_inc(v_out_written[k % 2], 16)
                        k = step - 1
                        if k >= 0:
                            wait_written(sp, p, k)
                            for part in range(3):
                                sp.dma_start(v_rows[40 * part + k:40 * (part + 1):KYS, :, :].rearrange("p h n -> p (h n)"),
                                             scratch[k, :, part % 2, :, :, :].rearrange("r y h n -> r y (h n)"))\
                                    .then_inc(v_moved[k % 2], 16)

            def group(g, last=False):
                for q in range(2, GQ):
                    wait_apart(sp, sum_made, g * ALL_CH + 4 * (q - 1), sp_passed)
                    load_x(g, q)
                with sp.Fori(0, LAYERS) as l:
                    passes(g, l)
                if not last:
                    wait_apart(sp, sum_made, g * ALL_CH + ALL_CH, sp_passed)
                    load_x(g + 1, 0)
                    load_x(g + 1, 1)
                for q in range(GQ):
                    wait_apart(sp, head_copied, g * GQ + q + 1 + FIRST, sp_passed)
                    for j in range(4):
                        dst = tokens[bass.ds(g * GB + q * QB, QB), :].rearrange("b (u j n) -> b u j n", u=2, j=4)[:, :, j, :]
                        src = head_out[32 * j:32 * j + QB, :].rearrange("p (u n) -> p u n", u=2)
                        sp.dma_start(dst, src).then_inc(head_stored, 16)

            with sp.Fori(0, GROUPS - 1) as g:
                group(g)
            group(GROUPS - 1, last=True)
            sp.wait_ge(head_stored, GROUPS * GQ * 4 * 16 + FIRST)

        def spread_block(engine, k, b):
            r = slice(b * C, (b + 1) * C)
            dst = mixw[r, k % 2, :, :, b * C:(b + 1) * C].bitcast(F32).rearrange("p s x o -> p (s x) o")
            return engine.tensor_copy(dst, w_hl[r, k, :, :, :].bitcast(F32).rearrange("p s x o -> p (s x) o"))

        @block.gpsimd
        def _(pool):
            for counted in (w_spread, w_spread_pool, mix_made, act_low, head_stored, turned_high, turned_low, v_low, hidden_made, head_copied):
                pool.sem_inc(counted, FIRST)
            with pool.Fori(0, GROUPS * LAYERS) as layer:
                for half in range(2):
                    for k in range(KYS):
                        wait_apart(pool, w_loaded, layer * 16 + 16, pool_passed)
                        wait_apart(pool, mix_made, (2 * layer + half) * KYS + max(k - 1, 0) + FIRST, pool_passed)
                        spread_block(nc.gpsimd, k, KYB - 1).then_inc(w_spread_pool, 1)

        @block.scalar
        def _(act):
            for l in range(LAYERS):
                act.wait_ge(w_raw_in[l % 2], 16 * (l // 2 + 1))
                if l >= 2:
                    act.wait_ge(w_stored[l % 2], 16 * (l // 2))
                nc.scalar.activation(w_halves[l % 2][:, :, 0, :], w_raw[l % 2], ACT.Copy, scale=W_SCALE).then_inc(w_high, 1)
            act.wait_ge(consts_ready, 1)

            def activate(first, n, func, add):
                act.wait_ge(sum_made, first + n + 1)
                act.wait_ge(act_low, (first + n - 2 if n >= 2 else first) + FIRST)
                nc.scalar.activation(act32[:, n % 3, :], chunk_banks(n), func, bias=add).then_inc(gelu_made, 1)

            def copy_turned(turn, n):
                act.wait_ge(pixels_turned, turn + n + 1)
                nc.scalar.activation(turned_part(n), bank(0).bitcast(F16), ACT.Copy).then_inc(turned_high, 1)

            def rows_of(p, t):
                act.wait_ge(rows_made, p * 16 + t + 1)
                nc.scalar.activation(rows_part(t // 8, 0, t % 8), rows_sum(t), ACT.Copy).then_inc(rows_high, 1)

            def one_pass(g, l, half, inverse_of, last=False):
                p = g * PASSES + l * 2 + half
                for t in range(16):
                    if t >= EARLY or inverse_of is None:
                        rows_of(p, t)
                    if t == 7:
                        for n in range(0, 8, 2):
                            copy_turned(first_turn(g, l, 2 * half + 1), n)
                    if t in (SPLIT_AT, 15):
                        q = t // 12
                        act.wait_ge(spec_made, p * 2 + q + 1)
                        nc.scalar.activation(spec_part(0, q), spec_sum(), ACT.Copy).then_inc(spec_high, 1)
                if inverse_of is not None:
                    inverse(g, *inverse_of)
                for step in range(KYS + 2):
                    k = step
                    if k < KYS:
                        act.wait_ge(mix_made, p * KYS + k + 1 + FIRST)
                        if k >= 2:
                            act.wait_ge(mix_turned, p * KYS + k - 1)
                        for part in (0, 2):
                            nc.scalar.activation(mix_part(k, part), mix_sum(k), ACT.Copy, scale=1.0 / W_SCALE).then_inc(mix_high, 1)
                    if step < 4 and not last:
                        copy_turned(first_turn(g, l, 2 * half + 2), 2 * step)
                    if step >= KYS and not last:
                        for t in (0, 1) if step == KYS else (2, 3):
                            rows_of(p + 1, t)
                    k = step - 1
                    if 0 <= k < KYS:
                        act.wait_ge(mix_turned, p * KYS + k + 1)
                        if k >= 1:
                            act.wait_ge(v_made, p * (2 * KYS) + 2 * k)
                        nc.scalar.activation(mixedT[:, :, :].rearrange("p b n -> p (b n)"), bank(4).bitcast(F16), ACT.Copy).then_inc(mixT_copied, 1)
                    k = step - 2
                    if k >= 0:
                        for n in range(2):
                            act.wait_ge(v_made, p * (2 * KYS) + 2 * k + n + 1)
                            if n == 0 and k >= 2:
                                wait_written(act, p, k - 2)
                            nc.scalar.activation(v_part(k, 0, n), v_sum(2 * k + n), ACT.Copy).then_inc(v_high, 1)

            def inverse(g, l, half):
                act.wait_ge(layer_consts, (g * PASSES + l * 2 + half) * 2 + 2)
                for n in range(HCH):
                    activate(first_chunk(g, l, half), n, ACT.Gelu, bias[:, half:half + 1])

            with act.Fori(0, GROUPS) as g:
                act.wait_ge(head_stored, g * (GQ * 4 * 16) + FIRST)
                for n in range(CHUNKS):
                    activate(g * ALL_CH, n, ACT.Identity, lift_b[:, :])
                act.wait_ge(w_stored[0], 16 * (LAYERS // 2))
                act.wait_ge(w_stored[1], 16 * (LAYERS // 2))
                for n in range(0, 8, 2):
                    copy_turned(first_turn(g, 0, 0), n)
                one_pass(g, 0, 0, None)
                one_pass(g, 0, 1, (0, 0))
                with act.Fori(1, LAYERS - 1) as l:
                    one_pass(g, l, 0, (l - 1, 1))
                    one_pass(g, l, 1, (l, 0))
                one_pass(g, LAYERS - 1, 0, (LAYERS - 2, 1))
                one_pass(g, LAYERS - 1, 1, (LAYERS - 1, 0), last=True)
                inverse(g, LAYERS - 1, 1)
                for n in range(8 * GQ):
                    act.wait_ge(fc1_made, g * (8 * GQ) + n + 1)
                    if n < 2:
                        act.wait_ge(act_low, g * ALL_CH + ALL_CH + FIRST)
                    else:
                        act.wait_ge(hidden_read, g * (8 * GQ) + n - 1)
                    nc.scalar.activation(hidden[:, n % 2, :, :], chunk_banks(n).rearrange("p (s n) -> p s n", s=2), ACT.Gelu, bias=fc1_b[:, :])\
                        .then_inc(hidden_made, 1)

        @block.vector
        def _(dve):
            def split_weights_low(l):
                dve.wait_ge(w_high, l + 1)
                nc.vector.scalar_tensor_tensor(out=w_halves[l % 2][:, :, 1, :], in0=w_raw[l % 2], scalar=W_SCALE, in1=w_halves[l % 2][:, :, 0, :],
                                               op0=ALU.mult, op1=ALU.subtract).then_inc(w_low, 1)

            for t in (conv32[:, 0:768], lift_w[:, :], fc2_w[:, :, :], mixw[:, :, :, :, :], mixed[:, :, :, :]):
                nc.vector.memset(t, 0.0).then_inc(fill, 1)
            dve.wait_ge(fill, 5)
            dve.sem_inc(zeroed, 1)
            split_weights_low(0)
            split_weights_low(1)
            dve.wait_ge(consts_in, 5 * 16)
            nc.vector.tensor_copy(f1_hl[:, :, :], start32[:, 0:160].rearrange("p (s n) -> p s n", s=2)).then_inc(fill, 1)
            nc.vector.tensor_copy(f2_hl[:, :, :, :], start32[:, 160:1440].rearrange("p (s m n) -> p s m n", s=2, m=4)).then_inc(fill, 1)
            nc.vector.tensor_copy(i1_hl[:, :], start32[0:120, 1440:1568]).then_inc(fill, 1)
            nc.vector.tensor_copy(i2_hl[:, :], start32[0:120, 1568:1632]).then_inc(fill, 1)
            nc.vector.tensor_copy(ident[:, :], start32[:, 1632:1760]).then_inc(fill, 1)
            split_weights_low(2)
            dve.wait_ge(placed, 16 * (5 * QB + 7))
            conv_raw = conv32[:, 0:512].rearrange("p (l n) -> p l n", l=LAYERS)
            fc1_raw = conv32[:, 512:768].rearrange("p (l n) -> p l n", l=2)
            nc.vector.tensor_copy(conv_all[:, :, 0, :], conv_raw).then_inc(fill, 1)
            nc.vector.tensor_copy(fc1_hl[:, :, 0, :], fc1_raw).then_inc(fill, 1)
            dve.wait_ge(fill, 12)
            nc.vector.tensor_tensor(conv_all[:, :, 1, :], conv_raw, conv_all[:, :, 0, :], ALU.subtract).then_inc(fill, 1)
            nc.vector.tensor_tensor(fc1_hl[:, :, 1, :], fc1_raw, fc1_hl[:, :, 0, :], ALU.subtract).then_inc(fill, 1)
            dve.wait_ge(fill, 14)
            dve.sem_inc(consts_ready, 1)
            split_weights_low(3)
            def split_chunk(first, n, at):
                dve.wait_ge(gelu_made, first + n + 1)
                nc.vector.tensor_copy(act_chunk(0, at), act32[:, n % 3, :]).then_inc(act_high, 1)
                dve.wait_ge(act_high, first + n + 1)
                nc.vector.tensor_tensor(act_chunk(1, at), act32[:, n % 3, :], act_chunk(0, at), ALU.subtract).then_inc(act_low, 1)

            def copy_turned(turn, n):
                dve.wait_ge(pixels_turned, turn + n + 1)
                nc.vector.tensor_copy(turned_part(n), bank(1).bitcast(F16)).then_inc(turned_low, 1)

            def spread(layer, p, k):
                dve.wait_ge(w_loaded, layer * 16 + 16)
                if k >= 2:
                    dve.wait_ge(mix_made, p * KYS + k - 1 + FIRST)
                for b in range(KYB - 1):
                    spread_block(nc.vector, k, b).then_inc(w_spread, 1)

            def layer_consts_of(l, half):
                nc.vector.tensor_copy(conv_hl[:, half, :, :], conv_all[:, bass.ds(l, 1), :, :].rearrange("p a s n -> p (a s) n")).then_inc(layer_consts, 1)
                nc.vector.tensor_copy(bias[:, half:half + 1], bias_all[:, bass.ds(l, 1)]).then_inc(layer_consts, 1)

            def inverse(g, l, half):
                for n in range(HCH):
                    split_chunk(first_chunk(g, l, half), n, HCH * half + n)

            def rows_of(p, t):
                dve.wait_ge(rows_high, p * 16 + t + 1)
                nc.vector.tensor_tensor(rows_part(t // 8, 1, t % 8), rows_sum(t), rows_part(t // 8, 0, t % 8), ALU.subtract).then_inc(rows_low, 1)

            def one_pass(g, l, half, inverse_of, last=False):
                p = g * PASSES + l * 2 + half
                layer = g * LAYERS + l
                for t in range(16):
                    if t >= EARLY or inverse_of is None:
                        rows_of(p, t)
                    if t == 7:
                        for n in range(1, 8, 2):
                            copy_turned(first_turn(g, l, 2 * half + 1), n)
                    if t == 15:
                        spread(layer, p, 0)
                        spread(layer, p, 1)
                    if t in (SPLIT_AT, 15):
                        q = t // 12
                        dve.wait_ge(spec_high, p * 2 + q + 1)
                        nc.vector.tensor_tensor(spec_part(1, q), spec_sum(), spec_part(0, q), ALU.subtract).then_inc(spec_low, 1)
                if inverse_of is not None:
                    inverse(g, *inverse_of)
                layer_consts_of(l, half)
                for step in range(KYS + 2):
                    k = step
                    if k < KYS:
                        dve.wait_ge(mix_high, p * (2 * KYS) + 2 * k + 2)
                        nc.vector.scalar_tensor_tensor(out=mix_part(k, 1), in0=mix_sum(k), scalar=1.0 / W_SCALE, in1=mix_part(k, 0),
                                                       op0=ALU.mult, op1=ALU.subtract).then_inc(mix_low, 1)
                    if step < 4 and not last:
                        copy_turned(first_turn(g, l, 2 * half + 2), 2 * step + 1)
                    if step >= KYS and not last:
                        for t in (0, 1) if step == KYS else (2, 3):
                            rows_of(p + 1, t)
                    if k + 2 < KYS:
                        spread(layer, p, k + 2)
                    k = step - 2
                    if k >= 0:
                        for n in range(2):
                            dve.wait_ge(v_high, p * (2 * KYS) + 2 * k + n + 1)
                            nc.vector.tensor_tensor(v_part(k, 1, n), v_sum(2 * k + n), v_part(k, 0, n), ALU.subtract).then_inc(v_low, 1)

            with dve.Fori(0, GROUPS) as g:
                for n in range(CHUNKS):
                    split_chunk(g * ALL_CH, n, n)
                dve.wait_ge(w_stored[0], 16 * (LAYERS // 2))
                dve.wait_ge(w_stored[1], 16 * (LAYERS // 2))
                for n in range(1, 8, 2):
                    copy_turned(first_turn(g, 0, 0), n)
                one_pass(g, 0, 0, None)
                one_pass(g, 0, 1, (0, 0))
                with dve.Fori(1, LAYERS - 1) as l:
                    one_pass(g, l, 0, (l - 1, 1))
                    one_pass(g, l, 1, (l, 0))
                one_pass(g, LAYERS - 1, 0, (LAYERS - 2, 1))
                one_pass(g, LAYERS - 1, 1, (LAYERS - 1, 0), last=True)
                inverse(g, LAYERS - 1, 1)
                for q in range(GQ):
                    dve.wait_ge(hidden_read, g * (8 * GQ) + 8 * q + 8)
                    dve.wait_ge(head_stored, (g * GQ + q) * (4 * 16) + FIRST)
                    nc.vector.tensor_scalar(head_out, bank(0, 2), fc2_b[:, :], None, ALU.add).then_inc(head_copied, 1)

        @block.tensor
        def _(pe):
            pe.wait_ge(consts_ready, 1)

            def three(out, weights, data, start, stop):
                for n, (a, b) in enumerate(((0, 0), (0, 1), (1, 0))):
                    last = nc.tensor.matmul(out, weights[a], data[b], start=start and n == 0, stop=stop and n == 2)
                return last

            def turn(first, act_done, q, n):
                if n == 0:
                    pe.wait_ge(act_low, act_done + FIRST)
                pe.wait_ge((turned_high, turned_low)[n % 2], first + n // 2 + FIRST)
                for j in range(8):
                    at = 128 * (8 * (n // 2) + j)
                    last = nc.tensor.transpose(bank(n % 2).bitcast(F16)[:, 128 * j:128 * (j + 1)], act_hl[:, q, n % 2, at:at + 128], ident[:, :])
                last.then_inc(pixels_turned, 1)

            def quad_ready(g, l, half, q):
                return first_chunk(g, l - 1, half) + 4 * (q + 1)

            def to_rows(g, l, quad, p, t):
                if t % 8 == 0:
                    done = g * (TURNS // 2) + l * 16 + 4 * quad + 4
                    pe.wait_ge(turned_high, done + FIRST)
                    pe.wait_ge(turned_low, done + FIRST)
                if t >= 3:
                    pe.wait_ge(rows_low, p * 16 + t - 2)
                for j in range(4):
                    c = 4 * (t % 8) + j
                    last = three(rows_bank(t)[:, TJ * j:TJ * (j + 1)], [pixT[:, s, c::C] for s in range(2)],
                                 [f1_hl[:, s, :] for s in range(2)], True, True)
                last.then_inc(rows_made, 1)

            def to_spectrum(p, q, k):
                if k == 0:
                    pe.wait_ge(rows_low, p * 16 + 8 * (q + 1))
                    if q == 0:
                        pe.wait_ge(v_low, p * (2 * KYS) + FIRST)
                    else:
                        pe.wait_ge(spec_low, p * 2 + q)
                for r in range(4):
                    at = C * (r * KYS + k) * KYB
                    last = three(bank(5, 3)[:, 256 * k:256 * k + 8 * M1], [rows[:, q, s, at:at + 128] for s in range(2)],
                                 [f2_hl[:, s, r, :] for s in range(2)], r == 0, r == 3)
                if k == KYS - 1:
                    last.then_inc(spec_made, 1)

            def inverse(g, l, half, after):
                p = g * PASSES + l * 2 + half
                first = first_chunk(g, l, half)
                pe.wait_ge(layer_consts, p * 2 + 2)
                for n in range(HCH):
                    if n == 1:
                        after()
                    if n >= 3:
                        pe.wait_ge(gelu_made, first + n - 2)
                    q = 2 * half + n // 4
                    banks = 2 + 2 * (n % 3)
                    for u in range(2):
                        at = 1024 * (n % 4) + 512 * u
                        three(bank(banks + u), [conv_hl[:, half, s, :] for s in range(2)], [act_hl[:, q, s, at:at + 512] for s in range(2)], True, False)
                    if n == 0:
                        wait_moved(pe, p, KYS - 1)
                        wait_moved(pe, p, KYS - 2)
                    for r in range(16):
                        last = nc.tensor.matmul(bank(banks + r // 8)[:, S * (r % 8):S * (r % 8 + 1)],
                                                v_rows[:, 16 * (n % 4) + r, 128 * (n // 4):128 * (n // 4 + 1)], i2_hl[:, :],
                                                start=False, stop=r % 8 == 7)
                    last.then_inc(sum_made, 1)

            def one_pass(g, l, half, inverse_of, last=False):
                p = g * PASSES + l * 2 + half
                for q in range(2):
                    for t in range(8 * q, 8 * q + 8):
                        if t >= EARLY or inverse_of is None:
                            to_rows(g, l, 2 * half + q, p, t)
                    for n in range(8):
                        if q == 0:
                            turn_at(g, l, 2 * half + 1, n)
                        if n >= 1 and n <= KYS:
                            to_spectrum(p, q, n - 1)
                spec_split = lambda: pe.wait_ge(spec_low, p * 2 + 2)
                if inverse_of is not None:
                    inverse(g, *inverse_of, spec_split)
                    pe.wait_ge(gelu_made, first_chunk(g, *inverse_of) + HCH - 1)
                else:
                    spec_split()
                for step in range(KYS + 2):
                    k = step
                    if k < KYS:
                        pe.wait_ge(w_spread, p * (3 * KYS) + 3 * k + 3 + FIRST)
                        pe.wait_ge(w_spread_pool, p * KYS + k + 1 + FIRST)
                        if k >= 2:
                            pe.wait_ge(mix_low, p * KYS + k - 1)
                        for x in range(M1):
                            y = 2 * (k * M1 + x)
                            mixing = three(bank(2 + k % 2)[:, 2 * HB * x:2 * HB * (x + 1)], [mixw[:, k % 2, s, x, :] for s in range(2)],
                                         [spec[:, s, y:y + 2, :] for s in range(2)], True, True)
                        mixing.then_inc(mix_made, 1)
                    if step < 4 and not last:
                        for n in (2 * step, 2 * step + 1):
                            turn_at(g, l, 2 * half + 2, n)
                    if step == KYS and not last:
                        to_rows(g, l, 2 * half + 2, p + 1, 0)
                    k = step - 1
                    if 0 <= k < KYS:
                        pe.wait_ge(mix_low, p * KYS + k + 1)
                        if k == 0 and inverse_of is not None:
                            pe.wait_ge(gelu_made, first_chunk(g, *inverse_of) + HCH)
                        if k >= 1:
                            pe.wait_ge(mixT_copied, p * KYS + k)
                        for j in range(HB):
                            turned = nc.tensor.transpose(bank(4).bitcast(F16)[:, 128 * j:128 * (j + 1)], mixed[:, k % 2, j, :], ident[:, :])
                        turned.then_inc(mix_turned, 1)
                    if step == KYS and not last:
                        to_rows(g, l, 2 * half + 2, p + 1, 1)
                    k = step - 2
                    if k >= 0:
                        pe.wait_ge(mixT_copied, p * KYS + k + 1)
                        for n in range(2):
                            t = 2 * k + n
                            if t >= 3:
                                pe.wait_ge(v_low, p * (2 * KYS) + t - 2 + FIRST)
                            nc.tensor.matmul(bank(5 + t % 3), i1_hl[:, :], mixedT[0:120, 4 * n:4 * n + 4, :], start=True, stop=True)\
                                .then_inc(v_made, 1)
                    if step == KYS + 1 and not last:
                        for t in (2, 3):
                            to_rows(g, l, 2 * half + 2, p + 1, t)

            def turn_at(g, l, j, n):
                ready = quad_ready(g, l, j // 2, j % 2) if j < 4 else quad_ready(g, l + 1, 0, 0)
                if j < 4 and isinstance(l, int) and l == 0:
                    ready = g * ALL_CH + 4 * (j + 1)
                turn(g * (TURNS // 2) + l * 16 + 4 * j, ready, j % 4, n)

            with pe.Fori(0, GROUPS) as g:
                for n in range(CHUNKS):
                    if n % 4 == 0:
                        pe.wait_ge(x_loaded[(n // 4) % 2], g * 32 + 16 * (n // 8 + 1))
                    if n == 0:
                        pe.wait_ge(hidden_made, g * (8 * GQ) + FIRST)
                    if n >= 3:
                        pe.wait_ge(gelu_made, g * ALL_CH + n - 2)
                    for u in range(2):
                        at = 1024 * (n % 4) + 512 * u
                        last = nc.tensor.matmul(bank(2 + 2 * (n % 3) + u), lift_w[:, :], x_in[:, (n // 4) % 2, at:at + 512], start=True, stop=True)
                    last.then_inc(sum_made, 1)
                pe.wait_ge(head_copied, g * GQ + FIRST)
                for n in range(8):
                    turn_at(g, 0, 0, n)
                pe.wait_ge(gelu_made, g * ALL_CH + CHUNKS)
                one_pass(g, 0, 0, None)
                one_pass(g, 0, 1, (0, 0))
                with pe.Fori(1, LAYERS - 1) as l:
                    one_pass(g, l, 0, (l - 1, 1))
                    one_pass(g, l, 1, (l, 0))
                one_pass(g, LAYERS - 1, 0, (LAYERS - 2, 1))
                one_pass(g, LAYERS - 1, 1, (LAYERS - 1, 0), last=True)
                inverse(g, LAYERS - 1, 1, lambda: pe.wait_ge(v_low, (g + 1) * (PASSES * 2 * KYS) + FIRST))

                pe.wait_ge(turned_high, (g + 1) * (TURNS // 2) + FIRST)
                pe.wait_ge(turned_low, (g + 1) * (TURNS // 2) + FIRST)
                pe.wait_ge(act_low, g * ALL_CH + ALL_CH + FIRST)
                for n in range(8 * GQ + 1):
                    if n < 8 * GQ:
                        if n >= 3:
                            pe.wait_ge(hidden_made, g * (8 * GQ) + n - 2 + FIRST)
                        at = 512 * (n % 8)
                        for pair in range(2):
                            last = three(bank(2 + 2 * (n % 3) + pair), [fc1_hl[:, pair, s, :] for s in range(2)],
                                         [act_hl[:, n // 8, s, at:at + 512] for s in range(2)], True, True)
                        last.then_inc(fc1_made, 1)
                    if n >= 1:
                        m = n - 1
                        pe.wait_ge(hidden_made, g * (8 * GQ) + m + 1 + FIRST)
                        if m % 8 == 0:
                            pe.wait_ge(head_copied, g * GQ + m // 8 + FIRST)
                        row = 32 * (m % 4)
                        for pair in range(2):
                            last = nc.tensor.matmul(bank((m % 8) // 4)[row:row + 32, :], fc2_w[:, pair, :], hidden[:, m % 2, pair, :],
                                                    start=pair == 0, stop=pair == 1)
                        last.then_inc(hidden_read, 1)


SIDES = 2
PAIRS = 2 * SIDES
BATCHES = B // (2 * PAIRS)
CH = 3 * PAIRS
VJ = CH // 2
PW = 3 * 128
HEADS = 8
HD = D // HEADS
FF = 2 * D
EXPERTS, TOP = 8, 2
STEPS = PAIRS * EXPERTS
LAG = 3
LN_EPS, ATT_EPS = 1e-5, 1e-6
AT_X, AT_QK, AT_KV, AT_MSG, AT_NORM1, AT_NORM2, AT_NORM3, AT_NORM4, AT_GATES, AT_END = 4, 4, 5, 7, 12, 20, 26, 31, 34, STEPS + LAG + 1


def token_tables():
    head = np.arange(2 * D) // HD
    one_head = (head[:, None] == head[None, :]).astype(np.float32)
    pick = np.zeros((128, EXPERTS, 128), np.float32)
    for e in range(EXPERTS):
        pick[[e, EXPERTS + e], e] = 1.0
    before = (np.arange(EXPERTS)[None, :] < np.arange(EXPERTS)[:, None]).astype(np.float32).reshape(1, -1)
    return {"one_head": one_head, "pick": pick.reshape(128, -1), "before": np.ascontiguousarray(np.broadcast_to(before, (128, 64)))}


def build_tokens(nc, ins, tokens, out):
    with ExitStack() as ctx:
        def sb(name, shape, dt=F32):
            return ctx.enter_context(nc.sbuf_tensor(name, shape, dt))

        def sem(name):
            return ctx.enter_context(nc.semaphore(name))

        h_in = sb("h_in", [128, 2, CH, D])
        x = sb("x", [128, CH, D])
        msg = sb("msg", [128, CH, D])
        centred = sb("centred", [128, CH, D])
        squares = sb("squares", [128, CH, D])
        stat = sb("stat", [128, 4, CH])
        xT = sb("xT", [128, SIDES, PW])
        q_neg = sb("q_neg", [128, SIDES, PW])
        q_exp = sb("q_exp", [128, SIDES, PW])
        q_pos = sb("q_pos", [128, SIDES, PW])
        k_neg = sb("k_neg", [128, CH, D])
        k_exp = sb("k_exp", [128, CH, D])
        k_pos = sb("k_pos", [128, CH, D])
        v_one = sb("v_one", [128, CH, D + 1])
        kv_head = sb("kv_head", [128, 4, 2, 2, D])
        z_inv = sb("z_inv", [128, SIDES, PW])
        msgT = sb("msgT", [128, SIDES, PW])
        normT = sb("normT", [128, SIDES, PW])
        hid = sb("hid", [128, PAIRS, PW])
        logit = sb("logit", [128, CH, EXPERTS])
        cmp_gt = sb("cmp_gt", [128, CH, EXPERTS, EXPERTS])
        cmp_eq = sb("cmp_eq", [128, CH, EXPERTS, EXPERTS])
        rank = sb("rank", [128, CH, EXPERTS])
        rexp = sb("rexp", [128, CH, EXPERTS])
        gate = sb("gate", [128, CH, EXPERTS])
        gate_hl = sb("gate_hl", [128, CH, 128], F16)
        xn = sb("xn", [128, CH, D])
        xn_hl = sb("xn_hl", [128, CH, 2, D], F16)
        h_mid = sb("h_mid", [128, 2, CH, D])
        xnT = sb("xnT", [128, 2, PAIRS, PW], F16)
        gateT = sb("gateT", [128, 2, PAIRS, PW], F16)
        h_out = sb("h_out", [128, CH, D])
        eh = sb("eh", [128, 2, PW])
        eg = sb("eg", [128, 4, PW])
        eg_hl = sb("eg_hl", [128, 4, 2, PW], F16)
        ident = sb("t_ident", [128, 128])
        ident16 = sb("t_ident16", [128, 128], F16)
        one_head = sb("one_head", [128, 2, D])
        before = sb("before", [128, EXPERTS, EXPERTS])
        proj = sb("proj", [128, 4, 128])
        w1 = sb("w1", [128, 2, 2, FF])
        w2 = sb("w2", [FF, D])
        vec_all = sb("vec_all", [128, 6 * D + EXPERTS])
        vecs = vec_all[:, 0:6 * D].rearrange("p (n w) -> p n w", n=6)
        br = vec_all[:, 6 * D:6 * D + EXPERTS]
        raw = sb("raw", [128, EXPERTS, FF])
        raw2 = sb("raw2", [FF, EXPERTS, D])
        raw_r = sb("raw_r", [128, EXPERTS])
        raw_b = sb("raw_b", [128, D])
        raw_p = sb("raw_p", [128, EXPERTS, 128])
        pick = sb("pick", [128, EXPERTS, 128], F16)
        wr = sb("wr", [128, 2, EXPERTS], F16)
        ew1 = sb("ew1", [128, 2, EXPERTS, FF], F16)
        eb1 = sb("eb1", [FF, EXPERTS])
        ew2 = sb("ew2", [FF, 2, EXPERTS, D], F16)
        eb2 = sb("eb2", [128, 2, D], F16)
        zeros = sb("zeros", [128, 3 * D], F16)
        psum = ctx.enter_context(nc.psum_tensor("t_psum", [128, 4096], F32))

        def sides_at(first):
            return psum[:, 512 * first:512 * (first + 2)].rearrange("p (v w) -> p v w", v=2)[:, :, 0:PW]

        def block_at(first, block):
            return sides_at(first)[:, block // 3, 128 * (block % 3):128 * (block % 3 + 1)]

        def side(t, v):
            return t[:, VJ * v:VJ * (v + 1), :].rearrange("p c w -> p (c w)")

        def block_of(t, block):
            return t[:, 2 * block:2 * block + 2, :].rearrange("p c w -> p (c w)")

        def turned_block(t, block):
            return t[:, block // 3, 128 * (block % 3):128 * (block % 3 + 1)]

        HIDDEN, GATES, SUMS = 4, 6, 7
        def bank(n, cols=PW):
            return psum[:, 512 * n:512 * n + cols]

        w_in = sem("w_in")
        zeros_set = sem("zeros_set")
        weights_ready = sem("weights_ready")
        pe_passed = sem("pe_passed")
        dve_passed = sem("dve_passed")
        sp_passed = sem("t_sp_passed")
        loaded = [sem("loaded0"), sem("loaded1")]
        dve_step = sem("dve_step")
        x_made = sem("x_made")
        x_turned = sem("x_turned")
        xT_copied = sem("xT_copied")
        qk_summed = sem("qk_summed")
        neg_made = sem("neg_made")
        exp_made = sem("exp_made")
        q_made = sem("q_made")
        k_made = sem("k_made")
        v_summed = sem("v_summed")
        v_copied = sem("v_copied")
        kv_made = sem("kv_made")
        kv_masked = sem("kv_masked")
        msg_summed = sem("msg_summed")
        msg_made = sem("msg_made")
        msg_mixed = sem("msg_mixed")
        message_normed = sem("message_normed")
        norm_turned = sem("norm_turned")
        normT_copied = sem("normT_copied")
        hid_summed = sem("hid_summed")
        hid_made = sem("hid_made")
        msg2_made = sem("msg2_made")
        h_mid_made = sem("h_mid_made")
        xn_made = sem("xn_made")
        xn_turned = sem("xn_turned")
        xnT_copied = sem("xnT_copied")
        logits_made = sem("logits_made")
        rexp_in = sem("rexp_in")
        rexp_made = sem("rexp_made")
        gate_made = sem("gate_made")
        gate_turned = sem("gate_turned")
        gateT_copied = sem("gateT_copied")
        e_summed = sem("e_summed")
        e_gates = sem("e_gates")
        e_gelu = sem("e_gelu")
        e_gated = sem("e_gated")
        e_high = sem("e_high")
        e_low = sem("e_low")
        e_added = sem("e_added")
        e_read = sem("e_read")
        stored = sem("stored")

        block = ctx.enter_context(nc.Block())
        weights = [(ident[:, :], "identity"), (one_head[:, :, :].rearrange("p u n -> p (u n)"), "one_head"),
                   (raw_p[:, :, :].rearrange("p e n -> p (e n)"), "pick"),
                   (before[:, :, :].rearrange("p a b -> p (a b)"), "before"), (w2[:, :], "W2"), (eb1[:, :], "eb1"), (raw2[:, :, :], "ew2")]
        for u in range(2):
            rows = slice(D * u, D * (u + 1))
            weights += [(proj[rows, :, D * u:D * (u + 1)], "proj"), (w1[rows, :, u, :], "W1")]
            weights += [(raw[rows, :, :], "ew1"), (raw_r[rows, :], "Wr"), (raw_b[EXPERTS * u:EXPERTS * (u + 1), :], "eb2")]
        N_W = len(weights) + 1
        tok_rows = tokens.rearrange("b (h w) -> (b h) w", h=S)
        chunks = lambda t: t.rearrange("p (v j u) w -> p v j u w", v=2, j=3)

        LAST = BATCHES - 1

        def batches(engine, run):
            run((0, 0), None)
            with engine.Fori(0, BATCHES // 2 - 1) as two:
                run((two * 2 + 1, 1), (two * 2, 0))
                run((two * 2 + 2, 0), (two * 2 + 1, 1))
            run((LAST, 1), (LAST - 1, 0))
            run(None, (LAST, 1))

        @block.sync
        def _(sp):
            sp.wait_ge(zeros_set, 1)
            def load(it, parity):
                src = tok_rows[bass.ds(it * (PAIRS * 128), PAIRS * 128), :].rearrange("(v u p) w -> p v u w", p=128, u=2)
                txt = ins["txt"][bass.ds(it * PAIRS, PAIRS), :, :, :].rearrange("(v u) t p w -> p v u t w", u=2)
                for u in range(2):
                    sp.dma_start(chunks(h_in[:, parity, :, :])[:, :, 1, u, :], src[:, :, u, :]).then_inc(loaded[parity], 16)
                    for t in range(2):
                        sp.dma_start(chunks(h_in[0:L_TXT, parity, :, :])[:, :, 2 * t, u, :], txt[:, :, u, t, :]).then_inc(loaded[parity], 16)

            load(0, 0)
            for dst, name in weights:
                sp.dma_start(dst, ins[name]).then_inc(w_in, 16)
            sp.dma_start(vec_all[:, :], ins["vecs"].to_broadcast([128, 6 * D + EXPERTS])).then_inc(w_in, 16)
            load(1, 1)

            def run(a, e):
                if a is not None and e is not None and a[0] is not LAST:
                    wait_apart(sp, h_mid_made, a[0], sp_passed)
                    load(a[0] + 1, 1 - a[1])
                if e is not None:
                    it = e[0]
                    wait_apart(sp, e_read, (it + 1) * PAIRS, sp_passed)
                    dst = out[bass.ds(it * PAIRS, PAIRS), :, :, :].rearrange("(v u) t p w -> p v u t w", u=2)
                    for u in range(2):
                        for t in range(2):
                            sp.dma_start(dst[0:S, :, u, t, :], chunks(h_out[S * t:S * (t + 1), :, :])[:, :, 1, u, :]).then_inc(stored, 16)
                            sp.dma_start(dst[S:S + L_TXT, :, u, t, :], chunks(h_out[0:L_TXT, :, :])[:, :, 2 * t, u, :]).then_inc(stored, 16)

            batches(sp, run)
            sp.wait_ge(stored, BATCHES * 8 * 16 + FIRST)

        @block.tensor
        def _(pe):
            mm = nc.tensor.matmul
            pe.wait_ge(weights_ready, 1)

            def run(a, e):
                done = [0]

                def experts_to(target):
                    while e is not None and done[0] < target:
                        step(e[0], e[1], done[0])
                        done[0] += 1

                def step(it, parity, s):
                    if s < STEPS:
                        n, x = s // EXPERTS, s % EXPERTS
                        if s == 0:
                            wait_apart(pe, gateT_copied, it + 1, pe_passed)
                        if s >= 2:
                            pe.wait_ge(e_gelu, it * STEPS + s - 1)
                        for part in range(2):
                            last = mm(bank(HIDDEN + s % 2), ew1[:, part, x, :], xnT[:, parity, n, :], start=part == 0, stop=part == 1)
                        last.then_inc(e_summed, 1)
                        if s >= 1:
                            pe.wait_ge(e_gated, it * STEPS + s)
                        mm(bank(GATES), pick[:, x, :], gateT[:, parity, n, :], start=True, stop=True).then_inc(e_gates, 1)
                    m = s - LAG
                    if 0 <= m < STEPS:
                        n, x = m // EXPERTS, m % EXPERTS
                        if m % EXPERTS == 0 and m > 0:
                            pe.wait_ge(e_read, it * PAIRS + n)
                        pe.wait_ge(e_low, it * STEPS + m + 1)
                        pe.wait_ge(e_high, it * STEPS + m + 1)
                        if x == 0:
                            mm(bank(SUMS, 3 * D), gateT[:, parity, n, 0:128], zeros[:, :], start=True, stop=False)
                        for j in range(3):
                            at = slice(128 * j, 128 * (j + 1))
                            dst = bank(SUMS)[:, D * j:D * (j + 1)]
                            if x == 0:
                                for part in range(2):
                                    mm(dst, gateT[:, parity, n, at], eb2[:, part, :], start=False, stop=False)
                            mm(dst, eg_hl[:, m % 4, 0, at], ew2[:, 0, x, :], start=False, stop=False)
                            mm(dst, eg_hl[:, m % 4, 0, at], ew2[:, 1, x, :], start=False, stop=False)
                            last = mm(dst, eg_hl[:, m % 4, 1, at], ew2[:, 0, x, :], start=False, stop=x == EXPERTS - 1 and j == 2)
                        last.then_inc(e_added, 1)

                if a is None:
                    experts_to(AT_END)
                    return
                it, parity = a
                experts_to(AT_X)
                if e is not None:
                    wait_apart(pe, gateT_copied, it, pe_passed)
                wait_apart(pe, x_made, it + 1, pe_passed)
                for v in range(2):
                    for n in range(3 * v, 3 * v + 3):
                        last = nc.tensor.transpose(block_at(0, n), block_of(x, n), ident[:, :])
                    last.then_inc(x_turned, 1)
                for v in range(2):
                    wait_apart(pe, xT_copied, it * 2 + v + 1, pe_passed)
                    mm(sides_at(0)[:, v, :], proj[:, 0, :], xT[:, v, :], start=True, stop=True)
                    for n in range(3 * v, 3 * v + 3):
                        last = mm(block_at(2, n), turned_block(xT, n), proj[:, 1, :], start=True, stop=True)
                    last.then_inc(qk_summed, 1)
                experts_to(AT_QK)
                for v in range(2):
                    wait_apart(pe, q_made, it * 2 + v + 1, pe_passed)
                    for n in range(3 * v, 3 * v + 3):
                        last = mm(block_at(0, n), turned_block(xT, n), proj[:, 2, :], start=True, stop=True)
                    last.then_inc(v_summed, 1)
                wait_apart(pe, k_made, it * 2 + 2, pe_passed)
                wait_apart(pe, v_copied, it * 2 + 2, pe_passed)
                for v in range(2):
                    for t in range(2):
                        dst = bank(2 + t, 512)[:, 130 * v:130 * (v + 1)]
                        for r, j in ((slice(S * t, S * (t + 1)), 1), (slice(0, L_TXT), 2 * t)):
                            c = 2 * (3 * v + j)
                            last = mm(dst, k_pos[r, c:c + 2, :].rearrange("p u w -> p (u w)"), v_one[r, c:c + 2, :].rearrange("p u w -> p (u w)"),
                                      start=j == 1, stop=j != 1)
                last.then_inc(kv_made, 1)
                experts_to(AT_KV)
                wait_apart(pe, kv_masked, it + 1, pe_passed)
                for v in range(2):
                    for part in (1, 0):
                        for t in range(2):
                            c = slice(192 * t, 192 * (t + 1))
                            last = mm(sides_at(2 * part)[:, v, c], kv_head[:, 2 * t + v, part, :, :].rearrange("p u w -> p (u w)"), q_pos[:, v, c],
                                      start=True, stop=True)
                    last.then_inc(msg_summed, 1)
                experts_to(AT_MSG)
                for v in range(2):
                    wait_apart(pe, msg_made, it * 2 + v + 1, pe_passed)
                    for n in range(3 * v, 3 * v + 3):
                        last = mm(block_at(0, n), turned_block(msgT, n), proj[:, 3, :], start=True, stop=True)
                last.then_inc(msg_mixed, 1)
                experts_to(AT_NORM1)
                wait_apart(pe, message_normed, it + 1, pe_passed)
                for v in range(2):
                    for n in range(3 * v, 3 * v + 3):
                        last = nc.tensor.transpose(block_at(2, n), block_of(msg, n), ident[:, :])
                    last.then_inc(norm_turned, 1)
                for n in range(PAIRS):
                    v, u = n // 2, n % 2
                    if u == 0:
                        wait_apart(pe, normT_copied, it * 2 + v + 1, pe_passed)
                    mm(bank(n), w1[:, 0, u, :], xT[:, v, :], start=True, stop=False)
                    mm(bank(n), w1[:, 1, u, :], normT[:, v, :], start=False, stop=True).then_inc(hid_summed, 1)
                for v in range(2):
                    wait_apart(pe, hid_made, it * PAIRS + 2 * v + 2, pe_passed)
                    for j in range(3):
                        for u in range(2):
                            last = mm(sides_at(0)[:, v, 128 * j + D * u:128 * j + D * (u + 1)], hid[:, 2 * v + u, 128 * j:128 * (j + 1)], w2[:, :],
                                      start=True, stop=True)
                last.then_inc(msg2_made, 1)
                experts_to(AT_NORM4)
                wait_apart(pe, xn_made, it + 1, pe_passed)
                for n in range(PAIRS):
                    for j in range(3):
                        at = 128 * (3 * n + j)
                        last = nc.tensor.transpose(bank(0, 1024).bitcast(F16)[:, at:at + 128],
                                                   xn_hl[:, 2 * (3 * (n // 2) + j) + n % 2, :, :].rearrange("p s w -> p (s w)"), ident16[:, :])
                last.then_inc(xn_turned, 1)
                wait_apart(pe, xnT_copied, it + 1, pe_passed)
                for n in range(PAIRS):
                    for j in range(3):
                        c = 2 * (3 * (n // 2) + j) + n % 2
                        for part in range(2):
                            last = mm(bank(2)[:, EXPERTS * c:EXPERTS * (c + 1)], xnT[:, parity, n, 128 * j:128 * (j + 1)], wr[:, part, :],
                                      start=part == 0, stop=part == 1)
                last.then_inc(logits_made, 1)
                experts_to(AT_GATES)
                wait_apart(pe, gate_made, it + 1, pe_passed)
                for n in range(PAIRS):
                    for j in range(3):
                        at = 128 * (3 * n + j)
                        last = nc.tensor.transpose(bank(0, 1024).bitcast(F16)[:, at:at + 128], gate_hl[:, 2 * (3 * (n // 2) + j) + n % 2, :], ident16[:, :])
                last.then_inc(gate_turned, 1)
                experts_to(AT_END)

            batches(pe, run)

        @block.gpsimd
        def _(pool):
            pool.sem_inc(stored, FIRST)
            with pool.Fori(0, BATCHES * STEPS // 4) as four:
                for s in range(4):
                    pool.wait_ge(e_high, four * 4 + s + 1)
                    nc.gpsimd.tensor_tensor(eg_hl[:, s, 1, :], eg[:, s, :], eg_hl[:, s, 0, :], ALU.subtract).then_inc(e_low, 1)

        @block.scalar
        def _(act):
            A = nc.scalar.activation
            act.wait_ge(weights_ready, 1)

            def run(a, e):
                done = [0]

                def experts_to(target):
                    while e is not None and done[0] < target:
                        step(e[0], e[1], done[0])
                        done[0] += 1

                def step(it, parity, s):
                    if s < STEPS:
                        act.wait_ge(e_summed, it * STEPS + s + 1)
                        if s >= 2:
                            act.wait_ge(e_gated, it * STEPS + s - 1)
                        A(eh[:, s % 2, :], bank(HIDDEN + s % 2), ACT.Gelu, bias=eb1[:, s % EXPERTS:s % EXPERTS + 1]).then_inc(e_gelu, 1)
                    m = s - 1
                    if 0 <= m < STEPS:
                        act.wait_ge(e_gated, it * STEPS + m + 1)
                        if m >= 4:
                            act.wait_ge(e_added, it * STEPS + m - 3)
                        A(eg_hl[:, m % 4, 0, :], eg[:, m % 4, :], ACT.Copy).then_inc(e_high, 1)

                if a is None:
                    experts_to(AT_END)
                    return
                it, parity = a
                experts_to(AT_X)
                for v in range(2):
                    act.wait_ge(x_turned, it * 2 + v + 1)
                    A(xT[:, v, :], sides_at(0)[:, v, :], ACT.Copy).then_inc(xT_copied, 1)
                for v in range(2):
                    act.wait_ge(neg_made, it * 2 + v + 1)
                    A(q_exp[:, v, :], q_neg[:, v, :], ACT.Exp)
                    A(side(k_exp, v), side(k_neg, v), ACT.Exp).then_inc(exp_made, 1)
                experts_to(AT_QK)
                for v in range(2):
                    act.wait_ge(v_summed, it * 2 + v + 1)
                    A(v_one[:, VJ * v:VJ * (v + 1), 0:D], sides_at(0)[:, v, :].rearrange("p (c w) -> p c w", w=D), ACT.Copy).then_inc(v_copied, 1)
                experts_to(AT_NORM1)
                for v in range(2):
                    act.wait_ge(norm_turned, it * 2 + v + 1)
                    A(normT[:, v, :], sides_at(2)[:, v, :], ACT.Copy).then_inc(normT_copied, 1)
                for n in range(PAIRS):
                    act.wait_ge(hid_summed, it * PAIRS + n + 1)
                    A(hid[:, n, :], bank(n), ACT.Relu).then_inc(hid_made, 1)
                experts_to(AT_NORM4)
                act.wait_ge(xn_turned, it + 1)
                A(xnT[:, parity, :, :].rearrange("p n w -> p (n w)"), bank(0, 1024).bitcast(F16)[:, 0:PAIRS * PW], ACT.Copy).then_inc(xnT_copied, 1)
                act.wait_ge(rexp_in, it + 1)
                A(rexp[:, :, :], logit[:, :, :], ACT.Exp).then_inc(rexp_made, 1)
                experts_to(AT_GATES)
                act.wait_ge(gate_turned, it + 1)
                A(gateT[:, parity, :, :].rearrange("p n w -> p (n w)"), bank(0, 1024).bitcast(F16)[:, 0:PAIRS * PW], ACT.Copy).then_inc(gateT_copied, 1)
                experts_to(AT_END)

            batches(act, run)

        @block.vector
        def _(dve):
            V = nc.vector
            start = (h_in[:, :, :, :], proj[:, :, :], w1[:, :, :, :], raw_b[:, :], gate_hl[:, :, :], ew1[D:128, 1, :, :], wr[D:128, 1, :], eb2[:, :, :], zeros[:, :])
            for t in start:
                V.memset(t, 0.0).then_inc(dve_step, 1)
            V.memset(v_one[:, :, :], 1.0).then_inc(dve_step, 1)
            dve.wait_ge(dve_step, len(start) + 1)
            dve.sem_inc(zeros_set, 1)
            dve.wait_ge(w_in, 16 * N_W)
            splits = ((ew1[:, 0, :, :], ew1[0:D, 0, :, :], ew1[0:D, 1, :, :], raw[:, :, :], raw[0:D, :, :]),
                      (wr[:, 0, :], wr[0:D, 0, :], wr[0:D, 1, :], raw_r[:, :], raw_r[0:D, :]),
                      (ew2[:, 0, :, :], ew2[:, 0, :, :], ew2[:, 1, :, :], raw2[:, :, :], raw2[:, :, :]),
                      (eb2[:, 0, :], eb2[0:EXPERTS, 0, :], eb2[0:EXPERTS, 1, :], raw_b[:, :], raw_b[0:EXPERTS, :]))
            for high, _, _, whole, _ in splits:
                V.tensor_copy(high, whole).then_inc(dve_step, 1)
            V.tensor_copy(ident16[:, :], ident[:, :]).then_inc(dve_step, 1)
            V.tensor_copy(pick[:, :, :], raw_p[:, :, :]).then_inc(dve_step, 1)
            STARTED = len(start) + 1 + len(splits) + 2
            dve.wait_ge(dve_step, STARTED)
            for _, high, low, _, whole in splits:
                V.tensor_tensor(low, whole, high, ALU.subtract).then_inc(dve_step, 1)
            STARTED += len(splits)
            dve.wait_ge(dve_step, STARTED)
            dve.sem_inc(weights_ready, 1)
            LINKS = 107

            def run(a, e):
                done = [0]

                def experts_to(target):
                    while e is not None and done[0] < target:
                        step(e[0], e[1], done[0])
                        done[0] += 1

                def step(it, parity, s):
                    if s >= LAG + EXPERTS and (s - LAG) % EXPERTS == 0:
                        n = (s - LAG) // EXPERTS - 1
                        dve.wait_ge(e_added, it * STEPS + EXPERTS * (n + 1))
                        if n == 0 and (not isinstance(it, int) or it > 0):
                            wait_apart(dve, stored, it * (8 * 16) + FIRST, dve_passed)
                        V.tensor_tensor(chunks(h_out[:, :, :])[:, n // 2, :, n % 2, :], chunks(h_mid[:, parity, :, :])[:, n // 2, :, n % 2, :],
                                        bank(SUMS, 3 * D).rearrange("p (j w) -> p j w", j=3), ALU.add).then_inc(e_read, 1)
                    if s < STEPS:
                        dve.wait_ge(e_gelu, it * STEPS + s + 1)
                        dve.wait_ge(e_gates, it * STEPS + s + 1)
                        if s >= 4:
                            dve.wait_ge(e_low, it * STEPS + s - 3)
                        V.tensor_tensor(eg[:, s % 4, :], eh[:, s % 2, :], bank(GATES), ALU.mult).then_inc(e_gated, 1)

                if a is None:
                    experts_to(AT_END)
                    return
                it, parity = a
                n = [STARTED]

                def link(instruction):
                    n[0] += 1
                    instruction.then_inc(dve_step, 1)
                    dve.wait_ge(dve_step, it * LINKS + n[0])

                def wide(t):
                    return t.unsqueeze(2).to_broadcast([128, CH, D])

                def rsqrt(y, v, t, u):
                    link(V.tensor_scalar(t.bitcast(I32), v.bitcast(I32), 1, None, ALU.logical_shift_right))
                    link(V.tensor_scalar(y.bitcast(I32), t.bitcast(I32), -1.0, float(0x5F3759DF), ALU.mult, ALU.add))
                    for _ in range(3):
                        link(V.scalar_tensor_tensor(out=t, in0=v, scalar=-0.5, in1=y, op0=ALU.mult, op1=ALU.mult))
                        link(V.tensor_tensor(u, t, y, ALU.mult))
                        link(V.scalar_tensor_tensor(out=y, in0=u, scalar=1.5, in1=y, op0=ALU.add, op1=ALU.mult))

                def norm(dst, src, steps, upto, by_side=False):
                    link(V.tensor_reduce(stat[:, 0, :] if not by_side else stat[:, 0, :].rearrange("p (v c) -> p v c", v=2), src, AX.X, ALU.add))
                    experts_to(steps + 1 * (upto - steps) // 5)
                    for v in range(2) if by_side else (None,):
                        c, part = (slice(0, CH), src) if v is None else (slice(VJ * v, VJ * (v + 1)), src[:, v, :, :])
                        sums = stat[:, 0, c].unsqueeze(2).to_broadcast(list(part.shape))
                        last = V.scalar_tensor_tensor(out=centred[:, c, :], in0=sums, scalar=-1.0 / D, in1=part, op0=ALU.mult, op1=ALU.add)
                    link(last)
                    experts_to(steps + 2 * (upto - steps) // 5)
                    link(V.tensor_tensor(squares[:, :, :], centred[:, :, :], centred[:, :, :], ALU.mult))
                    experts_to(steps + 3 * (upto - steps) // 5)
                    link(V.tensor_reduce(stat[:, 2, :], squares[:, :, :], AX.X, ALU.add))
                    experts_to(steps + 4 * (upto - steps) // 5)
                    link(V.tensor_scalar(stat[:, 3, :], stat[:, 2, :], 1.0 / D, LN_EPS, ALU.mult, ALU.add))
                    rsqrt(stat[:, 0, :], stat[:, 3, :], stat[:, 1, :], stat[:, 2, :])
                    experts_to(steps + 5 * (upto - steps) // 5)
                    return V.tensor_tensor(dst, centred[:, :, :], wide(stat[:, 0, :]), ALU.mult)

                def row(v):
                    return vecs[:, v:v + 1, :].to_broadcast([128, CH, D])

                by_chunk = lambda t: t.rearrange("p v (c w) -> p v c w", w=D)

                dve.wait_ge(loaded[parity], (it - parity) * (3 * 16) + 6 * 16)
                norm(x[:, :, :], h_in[:, parity, :, :], 0, AT_X).then_inc(x_made, 1)
                for v in range(2):
                    dve.wait_ge(qk_summed, it * 2 + v + 1)
                    V.tensor_scalar(q_neg[:, v, :], sides_at(0)[:, v, :], 0.0, None, ALU.min)
                    V.tensor_scalar(side(k_neg, v), sides_at(2)[:, v, :], 0.0, None, ALU.min).then_inc(neg_made, 1)
                experts_to(AT_QK - 1)
                for v in range(2):
                    dve.wait_ge(exp_made, it * 2 + v + 1)
                    V.scalar_tensor_tensor(out=q_pos[:, v, :], in0=sides_at(0)[:, v, :], scalar=0.0, in1=q_exp[:, v, :], op0=ALU.max, op1=ALU.add)\
                        .then_inc(q_made, 1)
                    V.scalar_tensor_tensor(out=side(k_pos, v), in0=sides_at(2)[:, v, :], scalar=0.0, in1=side(k_exp, v), op0=ALU.max, op1=ALU.add)\
                        .then_inc(k_made, 1)
                experts_to(AT_QK)
                dve.wait_ge(kv_made, it + 1)
                for t in range(2):
                    kv = bank(2 + t, 260).rearrange("p (v u c) -> p v u c", v=2, u=2)
                    for v in range(2):
                        V.tensor_tensor(kv_head[:, 2 * t + v, 0, :, :], kv[:, v, :, 0:D], one_head[:, :, :], ALU.mult)
                        last = V.tensor_tensor(kv_head[:, 2 * t + v, 1, :, :], kv[:, v, :, D:D + 1].to_broadcast([128, 2, D]), one_head[:, :, :], ALU.mult)
                    experts_to(AT_QK + (t + 1) * (AT_KV - AT_QK) // 2)
                last.then_inc(kv_masked, 1)
                for v in range(2):
                    dve.wait_ge(msg_summed, it * 2 + v + 1)
                    link(V.tensor_scalar(q_neg[:, v, :], sides_at(2)[:, v, :], ATT_EPS, None, ALU.add))
                    link(V.reciprocal(z_inv[:, v, :], q_neg[:, v, :]))
                    V.tensor_tensor(msgT[:, v, :], sides_at(0)[:, v, :], z_inv[:, v, :], ALU.mult).then_inc(msg_made, 1)
                    experts_to(((AT_KV + AT_MSG) // 2, AT_MSG)[v])
                dve.wait_ge(msg_mixed, it + 1)
                link(norm(squares[:, :, :], by_chunk(sides_at(0)), AT_MSG, AT_NORM1, by_side=True))
                link(V.tensor_tensor(centred[:, :, :], squares[:, :, :], row(0), ALU.mult))
                V.tensor_tensor(msg[:, :, :], centred[:, :, :], row(1), ALU.add).then_inc(message_normed, 1)
                dve.wait_ge(msg2_made, it + 1)
                link(norm(squares[:, :, :], by_chunk(sides_at(0)), AT_NORM1, AT_NORM2 - 3, by_side=True))
                experts_to(AT_NORM2 - 2)
                link(V.tensor_tensor(centred[:, :, :], squares[:, :, :], row(2), ALU.mult))
                link(V.tensor_tensor(squares[:, :, :], centred[:, :, :], row(3), ALU.add))
                experts_to(AT_NORM2 - 1)
                link(V.tensor_tensor(centred[:, :, :], squares[:, :, :], x[:, :, :], ALU.add))
                experts_to(AT_NORM2)
                link(V.tensor_tensor(h_mid[:, parity, :, :], centred[:, :, :], h_in[:, parity, :, :], ALU.add))
                dve.sem_inc(h_mid_made, 1)
                link(norm(squares[:, :, :], h_mid[:, parity, :, :], AT_NORM2, AT_NORM3))
                link(norm(xn[:, :, :], squares[:, :, :], AT_NORM3, AT_NORM4 - 1))
                link(V.tensor_tensor(centred[:, :, :], xn[:, :, :], row(4), ALU.mult))
                link(V.tensor_tensor(xn[:, :, :], centred[:, :, :], row(5), ALU.add))
                link(V.tensor_copy(xn_hl[:, :, 0, :], xn[:, :, :]))
                V.tensor_tensor(xn_hl[:, :, 1, :], xn[:, :, :], xn_hl[:, :, 0, :], ALU.subtract).then_inc(xn_made, 1)
                experts_to(AT_NORM4)
                dve.wait_ge(logits_made, it + 1)
                link(V.tensor_tensor(gate[:, :, :], bank(2, CH * EXPERTS).rearrange("p (c e) -> p c e", e=EXPERTS),
                                     br.unsqueeze(1).to_broadcast([128, CH, EXPERTS]), ALU.add))
                link(V.tensor_reduce(stat[:, 0, :], gate[:, :, :], AX.X, ALU.max))
                V.tensor_tensor(logit[:, :, :], gate[:, :, :], stat[:, 0, :].unsqueeze(2).to_broadcast([128, CH, EXPERTS]), ALU.subtract).then_inc(rexp_in, 1)
                all_, mine = (gate[:, :, :].unsqueeze(n).to_broadcast([128, CH, EXPERTS, EXPERTS]) for n in (2, 3))
                V.tensor_tensor(cmp_gt[:, :, :, :], all_, mine, ALU.is_gt)
                last = V.tensor_tensor(cmp_eq[:, :, :, :], all_, mine, ALU.is_equal)
                earlier = before[:, :, :].rearrange("p a b -> p (a b)").unsqueeze(1).to_broadcast([128, CH, 64])
                flat = lambda t: t[:, :, :, :].rearrange("p n a b -> p n (a b)")
                link(last)
                link(V.tensor_tensor(flat(cmp_eq), flat(cmp_eq), earlier, ALU.mult))
                link(V.tensor_tensor(flat(cmp_gt), flat(cmp_gt), flat(cmp_eq), ALU.add))
                link(V.tensor_reduce(rank[:, :, :].rearrange("p n e -> p (n e)"), cmp_gt[:, :, :, :].rearrange("p n a b -> p (n a) b"), AX.X, ALU.add))
                experts_to(AT_GATES)
                dve.wait_ge(rexp_made, it + 1)
                link(V.scalar_tensor_tensor(out=gate[:, :, :], in0=rank[:, :, :], scalar=TOP - 0.5, in1=rexp[:, :, :], op0=ALU.is_lt, op1=ALU.mult))
                link(V.tensor_reduce(stat[:, 1, :], gate[:, :, :], AX.X, ALU.add))
                link(V.reciprocal(stat[:, 2, :], stat[:, 1, :]))
                link(V.tensor_tensor(gate[:, :, :], gate[:, :, :], stat[:, 2, :].unsqueeze(2).to_broadcast([128, CH, EXPERTS]), ALU.mult))
                link(V.tensor_copy(gate_hl[:, :, 0:EXPERTS], gate[:, :, :]))
                V.tensor_tensor(gate_hl[:, :, EXPERTS:2 * EXPERTS], gate[:, :, :], gate_hl[:, :, 0:EXPERTS], ALU.subtract).then_inc(gate_made, 1)
                experts_to(AT_END)
                assert n[0] - STARTED == LINKS, n[0] - STARTED

            batches(dve, run)


def kernel(**inputs):
    import concourse.bacc as _bacc
    from concourse.bass_utils import run_bass_kernel_spmd as _run

    tok = lambda name: np.asarray(inputs["L0_tok_" + name])
    attn = lambda name: np.asarray(inputs["L0_attn_" + name])
    ffn = lambda name: np.asarray(inputs["L0_ffn_" + name])
    sw = np.stack([tok(f"sw{l}") for l in range(LAYERS)]).reshape(LAYERS, C, C, M1, KYB, KYS)
    arrays = {
        **transforms(), **token_tables(),
        "x": np.asarray(inputs["x"]).transpose(0, 3, 1, 2).reshape(B // QB, QB * CIN, PIX),
        "sw": sw.transpose(0, 4, 1, 5, 3, 2).reshape(LAYERS, KYB * C, KYS * M1 * C),
        "cw": np.stack([tok(f"cw{l}").T for l in range(LAYERS)], axis=1),
        "cb": np.stack([tok(f"cb{l}") for l in range(LAYERS)], axis=1),
        "fc0_w": tok("fc0_w"), "fc0_b": tok("fc0_b").reshape(C, 1),
        "fc1_w": tok("fc1_w"), "fc1_b": tok("fc1_b").reshape(FC1, 1),
        "fc2_w": tok("fc2_w"), "fc2_b": tok("fc2_b").reshape(1, 1),
        "txt": np.asarray(inputs["txt"]).reshape(B // 2, 2, L_TXT, D),
        "proj": np.stack([attn(n) for n in ("Wq", "Wk", "Wv", "Wm")], axis=1),
        "W1": attn("W1").reshape(2, D, FF).transpose(1, 0, 2), "W2": attn("W2"),
        "vecs": np.concatenate([*(attn(n) for n in ("g1", "b1", "g2", "b2")), ffn("gamma"), ffn("beta"), ffn("br")]).reshape(1, -1),
        "Wr": ffn("Wr"),
        "ew1": ffn("W1").transpose(1, 0, 2), "eb1": ffn("b1").T,
        "ew2": ffn("W2").transpose(1, 0, 2), "eb2": ffn("b2"),
    }
    nc = _bacc.Bacc("TRN2", target_bir_lowering=False, num_devices=1)
    arrays = {f"in_{name}_dram": np.ascontiguousarray(a) for name, a in arrays.items()}
    ins = {name[3:-5]: nc.dram_tensor(name, a.shape, mybir.dt.from_np(a.dtype), kind="ExternalInput").ap() for name, a in arrays.items()}
    tokens = nc.dram_tensor("tokens_dram", (B, PIX), F32, kind="Internal").ap()
    scratch = nc.dram_tensor("scratch_dram", (KYS, 2, 2, KYB, S, HB * C), F16, kind="Internal").ap()
    split_weights = nc.dram_tensor("split_weights_dram", (LAYERS, KYB * C, KYS * 2 * M1 * C), F16, kind="Internal").ap()
    out = nc.dram_tensor("out_0_dram", (B // 2, 2, S + L_TXT, D), F32, kind="ExternalOutput").ap()
    build_operator(nc, ins, split_weights, scratch, tokens)
    build_tokens(nc, ins, tokens, out)
    r = _run(nc, [arrays], core_ids=[0])
    return r.results[0]["out_0_dram"].reshape(B, S + L_TXT, D)
```
